# Optimizing a Trainium2 kernel written in Bass

```python
import numpy as np
import jax
import jax.numpy as jnp

def _softmax(x, axis=-1):
    return jax.nn.softmax(x, axis=axis)

def _gelu(x):
    return jax.nn.gelu(x, approximate=True)

def _silu(x):
    return jax.nn.silu(x)

def _sigmoid(x):
    return jax.nn.sigmoid(x)

def _layernorm(x, axis=-1, eps=1e-05):
    m = jnp.mean(x, axis=axis, keepdims=True)
    v = jnp.var(x, axis=axis, keepdims=True)
    return (x - m) / jnp.sqrt(v + eps)

def _scatter_add(tgt, idx, src, axis=0):
    return tgt.at[idx].add(src)

def _segment_sum(src, seg, n):
    return jax.ops.segment_sum(src, seg, n)
kernel_name = 'mk_sandwich_d2_jaxref_r8_f7cb27'

def setup_inputs(seed: int=0):
    np.random.seed(seed)
    _w = jnp.asarray

    def _L0_attn_setup():
        import jax, jax.numpy as jnp
        import numpy as np
        DIM = 128
        QK_DIM = 128
        HIDDEN = 256
        B, N = (4, 512)

        def _layernorm(x, g, b, eps=1e-05):
            mu = jnp.mean(x, axis=-1, keepdims=True)
            var = jnp.var(x, axis=-1, keepdims=True)
            return (x - mu) * jax.lax.rsqrt(var + eps) * g + b
        key = jax.random.key(seed)
        ks = jax.random.split(key, 10)
        std = 0.02
        return {'x': jax.random.normal(ks[0], (B, N, DIM), dtype=jnp.float32), 'ln_g': jnp.ones((DIM,), jnp.float32), 'ln_b': jnp.zeros((DIM,), jnp.float32), 'W_hidden': jax.random.normal(ks[1], (DIM, 2 * HIDDEN), jnp.float32) * (1.0 / np.sqrt(DIM)), 'b_hidden': jnp.zeros((2 * HIDDEN,), jnp.float32), 'W_qk': jax.random.normal(ks[2], (DIM, QK_DIM), jnp.float32) * (1.0 / np.sqrt(DIM)), 'b_qk': jnp.zeros((QK_DIM,), jnp.float32), 'os_gamma': jax.random.normal(ks[3], (2, QK_DIM), jnp.float32) * std, 'os_beta': jnp.zeros((2, QK_DIM), jnp.float32), 'W_out': jax.random.normal(ks[4], (HIDDEN, DIM), jnp.float32) * (1.0 / np.sqrt(HIDDEN)), 'b_out': jnp.zeros((DIM,), jnp.float32)}
    _L0_attn_in = _L0_attn_setup()

    def _L0_ffn_setup():
        import jax, jax.numpy as jnp
        import numpy as np
        DIM = 128

        def _reference_tuple_inner(x, W_r, W_k, W_v, mu_r, mu_k):
            B, T, C = x.shape
            x_prev = jnp.concatenate([jnp.zeros((B, 1, C), x.dtype), x[:, :-1, :]], axis=1)
            xr = mu_r * x + (1.0 - mu_r) * x_prev
            xk = mu_k * x + (1.0 - mu_k) * x_prev
            r = jax.nn.sigmoid(jnp.einsum('btc,dc->btd', xr, W_r))
            k = jnp.einsum('btc,dc->btd', xk, W_k)
            k_act = jnp.square(jax.nn.relu(k))
            out = r * jnp.einsum('btc,dc->btd', k_act, W_v)
            new_state = x[:, -1, :]
            return (out, new_state)
        key = jax.random.key(seed)
        ks = jax.random.split(key, 6)
        B, T, C = (8, 256, DIM)
        x = jax.random.normal(ks[0], (B, T, C), dtype=jnp.float32)
        s = 1.0 / np.sqrt(C)
        W_r = jax.random.uniform(ks[1], (C, C), jnp.float32, -s, s)
        W_k = jax.random.uniform(ks[2], (C, C), jnp.float32, -s, s)
        W_v = jax.random.uniform(ks[3], (C, C), jnp.float32, -s, s)
        mu_r = jax.random.uniform(ks[4], (C,), jnp.float32)
        mu_k = jax.random.uniform(ks[5], (C,), jnp.float32)
        return {'x': x, 'W_r': W_r, 'W_k': W_k, 'W_v': W_v, 'mu_r': mu_r, 'mu_k': mu_k}
    _L0_ffn_in = _L0_ffn_setup()

    def _L1_attn_setup():
        import math
        import jax, jax.numpy as jnp
        import numpy as np
        D_MODEL = 128
        N_HEADS = 16
        HEAD_DIM = D_MODEL // N_HEADS
        ROPE_THETA = 10000.0

        def _apply_rope(t, offset=0):
            B, H, T, Dh = t.shape
            inv_freq = 1.0 / ROPE_THETA ** (jnp.arange(0, Dh, 2, dtype=jnp.float32) / Dh)
            pos = jnp.arange(T, dtype=jnp.float32) + offset
            ang = pos[:, None] * inv_freq[None, :]
            cos = jnp.concatenate([jnp.cos(ang), jnp.cos(ang)], axis=-1)
            sin = jnp.concatenate([jnp.sin(ang), jnp.sin(ang)], axis=-1)
            t1, t2 = (t[..., :Dh // 2], t[..., Dh // 2:])
            rot = jnp.concatenate([-t2, t1], axis=-1)
            return t * cos + rot * sin

        def _forward(x, Wq, Wk, Wv, Wo):
            B, T, _ = x.shape
            scale = 1.0 / math.sqrt(HEAD_DIM)

            def split_heads(y):
                return y.reshape(B, T, N_HEADS, HEAD_DIM).transpose(0, 2, 1, 3)
            q = split_heads(x @ Wq.T)
            k = split_heads(x @ Wk.T)
            v = split_heads(x @ Wv.T)
            q = _apply_rope(q)
            k = _apply_rope(k)
            scores = jnp.einsum('bhtd,bhsd->bhts', q, k) * scale
            causal = jnp.triu(jnp.ones((T, T), dtype=bool), k=1)
            scores = jnp.where(causal[None, None], -jnp.inf, scores)
            attn = jax.nn.softmax(scores, axis=-1)
            attn = jnp.nan_to_num(attn, nan=0.0)
            out = jnp.einsum('bhts,bhsd->bhtd', attn, v)
            out = out.transpose(0, 2, 1, 3).reshape(B, T, N_HEADS * HEAD_DIM)
            return out @ Wo.T
        key = jax.random.key(seed)
        ks = jax.random.split(key, 5)
        B, T = (4, 256)
        w_scale = math.sqrt(2.0 / (D_MODEL + D_MODEL))
        return {'x': jax.random.normal(ks[0], (B, T, D_MODEL), dtype=jnp.float32), 'Wq': jax.random.normal(ks[1], (D_MODEL, D_MODEL), dtype=jnp.float32) * w_scale, 'Wk': jax.random.normal(ks[2], (D_MODEL, D_MODEL), dtype=jnp.float32) * w_scale, 'Wv': jax.random.normal(ks[3], (D_MODEL, D_MODEL), dtype=jnp.float32) * w_scale, 'Wo': jax.random.normal(ks[4], (D_MODEL, D_MODEL), dtype=jnp.float32) * w_scale}
    _L1_attn_in = _L1_attn_setup()

    def _L1_ffn_setup():
        import jax, jax.numpy as jnp
        import numpy as np
        EPS = 1e-12

        def rms_norm(t, gamma):
            n = jnp.maximum(jnp.linalg.norm(t, axis=-1, keepdims=True), EPS)
            scale = jnp.sqrt(jnp.asarray(t.shape[-1], t.dtype))
            return t / n * scale * gamma
        key = jax.random.key(seed)
        ks = jax.random.split(key, 4)
        b, s, d = (4, 512, 128)
        e, t = (8, 64)
        hidden = 4 * d
        return {'x': jax.random.normal(ks[0], (b, s, d), dtype=jnp.float32), 'gamma_x': jnp.ones((d,), dtype=jnp.float32), 'gamma_slot': jnp.ones((d,), dtype=jnp.float32), 'slot_embeds': jax.random.normal(ks[1], (e, t, d), dtype=jnp.float32), 'w1': jax.random.normal(ks[2], (d, hidden), dtype=jnp.float32) * (1.0 / np.sqrt(d)), 'w2': jax.random.normal(ks[3], (hidden, d), dtype=jnp.float32) * (1.0 / np.sqrt(hidden))}
    _L1_ffn_in = _L1_ffn_setup()
    _d = {'L0_attn_x': _L0_attn_in['x'], 'L0_attn_ln_g': _L0_attn_in['ln_g'], 'L0_attn_ln_b': _L0_attn_in['ln_b'], 'L0_attn_W_hidden': _L0_attn_in['W_hidden'], 'L0_attn_b_hidden': _L0_attn_in['b_hidden'], 'L0_attn_W_qk': _L0_attn_in['W_qk'], 'L0_attn_b_qk': _L0_attn_in['b_qk'], 'L0_attn_os_gamma': _L0_attn_in['os_gamma'], 'L0_attn_os_beta': _L0_attn_in['os_beta'], 'L0_attn_W_out': _L0_attn_in['W_out'], 'L0_attn_b_out': _L0_attn_in['b_out'], 'L0_ffn_W_r': _L0_ffn_in['W_r'], 'L0_ffn_W_k': _L0_ffn_in['W_k'], 'L0_ffn_W_v': _L0_ffn_in['W_v'], 'L0_ffn_mu_r': _L0_ffn_in['mu_r'], 'L0_ffn_mu_k': _L0_ffn_in['mu_k'], 'L1_attn_Wq': _L1_attn_in['Wq'], 'L1_attn_Wk': _L1_attn_in['Wk'], 'L1_attn_Wv': _L1_attn_in['Wv'], 'L1_attn_Wo': _L1_attn_in['Wo'], 'L1_ffn_gamma_x': _L1_ffn_in['gamma_x'], 'L1_ffn_gamma_slot': _L1_ffn_in['gamma_slot'], 'L1_ffn_slot_embeds': _L1_ffn_in['slot_embeds'], 'L1_ffn_w1': _L1_ffn_in['w1'], 'L1_ffn_w2': _L1_ffn_in['w2']}
    _x0 = _d['L0_attn_x']
    _d['L0_attn_x'] = jax.random.normal(jax.random.fold_in(jax.random.key(seed), 1), (16, 512, 128), dtype=_x0.dtype)
    del _x0
    return _d

def reference(L0_attn_x, L0_attn_ln_g, L0_attn_ln_b, L0_attn_W_hidden, L0_attn_b_hidden, L0_attn_W_qk, L0_attn_b_qk, L0_attn_os_gamma, L0_attn_os_beta, L0_attn_W_out, L0_attn_b_out, L0_ffn_W_r, L0_ffn_W_k, L0_ffn_W_v, L0_ffn_mu_r, L0_ffn_mu_k, L1_attn_Wq, L1_attn_Wk, L1_attn_Wv, L1_attn_Wo, L1_ffn_gamma_x, L1_ffn_gamma_slot, L1_ffn_slot_embeds, L1_ffn_w1, L1_ffn_w2):

    def _L0_attn_ref(x, ln_g, ln_b, W_hidden, b_hidden, W_qk, b_qk, os_gamma, os_beta, W_out, b_out):
        import jax, jax.numpy as jnp
        import numpy as np
        DIM = 128
        QK_DIM = 128
        HIDDEN = 256
        B, N = (4, 512)

        def _layernorm(x, g, b, eps=1e-05):
            mu = jnp.mean(x, axis=-1, keepdims=True)
            var = jnp.var(x, axis=-1, keepdims=True)
            return (x - mu) * jax.lax.rsqrt(var + eps) * g + b
        n = x.shape[-2]
        normed = _layernorm(x, ln_g, ln_b)
        hidden = jax.nn.silu(normed @ W_hidden + b_hidden)
        v, gate = jnp.split(hidden, 2, axis=-1)
        qk = jax.nn.silu(normed @ W_qk + b_qk)
        q = qk * os_gamma[0] + os_beta[0]
        k = qk * os_gamma[1] + os_beta[1]
        sim = jnp.einsum('bid,bjd->bij', q, k)
        denom = (jnp.arange(n, dtype=x.dtype) + 1.0)[:, None]
        sim = sim / denom
        attn = jnp.square(jax.nn.relu(sim))
        causal_mask = jnp.triu(jnp.ones((n, n), dtype=bool), k=1)
        attn = jnp.where(causal_mask, 0.0, attn)
        out = jnp.einsum('bij,bjd->bid', attn, v)
        out = out * gate
        out = out @ W_out + b_out
        return out + x

    def _L0_ffn_ref(x, W_r, W_k, W_v, mu_r, mu_k):
        import jax, jax.numpy as jnp
        import numpy as np
        DIM = 128

        def _reference_tuple_inner(x, W_r, W_k, W_v, mu_r, mu_k):
            B, T, C = x.shape
            x_prev = jnp.concatenate([jnp.zeros((B, 1, C), x.dtype), x[:, :-1, :]], axis=1)
            xr = mu_r * x + (1.0 - mu_r) * x_prev
            xk = mu_k * x + (1.0 - mu_k) * x_prev
            r = jax.nn.sigmoid(jnp.einsum('btc,dc->btd', xr, W_r))
            k = jnp.einsum('btc,dc->btd', xk, W_k)
            k_act = jnp.square(jax.nn.relu(k))
            out = r * jnp.einsum('btc,dc->btd', k_act, W_v)
            new_state = x[:, -1, :]
            return (out, new_state)
        return _reference_tuple_inner(x, W_r, W_k, W_v, mu_r, mu_k)[0]

    def _L1_attn_ref(x, Wq, Wk, Wv, Wo):
        import math
        import jax, jax.numpy as jnp
        import numpy as np
        D_MODEL = 128
        N_HEADS = 16
        HEAD_DIM = D_MODEL // N_HEADS
        ROPE_THETA = 10000.0

        def _apply_rope(t, offset=0):
            B, H, T, Dh = t.shape
            inv_freq = 1.0 / ROPE_THETA ** (jnp.arange(0, Dh, 2, dtype=jnp.float32) / Dh)
            pos = jnp.arange(T, dtype=jnp.float32) + offset
            ang = pos[:, None] * inv_freq[None, :]
            cos = jnp.concatenate([jnp.cos(ang), jnp.cos(ang)], axis=-1)
            sin = jnp.concatenate([jnp.sin(ang), jnp.sin(ang)], axis=-1)
            t1, t2 = (t[..., :Dh // 2], t[..., Dh // 2:])
            rot = jnp.concatenate([-t2, t1], axis=-1)
            return t * cos + rot * sin

        def _forward(x, Wq, Wk, Wv, Wo):
            B, T, _ = x.shape
            scale = 1.0 / math.sqrt(HEAD_DIM)

            def split_heads(y):
                return y.reshape(B, T, N_HEADS, HEAD_DIM).transpose(0, 2, 1, 3)
            q = split_heads(x @ Wq.T)
            k = split_heads(x @ Wk.T)
            v = split_heads(x @ Wv.T)
            q = _apply_rope(q)
            k = _apply_rope(k)
            scores = jnp.einsum('bhtd,bhsd->bhts', q, k) * scale
            causal = jnp.triu(jnp.ones((T, T), dtype=bool), k=1)
            scores = jnp.where(causal[None, None], -jnp.inf, scores)
            attn = jax.nn.softmax(scores, axis=-1)
            attn = jnp.nan_to_num(attn, nan=0.0)
            out = jnp.einsum('bhts,bhsd->bhtd', attn, v)
            out = out.transpose(0, 2, 1, 3).reshape(B, T, N_HEADS * HEAD_DIM)
            return out @ Wo.T
        return _forward(x, Wq, Wk, Wv, Wo)

    def _L1_ffn_ref(x, gamma_x, gamma_slot, slot_embeds, w1, w2):
        import jax, jax.numpy as jnp
        import numpy as np
        EPS = 1e-12

        def rms_norm(t, gamma):
            n = jnp.maximum(jnp.linalg.norm(t, axis=-1, keepdims=True), EPS)
            scale = jnp.sqrt(jnp.asarray(t.shape[-1], t.dtype))
            return t / n * scale * gamma
        b, s, d = x.shape
        e, t, _ = slot_embeds.shape
        xn = rms_norm(x, gamma_x)
        se = rms_norm(slot_embeds, gamma_slot)
        logits = jnp.einsum('bsd,etd->bset', xn, se)
        dispatch = jax.nn.softmax(logits, axis=1)
        slots = jnp.einsum('bsd,bset->betd', xn, dispatch)
        h = jax.nn.gelu(slots @ w1, approximate=False)
        processed = h @ w2
        combine = jax.nn.softmax(logits.reshape(b, s, e * t), axis=-1)
        out = jnp.einsum('bnd,bsn->bsd', processed.reshape(b, e * t, d), combine)
        return out
    x = L0_attn_x
    x = x + _layernorm(_L0_attn_ref(_layernorm(x, axis=-1), L0_attn_ln_g, L0_attn_ln_b, L0_attn_W_hidden, L0_attn_b_hidden, L0_attn_W_qk, L0_attn_b_qk, L0_attn_os_gamma, L0_attn_os_beta, L0_attn_W_out, L0_attn_b_out), axis=-1)
    x = x + _layernorm(_L0_ffn_ref(_layernorm(x, axis=-1), L0_ffn_W_r, L0_ffn_W_k, L0_ffn_W_v, L0_ffn_mu_r, L0_ffn_mu_k), axis=-1)
    x = x + _layernorm(_L1_attn_ref(_layernorm(x, axis=-1), L1_attn_Wq, L1_attn_Wk, L1_attn_Wv, L1_attn_Wo), axis=-1)
    x = x + _layernorm(_L1_ffn_ref(_layernorm(x, axis=-1), L1_ffn_gamma_x, L1_ffn_gamma_slot, L1_ffn_slot_embeds, L1_ffn_w1, L1_ffn_w2), axis=-1)
    return x

_drawn_inputs = setup_inputs


def setup_inputs(seed=0):
    import zlib

    import numpy as np

    out = dict(_drawn_inputs(seed))
    spreads = {'L0_attn_ln_g': (1.0, 0.6),
     'L0_attn_ln_b': (0.0, 0.8),
     'L0_attn_b_hidden': (0.0, 0.8),
     'L0_attn_b_qk': (0.0, 0.8),
     'L0_attn_os_beta': (0.0, 0.8),
     'L0_attn_b_out': (0.0, 0.778),
     'L1_ffn_gamma_x': (1.0, 0.2),
     'L1_ffn_gamma_slot': (1.0, 0.2)}
    factors = {'L0_attn_W_hidden': 8.0,
     'L0_attn_W_qk': 8.0,
     'L0_attn_os_gamma': 8.0,
     'L0_attn_W_out': 8.0}
    for name, (base, spread) in spreads.items():
        noise = np.random.default_rng([zlib.crc32(name.encode()), seed]).standard_normal(out[name].shape)
        drawn = base * np.exp(spread * noise) if base else spread * noise
        out[name] = jnp.asarray(drawn.astype(out[name].dtype))
    for name, factor in factors.items():
        out[name] = (out[name] * factor).astype(out[name].dtype)
    return out
```

```python
from contextlib import ExitStack

import numpy as np

import concourse.bass as bass
from concourse import mybir
from concourse.alu_op_type import AluOpType as ALU

F32 = mybir.dt.float32
BF16 = mybir.dt.bfloat16
ACT = mybir.ActivationFunctionType
AXX = mybir.AxisListType.X

P = 128
B = 16
N = 512
T = N // P
D = 128
HID = 256
NH, DH = 16, 8
HH = NH // 2
E_T = 512
FF = 512
EPS = 1e-5
NORM_FLOOR = 1e-24 / D
MASKED = -1e30
PARTS_Q = (0, 0, 1, 1, 0, 2)
PARTS_K = (0, 1, 0, 1, 2, 0)
KS = DH * len(PARTS_Q)
KM = KS + 2


def live(b):
    return not isinstance(b, int) or 0 <= b < B


def upto(engine, sem, value):
    if not isinstance(value, int) or value > 0:
        engine.wait_ge(sem, value)


def run_steps(engine, step, first, loop_from, loop_to, last):
    for s in range(first, loop_from):
        step(s, s % 2)
    with engine.Fori(0, (loop_to - loop_from) // 2) as pair:
        for k in range(2):
            step(2 * pair + (loop_from + k), (loop_from + k) % 2)
    for s in range(loop_to, last):
        step(s, s % 2)


def qk_rows(turned=False):
    half, d, h = np.meshgrid(np.arange(2), np.arange(DH), np.arange(HH), indexing="ij")
    d = (d + DH // 2) % DH if turned else d
    return ((half * HH + h) * DH + d).reshape(-1)


def constants():
    p, col = np.arange(P), np.arange(N)
    inv_freq = (1.0 / np.float32(10000.0) ** (np.arange(0, DH, 2, dtype=np.float32) / DH)).astype(np.float32)
    d = p // HH % DH
    angle = col.astype(np.float32)[None, :] * inv_freq[d % (DH // 2)][:, None]
    tables = {
        "ident": np.eye(P),
        "keep": np.where((col[None, :] >= p[:, None]) | (col[None, :] >= P), 1.0, 0.0),
        "inv_pos": np.broadcast_to(1.0 / (col[None, :] + 1.0), (P, N)),
        "cos": np.cos(angle),
        "sin": np.sin(angle) * np.where(d < DH // 2, -1.0, 1.0)[:, None],
        "future": np.tile(np.where(p[None, :] > p[:, None], MASKED, 0.0), (1, 2)),
    }
    return {name: np.ascontiguousarray(a, dtype=np.float32) for name, a in tables.items()}


class Core:

    def __init__(self, nc, ctx, dram):
        self.nc, self.ctx, self.dram = nc, ctx, dram
        self.x = self.sb("x", [P, B, T, D])
        self.ps = ctx.enter_context(nc.psum_tensor("ps", [P, 8, N], F32))
        self.ident = self.sb("ident", [P, P])
        self.ident_bf = self.sb("ident_bf", [P, P], BF16)
        self.eps = self.sb("eps", [P, T])
        self.minus_half = self.sb("minus_half", [P, T])

    def sb(self, name, shape, dtype=F32):
        return self.ctx.enter_context(self.nc.sbuf_tensor(name, shape, dtype))

    def sem(self, name):
        return self.ctx.enter_context(self.nc.semaphore(name))


class Layer:

    def __init__(self, core, prefix, ctx):
        self.nc, self.prefix, self.ctx = core.nc, prefix, ctx

    def sb(self, name, shape, dtype=F32):
        return self.ctx.enter_context(self.nc.sbuf_tensor(f"{self.prefix}_{name}", shape, dtype))

    def sem(self, name):
        return self.ctx.enter_context(self.nc.semaphore(f"{self.prefix}_{name}"))


class Stats:

    def __init__(self, layer, name):
        self.stats = layer.sb(f"{name}_stats", [P, T, 6])
        self.moments = layer.sb(f"{name}_moments", [P, T, 2])
        self.shifted = layer.sb(f"{name}_shifted", [P, T])
        self.rstd = layer.sb(f"{name}_rstd", [P, T])
        self.stats_done = layer.sem(f"{name}_stats_done")
        self.moments_done = layer.sem(f"{name}_moments_done")
        self.shifted_done = layer.sem(f"{name}_shifted_done")
        self.rstd_done = layer.sem(f"{name}_rstd_done")


def take_moments(core, dve, st, src, b):
    nc = core.nc
    for t in range(T):
        nc.vector.bn_stats(st.stats[:, t, :], src(t)).then_inc(st.stats_done, 1)
    dve.wait_ge(st.stats_done, T * b + T)
    dve.sem_inc(core.tick, 1)
    for t in range(T):
        last = nc.vector.bn_aggr(st.moments[:, t, :], st.stats[:, t, :])
    last.then_inc(st.moments_done, 1)


def take_rstd(core, pool, st, b):
    nc = core.nc
    pool.wait_ge(st.moments_done, b + 1)
    nc.gpsimd.tensor_tensor(st.shifted[:, :], st.moments[:, :, 1], core.eps[:, :],
                            ALU.add).then_inc(st.shifted_done, 1)
    pool.wait_ge(st.shifted_done, b + 1)
    nc.gpsimd.tensor_tensor(st.rstd[:, :], st.shifted[:, :], core.minus_half[:, :],
                            ALU.pow).then_inc(st.rstd_done, 1)


def normalize(nc, st, dst, src):
    for t in range(T):
        last = nc.vector.tensor_scalar(dst(t), src(t), st.moments[:, t, 0:1], st.rstd[:, t:t + 1],
                                       ALU.subtract, ALU.mult)
    return last


def set_up(core):
    nc, dram = core.nc, core.dram
    with ExitStack() as ctx:
        L = Layer(core, "setup", ctx)
        loaded, made = L.sem("loaded"), L.sem("made")
        with nc.Block() as block:
            @block.sync
            def _(sp):
                sp.dma_start(core.ident[:, :], dram["ident"]).then_inc(loaded, 16)

            @block.vector
            def _(dve):
                nc.vector.memset(core.eps[:, :], EPS)
                nc.vector.memset(core.minus_half[:, :], -0.5)
                dve.wait_ge(loaded, 16)
                nc.vector.tensor_copy(core.ident_bf[:, :], core.ident[:, :]).then_inc(made, 1)
                dve.wait_ge(made, 1)


def gated_attention(core):
    nc, dram, x, ps = core.nc, core.dram, core.x, core.ps
    with ExitStack() as ctx:
        L = Layer(core, "gau", ctx)
        w_hidden = L.sb("w_hidden", [P, 2 * HID])
        w_qk = L.sb("w_qk", [P, D])
        w_out = L.sb("w_out", [P, HID // P, D])
        keep, inv_pos = L.sb("keep", [P, N]), L.sb("inv_pos", [P, N])
        b_value = L.sb("b_value", [P, HID])
        b_out = L.sb("b_out", [P, D])
        per_feature = L.sb("per_feature", [P, 9])
        ln_g, ln_b, b_qk = (per_feature[:, i:i + 1] for i in range(3))
        b_gate, os_gamma, os_beta = (per_feature[:, i:i + 2] for i in (3, 5, 7))
        a = L.sb("a", [P, 2, T, D])
        a_bias = L.sb("a_bias", [P, 2, T, D])
        n2 = L.sb("n2", [P, T, D])
        nT = L.sb("nT", [P, N])
        value_pre = L.sb("value_pre", [P, T, HID])
        value = L.sb("value", [P, 2, T, HID])
        gateT = L.sb("gateT", [P, 2, 2, N])
        qk_act, q_aff = L.sb("qk_act", [P, N]), L.sb("q_aff", [P, N])
        qT, kT = L.sb("qT", [P, N]), L.sb("kT", [P, N])
        relu = L.sb("relu", [P, 3, N])
        prob = L.sb("prob", [P, 3, N])
        gatedT = L.sb("gatedT", [P, 2, N])
        y, z = L.sb("y", [P, T, D]), L.sb("z", [P, T, D])
        ln_x, ln_a, ln_y = Stats(L, "ln_x"), Stats(L, "ln_a"), Stats(L, "ln_y")

        weights_in = L.sem("weights_in")
        x_in = [L.sem("x_in_even"), L.sem("x_in_odd")]
        a_ok, n2_ok, a_bias_ok = L.sem("a_ok"), L.sem("n2_ok"), L.sem("a_bias_ok")
        nT_mm, nT_ok = L.sem("nT_mm"), L.sem("nT_ok")
        value_mm, value_pre_ok, value_ok = L.sem("value_mm"), L.sem("value_pre_ok"), L.sem("value_ok")
        gate_mm, gate_ok = L.sem("gate_mm"), L.sem("gate_ok")
        qk_mm, qk_act_ok, q_aff_ok, qk_ok = L.sem("qk_mm"), L.sem("qk_act_ok"), L.sem("q_aff_ok"), L.sem("qk_ok")
        score_mm, relu_ok, prob_ok = L.sem("score_mm"), L.sem("relu_ok"), L.sem("prob_ok")
        attn_mm, gated_ok = L.sem("attn_mm"), L.sem("gated_ok")
        out_mm, y_ok, z_ok, x_ok = L.sem("out_mm"), L.sem("y_ok"), L.sem("z_ok"), L.sem("x_ok")

        BK_NT, BK_VALUE, BK_GATE, BK_SCORE = 0, 1, 3, 5
        BK_QK, BK_ATTN, BK_OUT = 0, 5, 7
        SCORES = ((0, 0, 0), (1, 1, 0), (3, 1, 3 * P), (2, 2, 0))

        def width(kt):
            return N - kt * P

        w_loads = [
            (w_hidden[:, :], dram["W_hidden"]), (w_qk[:, :], dram["W_qk"]),
            (w_out[:, :, :], dram["W_out"].rearrange("(j p) d -> p j d", p=P)),
            (keep[:, :], dram["keep"]), (inv_pos[:, :], dram["inv_pos"]),
            (b_value[:, :], dram["b_hidden"][0:HID].partition_broadcast(P)),
            (b_out[:, :], dram["b_out"].partition_broadcast(P)),
            (per_feature[:, :], dram["gau_vectors"]),
        ]
        W_IN = 16 * len(w_loads)

        with nc.Block() as block:
            @block.sync
            def _(sp):
                def load_x(b, u):
                    sp.dma_start(x[:, b, :, :], dram["x"][b].rearrange("(t p) d -> p t d", p=P)).then_inc(x_in[u], 16)

                load_x(0, 0)
                load_x(1, 1)
                for dst, src in w_loads:
                    sp.dma_start(dst, src).then_inc(weights_in, 16)
                with sp.Fori(1, B // 2) as pair:
                    for u in range(2):
                        sp.wait_ge(x_in[u], 16 * pair)
                        load_x(2 * pair + u, u)

            @block.vector
            def _(dve):
                dve.wait_ge(weights_in, W_IN)

                def step(s, u):
                    g, f, gu, fu = s + 2, s + 1, u, 1 - u
                    if live(g):
                        dve.wait_ge(x_in[gu], 16 + 8 * (g - gu))
                        take_moments(core, dve, ln_x, lambda t: x[:, g, t, :], g)
                    if live(s):
                        for i, (kt, bank, at) in enumerate(SCORES):
                            dve.wait_ge(score_mm, 3 * s + bank + 1)
                            if i == 0:
                                upto(dve, prob_ok, 3 * s)
                            w = width(kt)
                            r = nc.vector.scalar_tensor_tensor(
                                relu[:, bank, at:at + w], ps[:, BK_SCORE + bank, at:at + w], 0.0, keep[:, 0:w],
                                ALU.max, ALU.mult)
                            if kt != 1:
                                r.then_inc(relu_ok, 1)
                    if live(g):
                        dve.wait_ge(ln_x.rstd_done, g + 1)
                        upto(dve, a_bias_ok, g - 1)
                        normalize(nc, ln_x, lambda t: a[:, gu, t, :], lambda t: x[:, g, t, :]).then_inc(a_ok, 1)
                    if live(f):
                        dve.wait_ge(value_mm, f + 1)
                        upto(dve, value_ok, f)
                        for j in range(2):
                            last = nc.vector.tensor_tensor(
                                value_pre[:, 2 * j:2 * j + 2, :],
                                ps[:, BK_VALUE + j, :].rearrange("p (t h) -> p t h", t=2),
                                b_value[:, :].unsqueeze(1).broadcast_to([P, 2, HID]), ALU.add)
                        last.then_inc(value_pre_ok, 1)
                    if live(g):
                        dve.wait_ge(a_ok, g + 1)
                        take_moments(core, dve, ln_a, lambda t: a[:, gu, t, :], g)
                    if live(s):
                        dve.wait_ge(gate_ok, s + 1)
                        upto(dve, out_mm, s)
                        for j in range(2):
                            dve.wait_ge(attn_mm, 2 * s + j + 1)
                            nc.vector.tensor_tensor(gatedT[:, j, :], ps[:, BK_ATTN + j, :], gateT[:, u, j, :],
                                                    ALU.mult).then_inc(gated_ok, 1)
                    if live(g):
                        dve.wait_ge(ln_a.rstd_done, g + 1)
                        upto(dve, nT_mm, g)
                        normalize(nc, ln_a, lambda t: n2[:, t, :], lambda t: a[:, gu, t, :]).then_inc(n2_ok, 1)
                    if live(s):
                        dve.wait_ge(out_mm, s + 1)
                        dve.wait_ge(a_bias_ok, s + 1)
                        upto(dve, z_ok, s)
                        nc.vector.tensor_tensor(y[:, :, :], ps[:, BK_OUT, :].rearrange("p (t d) -> p t d", t=T),
                                                a_bias[:, u, :, :], ALU.add).then_inc(y_ok, 1)
                        dve.wait_ge(y_ok, s + 1)
                        take_moments(core, dve, ln_y, lambda t: y[:, t, :], s)
                        dve.wait_ge(ln_y.rstd_done, s + 1)
                        upto(dve, x_ok, s)
                        normalize(nc, ln_y, lambda t: z[:, t, :], lambda t: y[:, t, :]).then_inc(z_ok, 1)

                run_steps(dve, step, -2, 1, 13, B)

            @block.gpsimd
            def _(pool):
                pool.wait_ge(weights_in, W_IN)

                def step(s, u):
                    g, f, gu, fu = s + 2, s + 1, u, 1 - u
                    if live(f):
                        pool.wait_ge(a_ok, f + 1)
                        upto(pool, y_ok, f - 1)
                        nc.gpsimd.tensor_tensor(
                            a_bias[:, fu, :, :], a[:, fu, :, :], b_out[:, :].unsqueeze(1).broadcast_to([P, T, D]),
                            ALU.add).then_inc(a_bias_ok, 1)
                    if live(g):
                        take_rstd(core, pool, ln_x, g)
                        take_rstd(core, pool, ln_a, g)
                    if live(f):
                        pool.wait_ge(qk_act_ok, f + 1)
                        upto(pool, score_mm, 3 * f)
                        nc.gpsimd.tensor_tensor(q_aff[:, :], qk_act[:, :], os_gamma[:, 0:1].broadcast_to([P, N]),
                                                ALU.mult).then_inc(q_aff_ok, 1)
                        pool.wait_ge(q_aff_ok, 2 * f + 1)
                        nc.gpsimd.tensor_tensor(q_aff[:, :], q_aff[:, :], os_beta[:, 0:1].broadcast_to([P, N]),
                                                ALU.add).then_inc(q_aff_ok, 1)
                        pool.wait_ge(q_aff_ok, 2 * f + 2)
                        nc.gpsimd.tensor_tensor(qT[:, :], q_aff[:, :], inv_pos[:, :], ALU.mult)
                        nc.gpsimd.tensor_scalar(kT[:, :], qk_act[:, :], os_gamma[:, 1:2], os_beta[:, 1:2],
                                                ALU.mult, ALU.add).then_inc(qk_ok, 1)
                    if live(s):
                        take_rstd(core, pool, ln_y, s)
                        pool.wait_ge(z_ok, s + 1)
                        pool.sem_inc(core.tick, 1)
                        nc.gpsimd.tensor_tensor(x[:, s, :, :], x[:, s, :, :], z[:, :, :], ALU.add).then_inc(x_ok, 1)

                run_steps(pool, step, -2, 1, 13, B)

            @block.scalar
            def _(act):
                act.wait_ge(weights_in, W_IN)

                def step(s, u):
                    f, fu = s + 1, 1 - u
                    if live(f):
                        act.wait_ge(nT_mm, f + 1)
                        nc.scalar.activation(nT[:, :], ps[:, BK_NT, :], ACT.Identity, bias=ln_b,
                                             scale=ln_g).then_inc(nT_ok, 1)
                    if live(s):
                        upto(act, attn_mm, 2 * s)
                        for bank, w in ((0, N), (1, N), (2, width(2))):
                            act.wait_ge(relu_ok, 3 * s + bank + 1)
                            nc.scalar.activation(prob[:, bank, 0:w], relu[:, bank, 0:w],
                                                 ACT.Square).then_inc(prob_ok, 1)
                    if live(f):
                        act.wait_ge(value_pre_ok, f + 1)
                        upto(act, attn_mm, 2 * (f - 1))
                        nc.scalar.activation(value[:, fu, :, :], value_pre[:, :, :], ACT.Silu).then_inc(value_ok, 1)
                        upto(act, gated_ok, 2 * (f - 1))
                        act.wait_ge(gate_mm, f + 1)
                        for j in range(2):
                            last = nc.scalar.activation(gateT[:, fu, j, :], ps[:, BK_GATE + j, :], ACT.Silu,
                                                        bias=b_gate[:, j:j + 1])
                        last.then_inc(gate_ok, 1)
                        act.wait_ge(qk_mm, f + 1)
                        upto(act, qk_ok, f)
                        nc.scalar.activation(qk_act[:, :], ps[:, BK_QK, :], ACT.Silu,
                                             bias=b_qk).then_inc(qk_act_ok, 1)

                run_steps(act, step, -2, 1, 13, B)

            @block.tensor
            def _(pe):
                pe.wait_ge(weights_in, W_IN)

                def step(s, u):
                    f, fu = s + 1, 1 - u
                    if live(f):
                        pe.wait_ge(n2_ok, f + 1)
                        upto(pe, qk_act_ok, f)
                        for t in range(T):
                            last = nc.tensor.transpose(ps[:, BK_NT, t * P:t * P + P], n2[:, t, :], core.ident[:, :])
                        last.then_inc(nT_mm, 1)
                    if live(s):
                        pe.wait_ge(qk_ok, s + 1)
                        upto(pe, y_ok, s)
                        for kt, bank, at in SCORES:
                            last = nc.tensor.matmul(ps[:, BK_SCORE + bank, at:at + width(kt)],
                                                    kT[:, kt * P:kt * P + P], qT[:, kt * P:N], start=True, stop=True)
                            if kt != 1:
                                last.then_inc(score_mm, 1)
                    if live(f):
                        pe.wait_ge(nT_ok, f + 1)
                        upto(pe, value_pre_ok, f)
                        for t in range(T):
                            last = nc.tensor.matmul(ps[:, BK_VALUE + t // 2, t % 2 * HID:t % 2 * HID + HID],
                                                    nT[:, t * P:t * P + P], w_hidden[:, 0:HID], start=True, stop=True)
                        last.then_inc(value_mm, 1)
                    if live(s):
                        pe.wait_ge(value_ok, s + 1)
                        pe.wait_ge(prob_ok, 3 * s + 3)
                        for j in range(2):
                            for i, (kt, bank, at) in enumerate(SCORES):
                                last = nc.tensor.matmul(ps[:, BK_ATTN + j, kt * P:N],
                                                        value[:, u, kt, j * P:j * P + P],
                                                        prob[:, bank, at:at + width(kt)], start=i == 0, stop=i == T - 1)
                            last.then_inc(attn_mm, 1)
                    if live(f):
                        upto(pe, gate_ok, f)
                        for j in range(2):
                            last = nc.tensor.matmul(ps[:, BK_GATE + j, :], w_hidden[:, HID + j * P:HID + j * P + P],
                                                    nT[:, :], start=True, stop=True)
                        last.then_inc(gate_mm, 1)
                        nc.tensor.matmul(ps[:, BK_QK, :], w_qk[:, :], nT[:, :], start=True,
                                         stop=True).then_inc(qk_mm, 1)
                    if live(s):
                        pe.wait_ge(gated_ok, 2 * s + 2)
                        for t in range(T):
                            for j in range(2):
                                last = nc.tensor.matmul(ps[:, BK_OUT, t * D:t * D + D],
                                                        gatedT[:, j, t * P:t * P + P], w_out[:, j, :],
                                                        start=j == 0, stop=j == 1)
                        last.then_inc(out_mm, 1)

                run_steps(pe, step, -2, 1, 13, B)


def channel_mix(core):
    nc, dram, x, ps = core.nc, core.dram, core.x, core.ps
    with ExitStack() as ctx:
        L = Layer(core, "mix", ctx)
        w_r, w_k, w_v = L.sb("w_r", [P, D]), L.sb("w_k", [P, D]), L.sb("w_v", [P, D])
        mu = L.sb("mu", [P, 2])
        mu_r, mu_k = mu[:, 0:1], mu[:, 1:2]
        a = L.sb("a", [P, T, D])
        aT = L.sb("aT", [P, 1 + N])
        step_aT = L.sb("step_aT", [P, N])
        mixed_r, mixed_k = L.sb("mixed_r", [P, N]), L.sb("mixed_k", [P, N])
        r = L.sb("r", [P, 2, T, D])
        relu_k, k_act = L.sb("relu_k", [P, N]), L.sb("k_act", [P, N])
        y, z = L.sb("y", [P, T, D]), L.sb("z", [P, T, D])
        ln_x, ln_y = Stats(L, "ln_x"), Stats(L, "ln_y")
        weights_in, zero_ok = L.sem("weights_in"), L.sem("zero_ok")
        a_ok, aT_mm, aT_ok = L.sem("a_ok"), L.sem("aT_mm"), L.sem("aT_ok")
        step_ok, mixed_ok = L.sem("step_ok"), L.sem("mixed_ok")
        k_mm, r_mm, r_ok, relu_ok, k_act_ok = (L.sem("k_mm"), L.sem("r_mm"), L.sem("r_ok"), L.sem("relu_ok"),
                                               L.sem("k_act_ok"))
        out_mm, y_ok, z_ok, x_ok = L.sem("out_mm"), L.sem("y_ok"), L.sem("z_ok"), L.sem("x_ok")
        BK_AT, BK_K, BK_R, BK_OUT = 0, 1, 2, 3
        w_loads = [(w_r[:, :], dram["W_r_T"]), (w_k[:, :], dram["W_k_T"]), (w_v[:, :], dram["W_v_T"]),
                   (mu[:, :], dram["mix_vectors"])]
        W_IN = 16 * len(w_loads)

        with nc.Block() as block:
            @block.sync
            def _(sp):
                for dst, src in w_loads:
                    sp.dma_start(dst, src).then_inc(weights_in, 16)

            @block.vector
            def _(dve):
                nc.vector.memset(aT[:, 0:1], 0.0).then_inc(zero_ok, 1)
                dve.wait_ge(zero_ok, 1)
                dve.wait_ge(weights_in, W_IN)

                def step(s, u):
                    g, f = s + 2, s + 1
                    if live(s):
                        dve.wait_ge(out_mm, s + 1)
                        dve.wait_ge(r_ok, s + 1)
                        upto(dve, z_ok, s)
                        nc.vector.tensor_tensor(y[:, :, :], ps[:, BK_OUT, :].rearrange("p (t d) -> p t d", t=T),
                                                r[:, u, :, :], ALU.mult).then_inc(y_ok, 1)
                        dve.wait_ge(y_ok, s + 1)
                        take_moments(core, dve, ln_y, lambda t: y[:, t, :], s)
                    if live(g):
                        take_moments(core, dve, ln_x, lambda t: x[:, g, t, :], g)
                    if live(f):
                        dve.wait_ge(aT_ok, f + 1)
                        upto(dve, mixed_ok, 2 * f)
                        nc.vector.tensor_tensor(step_aT[:, :], aT[:, 1:1 + N], aT[:, 0:N],
                                                ALU.subtract).then_inc(step_ok, 1)
                        dve.wait_ge(step_ok, f + 1)
                        upto(dve, k_mm, f)
                        nc.vector.scalar_tensor_tensor(mixed_k[:, :], step_aT[:, :], mu_k, aT[:, 0:N],
                                                       ALU.mult, ALU.add).then_inc(mixed_ok, 1)
                        upto(dve, r_mm, f)
                        nc.vector.scalar_tensor_tensor(mixed_r[:, :], step_aT[:, :], mu_r, aT[:, 0:N],
                                                       ALU.mult, ALU.add).then_inc(mixed_ok, 1)
                    if live(s):
                        dve.wait_ge(ln_y.rstd_done, s + 1)
                        upto(dve, x_ok, s)
                        normalize(nc, ln_y, lambda t: z[:, t, :], lambda t: y[:, t, :]).then_inc(z_ok, 1)
                    if live(g):
                        dve.wait_ge(ln_x.rstd_done, g + 1)
                        upto(dve, aT_mm, g)
                        normalize(nc, ln_x, lambda t: a[:, t, :], lambda t: x[:, g, t, :]).then_inc(a_ok, 1)

                run_steps(dve, step, -2, 1, 13, B)

            @block.gpsimd
            def _(pool):
                def step(s, u):
                    g, f = s + 2, s + 1
                    if live(s):
                        take_rstd(core, pool, ln_y, s)
                    if live(g):
                        take_rstd(core, pool, ln_x, g)
                    if live(f):
                        pool.wait_ge(relu_ok, f + 1)
                        upto(pool, out_mm, f)
                        nc.gpsimd.tensor_tensor(k_act[:, :], relu_k[:, :], relu_k[:, :],
                                                ALU.mult).then_inc(k_act_ok, 1)
                    if live(s):
                        pool.wait_ge(z_ok, s + 1)
                        pool.sem_inc(core.tick, 1)
                        nc.gpsimd.tensor_tensor(x[:, s, :, :], x[:, s, :, :], z[:, :, :], ALU.add).then_inc(x_ok, 1)

                run_steps(pool, step, -2, 1, 13, B)

            @block.scalar
            def _(act):
                def step(s, u):
                    f, fu = s + 1, 1 - u
                    if live(f):
                        act.wait_ge(aT_mm, f + 1)
                        upto(act, mixed_ok, 2 * f)
                        nc.scalar.copy(aT[:, 1:1 + N], ps[:, BK_AT, :]).then_inc(aT_ok, 1)
                        act.wait_ge(k_mm, f + 1)
                        upto(act, k_act_ok, f)
                        nc.scalar.activation(relu_k[:, :], ps[:, BK_K, :], ACT.Relu).then_inc(relu_ok, 1)
                        act.wait_ge(r_mm, f + 1)
                        upto(act, y_ok, f - 1)
                        nc.scalar.activation(r[:, fu, :, :], ps[:, BK_R, :].rearrange("p (t d) -> p t d", t=T),
                                             ACT.Sigmoid).then_inc(r_ok, 1)

                run_steps(act, step, -2, 1, 13, B)

            @block.tensor
            def _(pe):
                pe.wait_ge(weights_in, W_IN)

                def step(s, u):
                    f = s + 1
                    if live(s):
                        pe.wait_ge(k_act_ok, s + 1)
                        upto(pe, y_ok, s)
                        for t in range(T):
                            last = nc.tensor.matmul(ps[:, BK_OUT, t * D:t * D + D], k_act[:, t * P:t * P + P],
                                                    w_v[:, :], start=True, stop=True)
                        last.then_inc(out_mm, 1)
                    if live(f):
                        pe.wait_ge(a_ok, f + 1)
                        upto(pe, aT_ok, f)
                        for t in range(T):
                            last = nc.tensor.transpose(ps[:, BK_AT, t * P:t * P + P], a[:, t, :], core.ident[:, :])
                        last.then_inc(aT_mm, 1)
                        pe.wait_ge(mixed_ok, 2 * f + 1)
                        upto(pe, relu_ok, f)
                        nc.tensor.matmul(ps[:, BK_K, :], w_k[:, :], mixed_k[:, :], start=True,
                                         stop=True).then_inc(k_mm, 1)
                        pe.wait_ge(mixed_ok, 2 * f + 2)
                        upto(pe, r_ok, f)
                        for t in range(T):
                            last = nc.tensor.matmul(ps[:, BK_R, t * D:t * D + D], mixed_r[:, t * P:t * P + P],
                                                    w_r[:, :], start=True, stop=True)
                        last.then_inc(r_mm, 1)

                run_steps(pe, step, -2, 1, 13, B)


SLOTS = 20
GROUPS, GH = 4, 4
SHARED = ((0, "aT", 2), (1, "top_late", 0), (2, "q", 2), (3, "natural_late", -1), (4, "q_turned", 2),
          (5, "oT", -1), (6, "k", 2), (7, "out", -1), (8, "natural_0", 0), (9, "k_turned", 2), (11, "v", 1),
          (13, "natural_1", 0), (15, "top_early", 1), (18, "natural_2", 0))
FIRST_STEP = -3


def shared_user_before(s, task):
    uses = [(s + back + ahead, name) for back in (-1, 0) for _, name, ahead in SHARED]
    at = len(SHARED) + [name for _, name, _ in SHARED].index(task)
    earlier = [(name, b) for b, name in uses[:at] if live(b)]
    return earlier[-1] if earlier else None


def top_unit_parts(n, i):
    half, j = divmod(n, SLOTS // 2)
    h = half * HH
    if j < 4:
        return [(3, h + 2 * j + i, 0)], (3 * P, 1)
    if j < 8:
        h += 2 * (j - 4) + i
        return [(2, h, 0), (0, h, 3 * P)], (2 * P, 2)
    h += 4 * (j - 8) + 2 * i
    return [(1, h, 0), (1, h + 1, 2 * P)], (P, 2)


def causal_attention(core):
    nc, dram, x, ps = core.nc, core.dram, core.x, core.ps
    with ExitStack() as ctx:
        L = Layer(core, "att", ctx)
        names = ("Wq_T", "Wq_turned_T", "Wk_T", "Wk_turned_T", "Wv_T", "Wo_T")
        w_q, w_q_turned, w_k, w_k_turned, w_v, w_o = (L.sb(name, [P, D]) for name in names)
        cos, sin = L.sb("cos", [P, N]), L.sb("sin", [P, N])
        future, future_bf = L.sb("future", [P, 2 * P]), L.sb("future_bf", [P, 2, P], BF16)
        a = L.sb("a", [P, T, D])
        aT = L.sb("aT", [P, 2, N])
        by_cos, by_sin = L.sb("by_cos", [P, N]), L.sb("by_sin", [P, N])
        full, rest = L.sb("full", [P, N]), L.sb("rest", [P, N])
        q_parts, k_parts = L.sb("q_parts", [P, 3, N], BF16), L.sb("k_parts", [P, 3, N], BF16)
        q_stack, k_stack = L.sb("q_stack", [KM, 2, NH, N], BF16), L.sb("k_stack", [KM, 2, NH, N], BF16)
        ones = L.sb("ones", [2, N], BF16)
        v = L.sb("v", [P, 2, T, NH, 32])
        top = L.sb("top", [P, T, NH])
        top_parts = L.sb("top_parts", [P, 2, T, 2, HH], BF16)
        top_row = L.sb("top_row", [2 * HH, N], BF16)
        e = L.sb("e", [P, 5, 2 * N])
        oT = L.sb("o_groupT", [P, N])
        o_rsum = L.sb("o_rsum", [P, T, GH])
        o, o_T = L.sb("o", [P, T, NH, DH]), L.sb("o_T", [P, N])
        y, z = L.sb("y", [P, T, D]), L.sb("z", [P, T, D])
        ln_x, ln_y = Stats(L, "ln_x"), Stats(L, "ln_y")

        weights_in, made, ones_in = L.sem("weights_in"), L.sem("made"), L.sem("ones_in")
        future_ok, v_made = L.sem("future_ok"), L.sem("v_made")
        a_ok, aT_mm, aT_ok = L.sem("a_ok"), L.sem("aT_mm"), L.sem("aT_ok")
        qk_mm = L.sem("qk_mm")
        rope_ok, full_ok, rest_ok, part_ok = L.sem("rope_ok"), L.sem("full_ok"), L.sem("rest_ok"), L.sem("part_ok")
        rest_last_ok = L.sem("rest_last_ok")
        stack_in = [L.sem("stack_in_early"), L.sem("stack_in_late")]
        v_mm, v_ok = L.sem("v_mm"), L.sem("v_ok")
        top_mm, top_ok, hi_ok, parts_ok = L.sem("top_mm"), L.sem("top_ok"), L.sem("hi_ok"), L.sem("parts_ok")
        row_mm, row_ok, row_in = L.sem("row_mm"), L.sem("row_ok"), L.sem("row_in")
        score_mm, exp_ok, causal_ok = L.sem("score_mm"), L.sem("exp_ok"), L.sem("causal_ok")
        attn_mm, oT_ok = L.sem("attn_mm"), L.sem("oT_ok")
        natural_mm, rsum_ok, o_ok = L.sem("natural_mm"), L.sem("rsum_ok"), L.sem("o_ok")
        o_T_mm, o_T_ok, out_mm, y_ok, z_ok, x_ok = (L.sem("o_T_mm"), L.sem("o_T_ok"), L.sem("out_mm"), L.sem("y_ok"),
                                                    L.sem("z_ok"), L.sem("x_ok"))

        BK_SCORE, BK_TOP, BK_ATTN, BK_SHARED = 0, 2, 6, 7
        shared = ps[:, BK_SHARED, :]
        shared_td = shared.rearrange("p (t d) -> p t d", t=T)
        shared_bf = shared.bitcast(BF16)
        STACK_IN = 16 * 2 * len(PARTS_Q)

        def e_heads(j):
            return e[:, j, :].rearrange("p (h c) -> p h c", h=2 if j < 4 else 4)

        UNIT = ((0, (0, 1)), (0, (2, 3)), (1, (0, 1)), (1, (2, 3)), (2, (0, 1, 2, 3)))

        w_loads = [(w[:, :], dram[name]) for w, name in zip((w_q, w_q_turned, w_k, w_k_turned, w_v, w_o), names)]
        w_loads += [(cos[:, :], dram["cos"]), (sin[:, :], dram["sin"]), (future[:, :], dram["future"])]
        W_IN = 16 * len(w_loads)

        with nc.Block() as block:
            @block.sync
            def _(sp):
                def load_top_row(b, half, u):
                    sp.wait_ge(row_ok, 2 * b + half + 1)
                    sp.dma_start(q_stack[KS:KM, u, half * HH:half * HH + HH, :],
                                 top_row[:, :]).then_inc(row_in, 16)

                def load_stacks(g, half, u):
                    for w, (stack, source, which) in enumerate(((q_stack, q_parts, PARTS_Q),
                                                                (k_stack, k_parts, PARTS_K))):
                        sp.wait_ge(rest_last_ok, 2 * g + w + 1)
                        for c, part in enumerate(which):
                            sp.dma_start(stack[c * DH:c * DH + DH, u, half * HH:half * HH + HH, :],
                                         source[half * DH * HH:half * DH * HH + DH * HH, part, :],
                                         ).then_inc(stack_in[half], 16)

                def step(s, u):
                    g, m = s + 2, s + 1
                    if live(s):
                        load_top_row(s, 1, u)
                        sp.wait_ge(score_mm, SLOTS * (2 * s + 1))
                    if live(g):
                        load_stacks(g, 0, u)
                    if live(m):
                        load_top_row(m, 0, 1 - u)
                    if live(g):
                        if live(s):
                            sp.wait_ge(score_mm, SLOTS * (2 * s + 2))
                        load_stacks(g, 1, u)

                for dst, src in w_loads:
                    sp.dma_start(dst, src).then_inc(weights_in, 16)
                sp.wait_ge(made, 1)
                sp.dma_start(k_stack[KS:KM, :, :, :].rearrange("r u h n -> r (u h) n"),
                             ones[:, :].unsqueeze(1).broadcast_to([2, 2 * NH, N])).then_inc(ones_in, 16)
                run_steps(sp, step, FIRST_STEP, 3, 13, B)

            @block.vector
            def _(dve):
                def reduce_unit(m, n):
                    dve.wait_ge(top_mm, SLOTS * m + n + 1)
                    banks = ps[:, BK_TOP + n % 2 * 2:BK_TOP + n % 2 * 2 + 2, :]
                    (qt, h, _), *more = top_unit_parts(n, 0)[0]
                    if qt == 3:
                        r = nc.vector.reduce_max(top[:, 3, h:h + 2], banks, AXX)
                    elif qt == 2:
                        nc.vector.reduce_max(top[:, 2, h:h + 2], banks[:, :, 0:3 * P], AXX)
                        r = nc.vector.reduce_max(top[:, 0, h:h + 2], banks[:, :, 3 * P:N], AXX)
                    else:
                        r = nc.vector.reduce_max(top[:, 1, h:h + 4], banks.rearrange("p i (h c) -> p (i h) c", h=2),
                                                 AXX)
                    r.then_inc(top_ok, 1)

                def split_top(m, half):
                    k = 2 * m + half
                    dve.wait_ge(top_ok, SLOTS * m + SLOTS // 2 * (half + 1))
                    upto(dve, row_mm, k - 1)
                    src = top[:, :, half * HH:half * HH + HH]
                    nc.vector.tensor_scalar(top_parts[:, half, :, 0, :], src, -1.0, None, ALU.mult).then_inc(hi_ok, 1)
                    dve.wait_ge(hi_ok, k + 1)
                    nc.vector.scalar_tensor_tensor(top_parts[:, half, :, 1, :], src, -1.0,
                                                   top_parts[:, half, :, 0, :], ALU.mult,
                                                   ALU.subtract).then_inc(parts_ok, 1)

                def rotate(g, i):
                    dve.wait_ge(qk_mm, 4 * g + i + 1)
                    upto(dve, full_ok, 2 * g + i // 2)
                    out, table = ((by_cos, cos), (by_sin, sin))[i % 2]
                    nc.vector.tensor_tensor(out[:, :], shared, table[:, :], ALU.mult).then_inc(rope_ok, 1)

                def normal_group(b, group):
                    k = GROUPS * b + group
                    dve.wait_ge(natural_mm, k + 1)
                    heads = shared.rearrange("p (t h c) -> p t h c", t=T, h=GH)
                    nc.vector.reciprocal(o_rsum[:, :, :], heads[:, :, :, DH]).then_inc(rsum_ok, 1)
                    dve.wait_ge(rsum_ok, k + 1)
                    if group == 0:
                        upto(dve, o_T_mm, b)
                    nc.vector.tensor_tensor(o[:, :, group * GH:group * GH + GH, :], heads[:, :, :, 0:DH],
                                            o_rsum[:, :, :].unsqueeze(3).broadcast_to([P, T, GH, DH]),
                                            ALU.mult).then_inc(o_ok, 1)

                def step(s, u):
                    l, g, m, p = s + 3, s + 2, s + 1, s - 1
                    for n in range(SLOTS):
                        if live(m):
                            reduce_unit(m, n)
                        for i, slot in enumerate((2, 4, 6, 9)):
                            if live(g) and n == slot:
                                rotate(g, i)
                        if live(p) and n == 3:
                            normal_group(p, 3)
                        for group, slot in enumerate((8, 13, 18)):
                            if live(s) and n == slot:
                                normal_group(s, group)
                        if live(p) and n == 10:
                            dve.wait_ge(y_ok, p + 1)
                            take_moments(core, dve, ln_y, lambda t: y[:, t, :], p)
                        if live(m) and n == 11:
                            split_top(m, 0)
                        if live(p) and n == 14:
                            dve.wait_ge(ln_y.rstd_done, p + 1)
                            upto(dve, x_ok, p)
                            normalize(nc, ln_y, lambda t: z[:, t, :], lambda t: y[:, t, :]).then_inc(z_ok, 1)
                        if live(l) and n == 12:
                            take_moments(core, dve, ln_x, lambda t: x[:, l, t, :], l)
                        if live(l) and n == 16:
                            dve.wait_ge(ln_x.rstd_done, l + 1)
                            upto(dve, aT_mm, l)
                            normalize(nc, ln_x, lambda t: a[:, t, :], lambda t: x[:, l, t, :]).then_inc(a_ok, 1)
                    if live(m):
                        split_top(m, 1)

                nc.vector.memset(ones[:, :], 1.0).then_inc(made, 1)
                step(FIRST_STEP, 1)
                dve.wait_ge(weights_in, W_IN)
                nc.vector.tensor_copy(future_bf[:, :, :], future[:, :].rearrange("p (i c) -> p i c",
                                                                                i=2)).then_inc(future_ok, 1)
                run_steps(dve, step, FIRST_STEP + 1, 3, 13, B + 1)

            @block.gpsimd
            def _(pool):
                def add_rotated(g, w):
                    k = 2 * g + w
                    pool.wait_ge(rope_ok, 4 * g + 2 * w + 2)
                    upto(pool, rest_ok, k)
                    nc.gpsimd.tensor_tensor(full[:, :], by_cos[:, :], by_sin[:, :], ALU.add).then_inc(full_ok, 1)

                def take_rest(g, w, part):
                    k = 2 * g + w
                    parts = (q_parts, k_parts)[w]
                    pool.wait_ge(part_ok, 2 * k + part + 1)
                    if part == 0:
                        upto(pool, rest_last_ok, k)
                        nc.gpsimd.tensor_tensor(rest[:, :], full[:, :], parts[:, 0, :],
                                                ALU.subtract).then_inc(rest_ok, 1)
                    else:
                        pool.wait_ge(rest_ok, k + 1)
                        if w == 0:
                            for half in range(2):
                                upto(pool, stack_in[half], STACK_IN * g)
                        nc.gpsimd.tensor_tensor(parts[:, 2, :], rest[:, :], parts[:, 1, :],
                                                ALU.subtract).then_inc(rest_last_ok, 1)

                def keep_causal(s, n):
                    j = n % 5
                    pool.wait_ge(exp_ok, 2 * SLOTS * s + 2 * n + 2)
                    pool.sem_inc(core.tick, 1)
                    if j in (2, 3):
                        blocks = e_heads(j)[:, :, 0:2 * P]
                        pattern = [[0, 2], [0, 2], [1, P]]
                    else:
                        blocks = e_heads(j)[:, :, 0:P]
                        pattern = [[0, 2 if j < 4 else 4], [1, P]]
                    nc.gpsimd.affine_select(blocks, blocks, pattern, ALU.is_ge, 0.0, 0, -1).then_inc(causal_ok, 1)

                def step(s, u):
                    l, g, p = s + 3, s + 2, s - 1
                    for n in range(SLOTS):
                        if live(s):
                            keep_causal(s, n)
                        if live(g):
                            for w, slot in ((0, 5), (1, 10)):
                                if n == slot:
                                    add_rotated(g, w)
                                if n == slot + 1:
                                    take_rest(g, w, 0)
                                if n == slot + 3:
                                    take_rest(g, w, 1)
                        if live(p) and n == 12:
                            take_rstd(core, pool, ln_y, p)
                        if live(p) and n == 16:
                            pool.wait_ge(z_ok, p + 1)
                            pool.sem_inc(core.tick, 1)
                            nc.gpsimd.tensor_tensor(x[:, p, :, :], x[:, p, :, :], z[:, :, :],
                                                    ALU.add).then_inc(x_ok, 1)
                        if live(l) and n == 14:
                            take_rstd(core, pool, ln_x, l)

                step(FIRST_STEP, 1)
                nc.gpsimd.memset(v[:, :, :, :, DH:DH + 1], 1.0).then_inc(v_made, 1)
                nc.gpsimd.memset(v[:, :, :, :, DH + 1:32], 0.0).then_inc(v_made, 1)
                run_steps(pool, step, FIRST_STEP + 1, 3, 13, B + 1)

            @block.scalar
            def _(act):
                def exp_unit(s, n):
                    group, j = divmod(n, 5)
                    k = GROUPS * s + group
                    upto(act, attn_mm, 3 * (k - 1) + (1, 1, 2, 2, 3)[j])
                    for i in range(2):
                        act.wait_ge(score_mm, 2 * SLOTS * s + 2 * n + i + 1)
                        nc.scalar.activation(e[:, j, i * N:i * N + N], ps[:, BK_SCORE + i, :], ACT.Exp,
                                             scale=DH ** -0.5).then_inc(exp_ok, 1)

                def take_part(g, w, part):
                    k = 2 * g + w
                    act.wait_ge((full_ok, rest_ok)[part], k + 1)
                    if part == 0 and w == 0:
                        for half in range(2):
                            upto(act, stack_in[half], STACK_IN * g)
                    nc.scalar.copy((q_parts, k_parts)[w][:, part, :],
                                   (full, rest)[part][:, :]).then_inc(part_ok, 1)

                def take_group(s, group):
                    k = GROUPS * s + group
                    act.wait_ge(attn_mm, 3 * k + 3)
                    upto(act, natural_mm, k)
                    nc.scalar.copy(oT[:, :], ps[:, BK_ATTN, :]).then_inc(oT_ok, 1)

                def take_top_rows(b, half):
                    k = 2 * b + half
                    act.wait_ge(row_mm, k + 1)
                    upto(act, row_in, 16 * k)
                    nc.scalar.copy(top_row[:, :], shared_bf[0:2 * HH, 0:N]).then_inc(row_ok, 1)

                def step(s, u):
                    g, m, p = s + 2, s + 1, s - 1
                    for n in range(SLOTS):
                        if live(s):
                            exp_unit(s, n)
                        if live(g) and n == 0:
                            act.wait_ge(aT_mm, g + 1)
                            upto(act, v_mm, g - 1)
                            nc.scalar.copy(aT[:, u, :], shared).then_inc(aT_ok, 1)
                        for w, slots in ((0, (6, 8)), (1, (11, 13))):
                            if live(g) and n in slots:
                                take_part(g, w, slots.index(n))
                        if live(s) and n == 1:
                            take_top_rows(s, 1)
                        if live(p) and n == 1:
                            take_group(p, 3)
                        if live(p) and n == 5:
                            act.wait_ge(o_T_mm, p + 1)
                            upto(act, out_mm, p)
                            nc.scalar.copy(o_T[:, :], shared).then_inc(o_T_ok, 1)
                        for group, slot in enumerate((6, 11, 16)):
                            if live(s) and n == slot:
                                take_group(s, group)
                        if live(p) and n == 7:
                            act.wait_ge(out_mm, p + 1)
                            upto(act, z_ok, p)
                            nc.scalar.copy(y[:, :, :], shared_td).then_inc(y_ok, 1)
                        if live(m) and n == 11:
                            act.wait_ge(v_mm, m + 1)
                            upto(act, attn_mm, 3 * GROUPS * (m - 1))
                            nc.scalar.copy(v[:, 1 - u, :, :, 0:DH], shared.rearrange(
                                "p (t h d) -> p t h d", t=T, h=NH)).then_inc(v_ok, 1)
                        if live(m) and n == 15:
                            take_top_rows(m, 0)

                run_steps(act, step, FIRST_STEP, 3, 13, B + 1)

            @block.tensor
            def _(pe):
                def score_unit(s, n, i, u):
                    group, j = divmod(n, 5)
                    if n % (SLOTS // 2) == 0 and i == 0:
                        pe.wait_ge(row_in, 16 * (2 * s + n // (SLOTS // 2) + 1))
                    upto(pe, exp_ok, 2 * SLOTS * s + 2 * n + i - 1)
                    kt, heads = UNIT[j]
                    for k, h in enumerate(heads[len(heads) // 2 * i:len(heads) // 2 * (i + 1)]):
                        head = group * GH + h
                        for tile, c in ((3, 0), (1, P)) if kt == 1 else ((kt, 2 * P * k),):
                            last = nc.tensor.matmul(
                                ps[:, BK_SCORE + i, c:c + N - tile * P],
                                k_stack[:, u, head, tile * P:tile * P + P], q_stack[:, u, head, tile * P:N],
                                start=True, stop=True)
                    last.then_inc(score_mm, 1)

                def top_unit(m, n, i, u):
                    if n % (SLOTS // 2) == 0 and i == 0:
                        pe.wait_ge(stack_in[n // (SLOTS // 2)], STACK_IN * (m + 1))
                    if i == 0:
                        upto(pe, top_ok, SLOTS * m + n - 1)
                    bank = ps[:, BK_TOP + n % 2 * 2 + i, :]
                    parts, (mask_at, masks) = top_unit_parts(n, i)
                    for j, (qt, head, c) in enumerate(parts):
                        nc.tensor.matmul(bank[:, c:c + (qt + 1) * P], q_stack[0:KS, u, head, qt * P:qt * P + P],
                                         k_stack[0:KS, u, head, 0:(qt + 1) * P], start=j == 0, stop=False,
                                         skip_group_check=True)
                    if masks == 1:
                        out = bank[:, mask_at:mask_at + P]
                    else:
                        stride = P if mask_at == 2 * P else 2 * P
                        out = bank.rearrange("p (i c) -> p i c", c=P)[:, mask_at // P::stride // P, :]
                    last = nc.tensor.matmul(out, core.ident_bf[:, :], future_bf[:, 0:masks, :], start=False,
                                            stop=True, skip_group_check=True)
                    if i == 1:
                        last.then_inc(top_mm, 1)

                def attend(b, group, part, u):
                    if part == 0:
                        if group == 0:
                            pe.wait_ge(v_ok, b + 1)
                        upto(pe, oT_ok, GROUPS * b + group)
                    pe.wait_ge(causal_ok, SLOTS * b + 5 * group + (2, 4, 5)[part])
                    for tile in ((0,), (1, 3), (2,))[part]:
                        for h in range(GH):
                            if tile == 2:
                                src = e_heads(4)[:, h, :]
                            else:
                                j = (0 if tile == 0 else 2) + h // 2
                                c = P if tile == 1 else 0
                                src = e_heads(j)[:, h % 2, c:c + N - tile * P]
                            last = nc.tensor.matmul(ps[32 * h:32 * h + 32, BK_ATTN, tile * P:N],
                                                    v[:, u, tile, group * GH + h, :], src, start=tile == 0,
                                                    stop=tile == 2, tile_position=(0, 32 * h), skip_group_check=True)
                    last.then_inc(attn_mm, 1)

                def use_shared(s, task):
                    before = shared_user_before(s, task)
                    if before is None:
                        return
                    name, b = before
                    if name == "aT":
                        pe.wait_ge(aT_ok, b + 1)
                    elif name in ("top_early", "top_late"):
                        pe.wait_ge(row_ok, 2 * b + 1 + (name == "top_late"))
                    elif name in ("q", "q_turned", "k", "k_turned"):
                        i = ("q", "q_turned", "k", "k_turned").index(name)
                        pe.wait_ge(rope_ok, 4 * b + i + 1)
                    elif name == "v":
                        pe.wait_ge(v_ok, b + 1)
                    elif name == "oT":
                        pe.wait_ge(o_T_ok, b + 1)
                    elif name == "out":
                        pe.wait_ge(y_ok, b + 1)
                    else:
                        group = 3 if name == "natural_late" else int(name[-1])
                        pe.wait_ge(o_ok, GROUPS * b + group + 1)

                def natural(b, group):
                    pe.wait_ge(oT_ok, GROUPS * b + group + 1)
                    for t in range(T):
                        last = nc.tensor.transpose(shared_td[:, t, :], oT[:, t * P:t * P + P], core.ident[:, :])
                    last.then_inc(natural_mm, 1)

                def top_rows(b, half):
                    pe.wait_ge(parts_ok, 2 * b + half + 1)
                    for t in range(T):
                        last = nc.tensor.transpose(shared_bf[0:2 * HH, t * P:t * P + P],
                                                   top_parts[:, half, t, :, :], core.ident_bf[:, :])
                    last.then_inc(row_mm, 1)

                def step(s, u):
                    g, m, p = s + 2, s + 1, s - 1
                    for n in range(SLOTS):
                        for i in range(2):
                            if live(s):
                                score_unit(s, n, i, u)
                            if live(m):
                                top_unit(m, n, i, 1 - u)
                        if n == 0 and live(p):
                            attend(p, 3, 1, 1 - u)
                        if n == 1 and live(p):
                            attend(p, 3, 2, 1 - u)
                        if live(s):
                            if n % 5 == 3:
                                attend(s, n // 5, 0, u)
                            if n % 5 == 0 and n:
                                attend(s, n // 5 - 1, 1, u)
                            if n % 5 == 1 and n > 1:
                                attend(s, n // 5 - 1, 2, u)
                        for slot, task, ahead in SHARED:
                            if slot != n or not live(s + ahead):
                                continue
                            use_shared(s, task)
                            if task == "aT":
                                pe.wait_ge(a_ok, g + 1)
                                for t in range(T):
                                    last = nc.tensor.transpose(shared_td[:, t, :], a[:, t, :], core.ident[:, :])
                                last.then_inc(aT_mm, 1)
                            elif task in ("q", "q_turned", "k", "k_turned"):
                                if task == "q":
                                    pe.wait_ge(aT_ok, g + 1)
                                w = {"q": w_q, "q_turned": w_q_turned, "k": w_k, "k_turned": w_k_turned}[task]
                                nc.tensor.matmul(shared, w[:, :], aT[:, u, :], start=True,
                                                 stop=True).then_inc(qk_mm, 1)
                            elif task == "v":
                                for t in range(T):
                                    last = nc.tensor.matmul(shared_td[:, t, :], aT[:, 1 - u, t * P:t * P + P],
                                                            w_v[:, :], start=True, stop=True)
                                last.then_inc(v_mm, 1)
                            elif task == "top_late":
                                top_rows(s, 1)
                            elif task == "top_early":
                                top_rows(m, 0)
                            elif task == "natural_late":
                                natural(p, 3)
                            elif task.startswith("natural"):
                                natural(s, int(task[-1]))
                            elif task == "oT":
                                pe.wait_ge(o_ok, GROUPS * p + GROUPS)
                                for t in range(T):
                                    last = nc.tensor.transpose(shared_td[:, t, :], o[:, t, :, :].rearrange(
                                        "p h d -> p (h d)"), core.ident[:, :])
                                last.then_inc(o_T_mm, 1)
                            elif task == "out":
                                pe.wait_ge(o_T_ok, p + 1)
                                for t in range(T):
                                    last = nc.tensor.matmul(shared_td[:, t, :], o_T[:, t * P:t * P + P],
                                                            w_o[:, :], start=True, stop=True)
                                last.then_inc(out_mm, 1)

                pe.wait_ge(weights_in, W_IN)
                step(FIRST_STEP, 1)
                step(FIRST_STEP + 1, 0)
                pe.wait_ge(future_ok, 1)
                step(FIRST_STEP + 2, 1)
                pe.wait_ge(ones_in, 16)
                pe.wait_ge(v_made, 2)
                run_steps(pe, step, 0, 3, 13, B + 1)


def soft_mixture(core):
    nc, dram, x, ps = core.nc, core.dram, core.x, core.ps
    with ExitStack() as ctx:
        L = Layer(core, "moe", ctx)
        w1, w2 = L.sb("w1", [P, FF]), L.sb("w2", [P, FF // P, D])
        gamma_row, gamma_slot_row = L.sb("gamma_row", [P, D]), L.sb("gamma_slot_row", [P, D])
        gamma = L.sb("gamma", [P, 1])
        slot_raw, slot_n = L.sb("slot_raw", [P, T, D]), L.sb("slot_n", [P, T, D])
        slotT, slotT_bf = L.sb("slotT", [P, E_T]), L.sb("slotT_bf", [P, E_T], BF16)
        ones = L.sb("ones", [2, P], BF16)
        a, unit = L.sb("a", [P, T, D]), L.sb("unit", [P, T, D])
        mean_sq, mean_sq_sum, rrms = L.sb("mean_sq", [P, T]), L.sb("mean_sq_sum", [P, T]), L.sb("rrms", [P, T])
        token = L.sb("token", [P, 2, T, D + 1])
        tokenT, tokenT_bf = L.sb("tokenT", [P, 2, N]), L.sb("tokenT_bf", [P, N], BF16)
        top = L.sb("top", [P, 2 * T])
        top_parts = L.sb("top_parts", [P, 2 * T, 2], BF16)
        top_row = L.sb("top_row", [2, 2, 2 * T, P], BF16)
        weight = L.sb("weight", [P, 2 * T, N])
        slot_rsum, slot_in = L.sb("slot_rsum", [P, T]), L.sb("slot_in", [P, T, D])
        slot_inT, hiddenT = L.sb("slot_inT", [P, E_T]), L.sb("hiddenT", [P, FF // P, E_T])
        slot_out = L.sb("slot_out", [P, T, D + 1])
        y_rsum, y, z = L.sb("y_rsum", [P, T]), L.sb("y", [P, T, D]), L.sb("z", [P, T, D])
        ln_x, rms, ln_y = Stats(L, "ln_x"), Stats(L, "rms"), Stats(L, "ln_y")

        weights_in, made = L.sem("weights_in"), L.sem("made")
        a_ok, mean_sq_ok, rrms_ok, unit_ok = L.sem("a_ok"), L.sem("mean_sq_ok"), L.sem("rrms_ok"), L.sem("unit_ok")
        token_ok, tokenT_mm, tokenT_ok, tokenT_bf_ok = (L.sem("token_ok"), L.sem("tokenT_mm"), L.sem("tokenT_ok"),
                                                        L.sem("tokenT_bf_ok"))
        top_mm, top_ok, hi_ok, parts_ok = L.sem("top_mm"), L.sem("top_ok"), L.sem("hi_ok"), L.sem("parts_ok")
        row_mm, row_ok = L.sem("row_mm"), L.sem("row_ok")
        logit_mm, weight_ok = L.sem("logit_mm"), L.sem("weight_ok")
        slot_mm, slot_rsum_ok, slot_ok = L.sem("slot_mm"), L.sem("slot_rsum_ok"), L.sem("slot_ok")
        slotT_mm, slotT_ok = L.sem("slotT_mm"), L.sem("slotT_ok")
        hidden_mm, hidden_ok = L.sem("hidden_mm"), L.sem("hidden_ok")
        slot_out_mm, slot_out_ok = L.sem("slot_out_mm"), L.sem("slot_out_ok")
        out_mm, y_rsum_ok, y_ok, z_ok, x_ok = (L.sem("out_mm"), L.sem("y_rsum_ok"), L.sem("y_ok"), L.sem("z_ok"),
                                               L.sem("x_ok"))
        stored = L.sem("stored")

        BK_T, BK_TOP, BK_ROW, BK_LOGIT, BK_WIDE = 0, 1, 3, 4, 6
        row_ps = ps[:, BK_ROW, :].bitcast(BF16)

        def wide(t):
            return ps[:, BK_WIDE + t // 2, t % 2 * (D + 1):t % 2 * (D + 1) + D + 1]

        def wide_sums(bank):
            return ps[:, BK_WIDE + bank, 0:2 * (D + 1)].rearrange("p (t c) -> p t c", t=2)[:, :, D]

        w_loads = [(w1[:, :], dram["w1"]), (w2[:, :, :], dram["w2"].rearrange("(j p) d -> p j d", p=P)),
                   (gamma_row[:, :], dram["gamma_x"].partition_broadcast(P)),
                   (gamma_slot_row[:, :], dram["gamma_slot"].partition_broadcast(P)),
                   (gamma[:, :], dram["gamma_x"].rearrange("(p o) -> p o", o=1)),
                   (slot_raw[:, :, :], dram["slot_embeds"].rearrange("(h e) s d -> (e s) h d", h=T))]
        W_IN = 16 * len(w_loads)

        def take_rrms(pool, k):
            pool.wait_ge(rms.moments_done, k + 1)
            nc.gpsimd.tensor_tensor(mean_sq[:, :], rms.moments[:, :, 0], rms.moments[:, :, 0],
                                    ALU.mult).then_inc(mean_sq_ok, 1)
            pool.wait_ge(mean_sq_ok, 3 * k + 1)
            nc.gpsimd.tensor_tensor(mean_sq_sum[:, :], mean_sq[:, :], rms.moments[:, :, 1],
                                    ALU.add).then_inc(mean_sq_ok, 1)
            pool.wait_ge(mean_sq_ok, 3 * k + 2)
            pool.sem_inc(core.tick, 1)
            nc.gpsimd.tensor_scalar(mean_sq[:, :], mean_sq_sum[:, :], NORM_FLOOR, None,
                                    ALU.max).then_inc(mean_sq_ok, 1)
            pool.wait_ge(mean_sq_ok, 3 * k + 3)
            nc.gpsimd.tensor_tensor(rrms[:, :], mean_sq[:, :], core.minus_half[:, :],
                                    ALU.pow).then_inc(rrms_ok, 1)

        with nc.Block() as block:
            @block.sync
            def _(sp):
                for dst, src in w_loads:
                    sp.dma_start(dst, src).then_inc(weights_in, 16)

            @block.vector
            def _(dve):
                nc.vector.memset(ones[:, :], 1.0)
                nc.vector.memset(token[:, :, :, D:D + 1], 1.0)
                nc.vector.memset(slot_out[:, :, D:D + 1], 1.0)
                dve.wait_ge(weights_in, W_IN)
                take_moments(core, dve, rms, lambda t: slot_raw[:, t, :], 0)
                dve.wait_ge(rrms_ok, 1)
                for t in range(T):
                    last = nc.vector.scalar_tensor_tensor(slot_n[:, t, :], slot_raw[:, t, :], rrms[:, t:t + 1],
                                                          gamma_slot_row[:, :], ALU.mult, ALU.mult)
                last.then_inc(made, 1)
                dve.wait_ge(made, 2)
                nc.vector.tensor_copy(slotT[:, :], ps[:, 0, :]).then_inc(made, 1)
                dve.wait_ge(made, 3)
                nc.vector.tensor_copy(slotT_bf[:, :], slotT[:, :])

            @block.gpsimd
            def _(pool):
                take_rrms(pool, 0)

            @block.tensor
            def _(pe):
                pe.wait_ge(made, 1)
                for t in range(T):
                    last = nc.tensor.transpose(ps[:, 0, t * P:t * P + P], slot_n[:, t, :], core.ident[:, :])
                last.then_inc(made, 1)

        with nc.Block() as block:
            @block.vector
            def _(dve):
                def top_unit(f, i):
                    dve.wait_ge(top_mm, 8 * f + i + 1)
                    nc.vector.reduce_max(top[:, i:i + 1], ps[:, BK_TOP + i % 2, :], AXX).then_inc(top_ok, 1)

                def step(s, u):
                    g, f = s + 2, s + 1
                    if live(f):
                        dve.wait_ge(tokenT_ok, f + 1)
                        nc.vector.tensor_copy(tokenT_bf[:, :], tokenT[:, 1 - u, :]).then_inc(tokenT_bf_ok, 1)
                    if live(g):
                        take_moments(core, dve, ln_x, lambda t: x[:, g, t, :], g)
                    if live(f):
                        top_unit(f, 0)
                        top_unit(f, 1)
                    if live(g):
                        dve.wait_ge(ln_x.rstd_done, g + 1)
                        normalize(nc, ln_x, lambda t: a[:, t, :], lambda t: x[:, g, t, :]).then_inc(a_ok, 1)
                    if live(f):
                        top_unit(f, 2)
                        top_unit(f, 3)
                    if live(s):
                        dve.wait_ge(slot_mm, s + 1)
                        for j in range(2):
                            last = nc.vector.reciprocal(slot_rsum[:, 2 * j:2 * j + 2], wide_sums(j))
                        last.then_inc(slot_rsum_ok, 1)
                        dve.wait_ge(slot_rsum_ok, s + 1)
                        for t in range(T):
                            last = nc.vector.tensor_scalar(slot_in[:, t, :], wide(t)[:, 0:D], slot_rsum[:, t:t + 1],
                                                           None, ALU.mult)
                        last.then_inc(slot_ok, 1)
                    if live(f):
                        top_unit(f, 4)
                        top_unit(f, 5)
                    if live(g):
                        dve.wait_ge(a_ok, g + 1)
                        take_moments(core, dve, rms, lambda t: a[:, t, :], g + 1)
                    if live(f):
                        top_unit(f, 6)
                        top_unit(f, 7)
                        dve.wait_ge(top_ok, 8 * f + 8)
                        upto(dve, row_mm, f)
                        nc.vector.tensor_scalar(top_parts[:, :, 0], top[:, :], -1.0, None,
                                                ALU.mult).then_inc(hi_ok, 1)
                        dve.wait_ge(hi_ok, f + 1)
                        nc.vector.scalar_tensor_tensor(top_parts[:, :, 1], top[:, :], -1.0, top_parts[:, :, 0],
                                                       ALU.mult, ALU.subtract).then_inc(parts_ok, 1)
                    if live(g):
                        dve.wait_ge(rrms_ok, g + 2)
                        upto(dve, token_ok, g)
                        upto(dve, tokenT_mm, g)
                        for t in range(T):
                            last = nc.vector.tensor_scalar(unit[:, t, :], a[:, t, :], rrms[:, t:t + 1], None, ALU.mult)
                        last.then_inc(unit_ok, 1)
                    if live(s):
                        dve.wait_ge(slot_out_mm, s + 1)
                        upto(dve, out_mm, s)
                        nc.vector.tensor_copy(slot_out[:, :, 0:D], ps[:, BK_T, :].rearrange(
                            "p (t d) -> p t d", t=T)).then_inc(slot_out_ok, 1)
                        dve.wait_ge(out_mm, s + 1)
                        for j in range(2):
                            last = nc.vector.reciprocal(y_rsum[:, 2 * j:2 * j + 2], wide_sums(j))
                        last.then_inc(y_rsum_ok, 1)
                        dve.wait_ge(y_rsum_ok, s + 1)
                        for t in range(T):
                            last = nc.vector.tensor_scalar(y[:, t, :], wide(t)[:, 0:D], y_rsum[:, t:t + 1],
                                                           None, ALU.mult)
                        last.then_inc(y_ok, 1)
                        dve.wait_ge(y_ok, s + 1)
                        take_moments(core, dve, ln_y, lambda t: y[:, t, :], s)
                        dve.wait_ge(ln_y.rstd_done, s + 1)
                        upto(dve, x_ok, s)
                        normalize(nc, ln_y, lambda t: z[:, t, :], lambda t: y[:, t, :]).then_inc(z_ok, 1)

                run_steps(dve, step, -2, 1, 13, B)

            @block.gpsimd
            def _(pool):
                def step(s, u):
                    g, f = s + 2, s + 1
                    if live(f):
                        pool.wait_ge(unit_ok, f + 1)
                        upto(pool, slot_mm, f - 1)
                        nc.gpsimd.tensor_tensor(token[:, 1 - u, :, 0:D], unit[:, :, :],
                                                gamma_row[:, :].unsqueeze(1).broadcast_to([P, T, D]),
                                                ALU.mult).then_inc(token_ok, 1)
                    if live(g):
                        take_rstd(core, pool, ln_x, g)
                        take_rrms(pool, g + 1)
                    if live(s):
                        take_rstd(core, pool, ln_y, s)
                        pool.wait_ge(z_ok, s + 1)
                        pool.sem_inc(core.tick, 1)
                        nc.gpsimd.tensor_tensor(x[:, s, :, :], x[:, s, :, :], z[:, :, :], ALU.add).then_inc(x_ok, 1)

                run_steps(pool, step, -2, 1, 13, B)

            @block.sync
            def _(sp):
                with sp.Fori(0, B) as b:
                    sp.wait_ge(x_ok, b + 1)
                    sp.dma_start(dram["out"][b].rearrange("(t p) d -> p t d", p=P),
                                 x[:, b, :, :]).then_inc(stored, 16)
                sp.wait_ge(stored, 16 * B)

            @block.scalar
            def _(act):
                def step(s, u):
                    f = s + 1
                    if live(f):
                        act.wait_ge(tokenT_mm, f + 1)
                        upto(act, logit_mm, 8 * (f - 1))
                        nc.scalar.activation(tokenT[:, 1 - u, :], ps[:, BK_T, :], ACT.Copy,
                                             scale=gamma[:, 0:1]).then_inc(tokenT_ok, 1)
                    if live(s):
                        for i in range(2 * T):
                            act.wait_ge(logit_mm, 8 * s + i + 1)
                            if i % T == 0:
                                upto(act, slot_mm if i == 0 else out_mm, s)
                            nc.scalar.activation(weight[:, i, :], ps[:, BK_LOGIT + i % 2, :],
                                                 ACT.Exp).then_inc(weight_ok, 1)
                        act.wait_ge(slotT_mm, s + 1)
                        upto(act, hidden_mm, 4 * s)
                        nc.scalar.copy(slot_inT[:, :], ps[:, BK_T, :]).then_inc(slotT_ok, 1)
                        upto(act, slot_out_mm, s)
                        for j in range(FF // P):
                            act.wait_ge(hidden_mm, 4 * s + j + 1)
                            nc.scalar.activation(hiddenT[:, j, :], ps[:, BK_LOGIT + j % 2, :],
                                                 ACT.Gelu).then_inc(hidden_ok, 1)
                    if live(f):
                        act.wait_ge(row_mm, f + 1)
                        upto(act, logit_mm, 8 * (f - 1))
                        nc.scalar.copy(top_row[:, 1 - u, :, :], row_ps[0:2, :].rearrange(
                            "r (i p) -> r i p", i=2 * T)).then_inc(row_ok, 1)

                run_steps(act, step, -2, 1, 13, B)

            @block.tensor
            def _(pe):
                def top_unit(f, i):
                    upto(pe, top_ok, 8 * f + i - 1)
                    lhs, rhs = (tokenT_bf, slotT_bf) if i < T else (slotT_bf, tokenT_bf)
                    c = i % T * P
                    nc.tensor.matmul(ps[:, BK_TOP + i % 2, :], lhs[:, c:c + P], rhs[:, :], start=True,
                                     stop=True).then_inc(top_mm, 1)

                def logits(s, u, half):
                    for i in range(half * T, half * T + T):
                        if i >= 2:
                            pe.wait_ge(weight_ok, 8 * s + i - 1)
                        c = i % T * P
                        bank = ps[:, BK_LOGIT + i % 2, :]
                        rows = top_row[:, u, T - half * T:2 * T - half * T, :]
                        nc.tensor.matmul(bank, ones[:, :], rows, start=True, stop=False)
                        lhs, rhs = (tokenT[:, u, :], slotT) if half == 0 else (slotT, tokenT[:, u, :])
                        nc.tensor.matmul(bank, lhs[:, c:c + P], rhs[:, :], start=False,
                                         stop=True).then_inc(logit_mm, 1)

                def step(s, u):
                    f = s + 1
                    if live(f):
                        pe.wait_ge(unit_ok, f + 1)
                        upto(pe, slot_out_ok, f - 1)
                        for t in range(T):
                            last = nc.tensor.transpose(ps[:, BK_T, t * P:t * P + P], unit[:, t, :], core.ident[:, :])
                        last.then_inc(tokenT_mm, 1)
                    if live(s):
                        pe.wait_ge(row_ok, s + 1)
                        upto(pe, hidden_ok, 4 * s)
                        logits(s, u, 0)
                    if live(f):
                        pe.wait_ge(tokenT_bf_ok, f + 1)
                        top_unit(f, 0)
                        top_unit(f, 1)
                    if live(s):
                        logits(s, u, 1)
                    if live(f):
                        top_unit(f, 2)
                        top_unit(f, 3)
                    if live(s):
                        pe.wait_ge(weight_ok, 8 * s + 4)
                        pe.wait_ge(token_ok, s + 1)
                        upto(pe, y_ok, s)
                        for e in range(T):
                            for t in range(T):
                                last = nc.tensor.matmul(wide(e), weight[:, t, e * P:e * P + P], token[:, u, t, :],
                                                        start=t == 0, stop=t == T - 1)
                        last.then_inc(slot_mm, 1)
                    if live(f):
                        top_unit(f, 4)
                        top_unit(f, 5)
                    if live(s):
                        pe.wait_ge(slot_ok, s + 1)
                        for e in range(T):
                            last = nc.tensor.transpose(ps[:, BK_T, e * P:e * P + P], slot_in[:, e, :],
                                                       core.ident[:, :])
                        last.then_inc(slotT_mm, 1)
                    if live(f):
                        top_unit(f, 6)
                        top_unit(f, 7)
                    if live(s):
                        pe.wait_ge(slotT_ok, s + 1)
                        for j in range(FF // P):
                            pe.wait_ge(weight_ok, 8 * s + 8)
                            if j >= 2:
                                pe.wait_ge(hidden_ok, 4 * s + j - 1)
                            nc.tensor.matmul(ps[:, BK_LOGIT + j % 2, :], w1[:, j * P:j * P + P], slot_inT[:, :],
                                             start=True, stop=True).then_inc(hidden_mm, 1)
                    if live(f):
                        pe.wait_ge(parts_ok, f + 1)
                        upto(pe, row_ok, f)
                        for i in range(2 * T):
                            last = nc.tensor.transpose(row_ps[0:2, i * P:i * P + P], top_parts[:, i, :],
                                                       core.ident_bf[:, :])
                        last.then_inc(row_mm, 1)
                    if live(s):
                        pe.wait_ge(hidden_ok, 4 * s + 4)
                        for e in range(T):
                            for j in range(FF // P):
                                last = nc.tensor.matmul(ps[:, BK_T, e * D:e * D + D], hiddenT[:, j, e * P:e * P + P],
                                                        w2[:, j, :], start=j == 0, stop=j == FF // P - 1)
                        last.then_inc(slot_out_mm, 1)
                        pe.wait_ge(slot_out_ok, s + 1)
                        for t in range(T):
                            for e in range(T):
                                last = nc.tensor.matmul(wide(t), weight[:, T + e, t * P:t * P + P],
                                                        slot_out[:, e, :], start=e == 0, stop=e == T - 1)
                        last.then_inc(out_mm, 1)

                run_steps(pe, step, -2, 1, 13, B)


def build(nc, dram):
    with ExitStack() as ctx:
        core = Core(nc, ctx, dram)
        core.tick = core.sem("tick")
        set_up(core)
        gated_attention(core)
        channel_mix(core)
        causal_attention(core)
        soft_mixture(core)


def kernel(**inputs):
    import concourse.bacc as bacc
    from concourse.bass_utils import run_bass_kernel_spmd

    got = {name: np.asarray(a) for name, a in inputs.items()}
    arrays = {}
    for name, a in got.items():
        short = name.split("_", 2)[2]
        arrays[short] = a
    for name in ("W_r", "W_k", "W_v", "Wv", "Wo"):
        arrays[f"{name}_T"] = arrays.pop(name).T
    for name in ("Wq", "Wk"):
        w = arrays.pop(name)
        arrays[f"{name}_T"] = w[qk_rows()].T
        arrays[f"{name}_turned_T"] = w[qk_rows(turned=True)].T
    arrays["gau_vectors"] = np.stack([arrays["ln_g"], arrays["ln_b"], arrays["b_qk"],
                                      *arrays["b_hidden"][HID:].reshape(2, D), *arrays["os_gamma"],
                                      *arrays["os_beta"]], axis=1)
    arrays["mix_vectors"] = np.stack([arrays.pop("mu_r"), arrays.pop("mu_k")], axis=1)
    for name in ("ln_g", "ln_b", "b_qk", "os_gamma", "os_beta"):
        arrays.pop(name)
    arrays.update(constants())
    arrays = {name: np.ascontiguousarray(a) for name, a in arrays.items()}

    nc = bacc.Bacc("TRN2", target_bir_lowering=False, num_devices=1)
    dram = {name: nc.dram_tensor(f"in_{name}", a.shape, mybir.dt.from_np(a.dtype), kind="ExternalInput").ap()
            for name, a in arrays.items()}
    dram["out"] = nc.dram_tensor("out", (B, N, D), F32, kind="ExternalOutput").ap()
    build(nc, dram)
    result = run_bass_kernel_spmd(nc, [{f"in_{name}": a for name, a in arrays.items()}], core_ids=[0])
    return result.results[0]["out"]
```

```python
from contextlib import ExitStack

import numpy as np

import concourse.bass as bass
from concourse import mybir
from concourse.alu_op_type import AluOpType as ALU

F32 = mybir.dt.float32
BF16 = mybir.dt.bfloat16
ACT = mybir.ActivationFunctionType
AXX = mybir.AxisListType.X

P = 128
B = 16
N = 512
T = N // P
D = 128
HID = 256
NH, DH = 16, 8
HH = NH // 2
E_T = 512
FF = 512
EPS = 1e-5
NORM_FLOOR = 1e-24 / D
MASKED = -1e30
PARTS_Q = (0, 0, 1, 1, 0, 2)
PARTS_K = (0, 1, 0, 1, 2, 0)
KS = DH * len(PARTS_Q)
KM = KS + 2


def live(b):
    return not isinstance(b, int) or 0 <= b < B


def upto(engine, sem, value):
    if not isinstance(value, int) or value > 0:
        engine.wait_ge(sem, value)


def run_steps(engine, step, first, loop_from, loop_to, last):
    for s in range(first, loop_from):
        step(s, s % 2)
    with engine.Fori(0, (loop_to - loop_from) // 2) as pair:
        for k in range(2):
            step(2 * pair + (loop_from + k), (loop_from + k) % 2)
    for s in range(loop_to, last):
        step(s, s % 2)


def qk_rows(turned=False):
    half, d, h = np.meshgrid(np.arange(2), np.arange(DH), np.arange(HH), indexing="ij")
    d = (d + DH // 2) % DH if turned else d
    return ((half * HH + h) * DH + d).reshape(-1)


def constants():
    p, col = np.arange(P), np.arange(N)
    inv_freq = (1.0 / np.float32(10000.0) ** (np.arange(0, DH, 2, dtype=np.float32) / DH)).astype(np.float32)
    d = p // HH % DH
    angle = col.astype(np.float32)[None, :] * inv_freq[d % (DH // 2)][:, None]
    tables = {
        "ident": np.eye(P),
        "keep": np.where((col[None, :] >= p[:, None]) | (col[None, :] >= P), 1.0, 0.0),
        "inv_pos": np.broadcast_to(1.0 / (col[None, :] + 1.0), (P, N)),
        "cos": np.cos(angle),
        "sin": np.sin(angle) * np.where(d < DH // 2, -1.0, 1.0)[:, None],
        "future": np.tile(np.where(p[None, :] > p[:, None], MASKED, 0.0), (1, 2)),
    }
    return {name: np.ascontiguousarray(a, dtype=np.float32) for name, a in tables.items()}


ATT_WEIGHTS = ("Wq_T", "Wq_turned_T", "Wk_T", "Wk_turned_T", "Wv_T", "Wo_T")


class Core:

    def __init__(self, nc, ctx, dram):
        self.nc, self.ctx, self.dram = nc, ctx, dram
        self.x = self.sb("x", [P, B, T, D])
        self.ps = ctx.enter_context(nc.psum_tensor("ps", [P, 8, N], F32))
        self.ident = self.sb("ident", [P, P])
        self.ident_bf = self.sb("ident_bf", [P, P], BF16)
        self.eps = self.sb("eps", [P, T])
        self.minus_half = self.sb("minus_half", [P, T])
        self.minus_one = self.sb("minus_one", [P, T])
        self.weights = {}
        self.loads = []
        self.weights_in = self.sem("weights_in")
        for name in ("W_r_T", "W_k_T", "W_v_T", *ATT_WEIGHTS):
            self.to_load(name, [P, D], dram[name])
        self.to_load("mix_vectors", [P, 2], dram["mix_vectors"])
        for name in ("cos", "sin"):
            self.to_load(name, [P, N], dram[name])
        self.to_load("future", [P, 2 * P], dram["future"])
        self.to_load("w1", [P, FF], dram["w1"])
        self.to_load("w2", [P, FF // P, D], dram["w2"].rearrange("(j p) d -> p j d", p=P))
        for name in ("gamma_x", "gamma_slot"):
            self.to_load(name, [P, D], dram[name].partition_broadcast(P))
        self.to_load("gamma_x_column", [P, 1], dram["gamma_x"].rearrange("(p o) -> p o", o=1))
        self.to_load("slot_embeds", [P, T, D], dram["slot_embeds"].rearrange("(h e) s d -> (e s) h d", h=T))

    def to_load(self, name, shape, source):
        self.weights[name] = self.sb(name, shape)
        self.loads.append((self.weights[name][tuple(slice(None) for _ in shape)], source))

    def load_weights(self, sp):
        for dst, src in self.loads:
            sp.dma_start(dst, src).then_inc(self.weights_in, 16)

    def wait_weights(self, engine):
        engine.wait_ge(self.weights_in, 16 * len(self.loads))

    def sb(self, name, shape, dtype=F32):
        return self.ctx.enter_context(self.nc.sbuf_tensor(name, shape, dtype))

    def sem(self, name):
        return self.ctx.enter_context(self.nc.semaphore(name))


class Layer:

    def __init__(self, core, prefix, ctx):
        self.nc, self.prefix, self.ctx, self.sems = core.nc, prefix, ctx, []

    def sb(self, name, shape, dtype=F32):
        return self.ctx.enter_context(self.nc.sbuf_tensor(f"{self.prefix}_{name}", shape, dtype))

    def sem(self, name):
        handle = self.nc.alloc_semaphore(name=f"{self.prefix}_{name}")
        self.sems.append(handle)
        return handle

    def free_semaphores(self):
        self.nc.clear_and_free_semaphores(self.sems)
        self.nc.all_engine_barrier()


class Stats:

    def __init__(self, layer, name, with_shift=False):
        self.stats = layer.sb(f"{name}_stats", [P, T, 6])
        self.moments = layer.sb(f"{name}_moments", [P, T, 2])
        self.shifted = layer.sb(f"{name}_shifted", [P, T])
        self.rstd = layer.sb(f"{name}_rstd", [P, T])
        if with_shift:
            self.minus_mean = layer.sb(f"{name}_minus_mean", [P, T])
            self.shift = layer.sb(f"{name}_shift", [P, T])
        self.stats_done = layer.sem(f"{name}_stats_done")
        self.moments_done = layer.sem(f"{name}_moments_done")
        self.shifted_done = layer.sem(f"{name}_shifted_done")
        self.rstd_done = layer.sem(f"{name}_rstd_done")
        self.with_shift = with_shift
        if with_shift:
            self.shift_done = layer.sem(f"{name}_shift_done")


def take_moments(core, dve, st, src, b):
    nc = core.nc
    for t in range(T):
        nc.vector.bn_stats(st.stats[:, t, :], src(t)).then_inc(st.stats_done, 1)
    dve.wait_ge(st.stats_done, T * b + T)
    dve.sem_inc(core.tick, 1)
    for t in range(T):
        last = nc.vector.bn_aggr(st.moments[:, t, :], st.stats[:, t, :])
    last.then_inc(st.moments_done, 1)


def take_rstd(core, pool, st, b):
    nc = core.nc
    pool.wait_ge(st.moments_done, b + 1)
    nc.gpsimd.tensor_tensor(st.shifted[:, :], st.moments[:, :, 1], core.eps[:, :],
                            ALU.add).then_inc(st.shifted_done, 1)
    pool.wait_ge(st.shifted_done, 2 * b + 1 if st.with_shift else b + 1)
    nc.gpsimd.tensor_tensor(st.rstd[:, :], st.shifted[:, :], core.minus_half[:, :],
                            ALU.pow).then_inc(st.rstd_done, 1)


def take_shift(core, pool, st, b):
    nc = core.nc
    nc.gpsimd.tensor_tensor(st.minus_mean[:, :], st.moments[:, :, 0], core.minus_one[:, :],
                            ALU.mult).then_inc(st.shifted_done, 1)
    pool.wait_ge(st.shifted_done, 2 * b + 2)
    pool.wait_ge(st.rstd_done, b + 1)
    nc.gpsimd.tensor_tensor(st.shift[:, :], st.minus_mean[:, :], st.rstd[:, :],
                            ALU.mult).then_inc(st.shift_done, 1)


def normalize_act(nc, st, dst, src):
    for t in range(T):
        last = nc.scalar.activation(dst(t), src(t), ACT.Identity, bias=st.shift[:, t:t + 1],
                                    scale=st.rstd[:, t:t + 1])
    return last


def normalize(nc, st, dst, src):
    for t in range(T):
        last = nc.vector.tensor_scalar(dst(t), src(t), st.moments[:, t, 0:1], st.rstd[:, t:t + 1],
                                       ALU.subtract, ALU.mult)
    return last


def gated_attention(core):
    nc, dram, x, ps = core.nc, core.dram, core.x, core.ps
    with ExitStack() as ctx:
        L = Layer(core, "gau", ctx)
        w_hidden = L.sb("w_hidden", [P, 2 * HID])
        w_qk = L.sb("w_qk", [P, D])
        w_out = L.sb("w_out", [P, HID // P, D])
        keep, inv_pos = L.sb("keep", [P, N]), L.sb("inv_pos", [P, N])
        b_value = L.sb("b_value", [P, HID])
        b_out = L.sb("b_out", [P, D])
        per_feature = L.sb("per_feature", [P, 9])
        ln_g, ln_b, b_qk = (per_feature[:, i:i + 1] for i in range(3))
        b_gate, os_gamma, os_beta = (per_feature[:, i:i + 2] for i in (3, 5, 7))
        a = L.sb("a", [P, 2, T, D])
        a_bias = L.sb("a_bias", [P, 2, T, D])
        n2 = L.sb("n2", [P, T, D])
        nT = L.sb("nT", [P, N])
        value_pre = L.sb("value_pre", [P, T, HID])
        value = L.sb("value", [P, 2, T, HID])
        gateT = L.sb("gateT", [P, 2, 2, N])
        qk_act, q_aff = L.sb("qk_act", [P, N]), L.sb("q_aff", [P, N])
        qT, kT = L.sb("qT", [P, N]), L.sb("kT", [P, N])
        relu = L.sb("relu", [P, 3, N])
        prob = L.sb("prob", [P, 3, N])
        gatedT = L.sb("gatedT", [P, 2, N])
        y, z = L.sb("y", [P, T, D]), L.sb("z", [P, T, D])
        ln_x, ln_a, ln_y = Stats(L, "ln_x"), Stats(L, "ln_a"), Stats(L, "ln_y")

        weights_in = L.sem("weights_in")
        x_in = [L.sem("x_in_even"), L.sem("x_in_odd")]
        a_ok, n2_ok, a_bias_ok = L.sem("a_ok"), L.sem("n2_ok"), L.sem("a_bias_ok")
        nT_mm, nT_ok = L.sem("nT_mm"), L.sem("nT_ok")
        value_mm, value_pre_ok, value_ok = L.sem("value_mm"), L.sem("value_pre_ok"), L.sem("value_ok")
        gate_mm, gate_ok = L.sem("gate_mm"), L.sem("gate_ok")
        qk_mm, qk_act_ok, q_aff_ok, q_ok, k_ok = (L.sem("qk_mm"), L.sem("qk_act_ok"), L.sem("q_aff_ok"), L.sem("q_ok"),
                                                  L.sem("k_ok"))
        score_mm, relu_ok, prob_ok = L.sem("score_mm"), L.sem("relu_ok"), L.sem("prob_ok")
        attn_mm, gated_ok = L.sem("attn_mm"), L.sem("gated_ok")
        out_mm, y_ok, z_ok, x_ok = L.sem("out_mm"), L.sem("y_ok"), L.sem("z_ok"), L.sem("x_ok")

        BK_NT, BK_VALUE, BK_GATE, BK_SCORE = 0, 1, 3, 5
        BK_QK, BK_ATTN, BK_OUT = 0, 5, 7
        SCORES = ((0, 0, 0), (1, 1, 0), (3, 1, 3 * P), (2, 2, 0))

        def width(kt):
            return N - kt * P

        w_loads = [
            (core.ident[:, :], dram["ident"]),
            (w_hidden[:, :], dram["W_hidden"]), (w_qk[:, :], dram["W_qk"]),
            (w_out[:, :, :], dram["W_out"].rearrange("(j p) d -> p j d", p=P)),
            (keep[:, :], dram["keep"]), (inv_pos[:, :], dram["inv_pos"]),
            (b_value[:, :], dram["b_hidden"][0:HID].partition_broadcast(P)),
            (b_out[:, :], dram["b_out"].partition_broadcast(P)),
            (per_feature[:, :], dram["gau_vectors"]),
        ]
        W_IN = 16 * len(w_loads)

        with nc.Block() as block:
            @block.sync
            def _(sp):
                def load_x(b, u):
                    sp.dma_start(x[:, b, :, :], dram["x"][b].rearrange("(t p) d -> p t d", p=P)).then_inc(x_in[u], 16)

                load_x(0, 0)
                load_x(1, 1)
                for dst, src in w_loads:
                    sp.dma_start(dst, src).then_inc(weights_in, 16)
                core.load_weights(sp)
                with sp.Fori(1, B // 2) as pair:
                    for u in range(2):
                        sp.wait_ge(x_in[u], 16 * pair)
                        load_x(2 * pair + u, u)

            @block.vector
            def _(dve):
                nc.vector.memset(core.eps[:, :], EPS)
                nc.vector.memset(core.minus_half[:, :], -0.5)
                nc.vector.memset(core.minus_one[:, :], -1.0)

                def step(s, u):
                    h, g, f, p, gu, fu = s + 3, s + 2, s + 1, s - 1, u, 1 - u
                    if live(s):
                        for i, (kt, bank, at) in enumerate(SCORES):
                            dve.wait_ge(score_mm, 3 * s + bank + 1)
                            if i == 0:
                                upto(dve, prob_ok, 3 * s)
                            w = width(kt)
                            r = nc.vector.scalar_tensor_tensor(
                                relu[:, bank, at:at + w], ps[:, BK_SCORE + bank, at:at + w], 0.0, keep[:, 0:w],
                                ALU.max, ALU.mult)
                            if kt != 1:
                                r.then_inc(relu_ok, 1)
                    if live(g):
                        dve.wait_ge(ln_x.rstd_done, g + 1)
                        upto(dve, a_bias_ok, g - 1)
                        normalize(nc, ln_x, lambda t: a[:, gu, t, :], lambda t: x[:, g, t, :]).then_inc(a_ok, 1)
                    if live(p):
                        dve.wait_ge(ln_y.rstd_done, p + 1)
                        upto(dve, x_ok, p)
                        normalize(nc, ln_y, lambda t: z[:, t, :], lambda t: y[:, t, :]).then_inc(z_ok, 1)
                    if live(f):
                        dve.wait_ge(value_mm, f + 1)
                        upto(dve, value_ok, f)
                        for j in range(2):
                            last = nc.vector.tensor_tensor(
                                value_pre[:, 2 * j:2 * j + 2, :],
                                ps[:, BK_VALUE + j, :].rearrange("p (t h) -> p t h", t=2),
                                b_value[:, :].unsqueeze(1).broadcast_to([P, 2, HID]), ALU.add)
                        last.then_inc(value_pre_ok, 1)
                    if live(g):
                        dve.wait_ge(a_ok, g + 1)
                        take_moments(core, dve, ln_a, lambda t: a[:, gu, t, :], g)
                    if live(s):
                        dve.wait_ge(gate_ok, s + 1)
                        upto(dve, out_mm, s)
                        for j in range(2):
                            dve.wait_ge(attn_mm, 2 * s + j + 1)
                            nc.vector.tensor_tensor(gatedT[:, j, :], ps[:, BK_ATTN + j, :], gateT[:, u, j, :],
                                                    ALU.mult).then_inc(gated_ok, 1)
                    if live(g):
                        dve.wait_ge(ln_a.rstd_done, g + 1)
                        upto(dve, nT_mm, g)
                        normalize(nc, ln_a, lambda t: n2[:, t, :], lambda t: a[:, gu, t, :]).then_inc(n2_ok, 1)
                    if live(s):
                        dve.wait_ge(out_mm, s + 1)
                        dve.wait_ge(a_bias_ok, s + 1)
                        upto(dve, z_ok, s)
                        nc.vector.tensor_tensor(y[:, :, :], ps[:, BK_OUT, :].rearrange("p (t d) -> p t d", t=T),
                                                a_bias[:, u, :, :], ALU.add).then_inc(y_ok, 1)
                        dve.wait_ge(y_ok, s + 1)
                        take_moments(core, dve, ln_y, lambda t: y[:, t, :], s)

                    if live(h):
                        dve.wait_ge(x_in[1 - u], 16 + 8 * (h - (1 - u)))
                        take_moments(core, dve, ln_x, lambda t: x[:, h, t, :], h)

                step(-3, 1)
                step(-2, 0)
                dve.wait_ge(weights_in, W_IN)
                nc.vector.tensor_copy(core.ident_bf[:, :], core.ident[:, :])
                run_steps(dve, step, -1, 3, 11, B + 1)

            @block.gpsimd
            def _(pool):
                def step(s, u):
                    h, g, f, p, fu = s + 3, s + 2, s + 1, s - 1, 1 - u
                    if live(f):
                        pool.wait_ge(a_ok, f + 1)
                        upto(pool, y_ok, f - 1)
                        nc.gpsimd.tensor_tensor(
                            a_bias[:, fu, :, :], a[:, fu, :, :], b_out[:, :].unsqueeze(1).broadcast_to([P, T, D]),
                            ALU.add).then_inc(a_bias_ok, 1)
                    if live(g):
                        take_rstd(core, pool, ln_a, g)
                    if live(f):
                        pool.wait_ge(q_aff_ok, f + 1)
                        upto(pool, score_mm, 3 * f)
                        nc.gpsimd.tensor_tensor(qT[:, :], q_aff[:, :], inv_pos[:, :], ALU.mult).then_inc(q_ok, 1)
                    if live(p):
                        pool.wait_ge(z_ok, p + 1)
                        pool.sem_inc(core.tick, 1)
                        nc.gpsimd.tensor_tensor(x[:, p, :, :], x[:, p, :, :], z[:, :, :], ALU.add).then_inc(x_ok, 1)
                    if live(s):
                        take_rstd(core, pool, ln_y, s)
                    if live(h):
                        take_rstd(core, pool, ln_x, h)

                step(-3, 1)
                step(-2, 0)
                pool.wait_ge(weights_in, W_IN)
                run_steps(pool, step, -1, 3, 11, B + 1)

            @block.scalar
            def _(act):
                act.wait_ge(weights_in, W_IN)

                def step(s, u):
                    f, fu = s + 1, 1 - u
                    if live(f):
                        act.wait_ge(nT_mm, f + 1)
                        nc.scalar.activation(nT[:, :], ps[:, BK_NT, :], ACT.Identity, bias=ln_b,
                                             scale=ln_g).then_inc(nT_ok, 1)
                    if live(s):
                        upto(act, attn_mm, 2 * s)
                        for bank, w in ((0, N), (1, N), (2, width(2))):
                            act.wait_ge(relu_ok, 3 * s + bank + 1)
                            nc.scalar.activation(prob[:, bank, 0:w], relu[:, bank, 0:w],
                                                 ACT.Square).then_inc(prob_ok, 1)
                    if live(f):
                        act.wait_ge(qk_mm, f + 1)
                        upto(act, q_aff_ok, f)
                        upto(act, k_ok, f)
                        nc.scalar.activation(qk_act[:, :], ps[:, BK_QK, :], ACT.Silu,
                                             bias=b_qk).then_inc(qk_act_ok, 1)
                        act.wait_ge(qk_act_ok, f + 1)
                        upto(act, q_ok, f)
                        nc.scalar.activation(q_aff[:, :], qk_act[:, :], ACT.Identity, bias=os_beta[:, 0:1],
                                             scale=os_gamma[:, 0:1]).then_inc(q_aff_ok, 1)
                        upto(act, score_mm, 3 * f)
                        nc.scalar.activation(kT[:, :], qk_act[:, :], ACT.Identity, bias=os_beta[:, 1:2],
                                             scale=os_gamma[:, 1:2]).then_inc(k_ok, 1)
                    if live(f):
                        act.wait_ge(value_pre_ok, f + 1)
                        upto(act, attn_mm, 2 * (f - 1))
                        nc.scalar.activation(value[:, fu, :, :], value_pre[:, :, :], ACT.Silu).then_inc(value_ok, 1)
                        upto(act, gated_ok, 2 * (f - 1))
                        act.wait_ge(gate_mm, f + 1)
                        for j in range(2):
                            last = nc.scalar.activation(gateT[:, fu, j, :], ps[:, BK_GATE + j, :], ACT.Silu,
                                                        bias=b_gate[:, j:j + 1])
                        last.then_inc(gate_ok, 1)

                run_steps(act, step, -2, 1, 13, B)

            @block.tensor
            def _(pe):
                pe.wait_ge(weights_in, W_IN)

                def step(s, u):
                    f, fu = s + 1, 1 - u
                    if live(f):
                        pe.wait_ge(n2_ok, f + 1)
                        upto(pe, qk_act_ok, f)
                        for t in range(T):
                            last = nc.tensor.transpose(ps[:, BK_NT, t * P:t * P + P], n2[:, t, :], core.ident[:, :])
                        last.then_inc(nT_mm, 1)
                    if live(s):
                        pe.wait_ge(q_ok, s + 1)
                        pe.wait_ge(k_ok, s + 1)
                        upto(pe, gated_ok, 2 * s)
                        for kt, bank, at in SCORES:
                            if kt == 2:
                                upto(pe, y_ok, s)
                            last = nc.tensor.matmul(ps[:, BK_SCORE + bank, at:at + width(kt)],
                                                    kT[:, kt * P:kt * P + P], qT[:, kt * P:N], start=True, stop=True)
                            if kt != 1:
                                last.then_inc(score_mm, 1)
                    if live(f):
                        pe.wait_ge(nT_ok, f + 1)
                        nc.tensor.matmul(ps[:, BK_QK, :], w_qk[:, :], nT[:, :], start=True,
                                         stop=True).then_inc(qk_mm, 1)
                        upto(pe, value_pre_ok, f)
                        for t in range(T):
                            last = nc.tensor.matmul(ps[:, BK_VALUE + t // 2, t % 2 * HID:t % 2 * HID + HID],
                                                    nT[:, t * P:t * P + P], w_hidden[:, 0:HID], start=True, stop=True)
                        last.then_inc(value_mm, 1)
                        upto(pe, gate_ok, f)
                        for j in range(2):
                            last = nc.tensor.matmul(ps[:, BK_GATE + j, :], w_hidden[:, HID + j * P:HID + j * P + P],
                                                    nT[:, :], start=True, stop=True)
                        last.then_inc(gate_mm, 1)
                    if live(s):
                        pe.wait_ge(value_ok, s + 1)
                        pe.wait_ge(prob_ok, 3 * s + 3)
                        for j in range(2):
                            for i, (kt, bank, at) in enumerate(SCORES):
                                last = nc.tensor.matmul(ps[:, BK_ATTN + j, kt * P:N],
                                                        value[:, u, kt, j * P:j * P + P],
                                                        prob[:, bank, at:at + width(kt)], start=i == 0, stop=i == T - 1)
                            last.then_inc(attn_mm, 1)
                    if live(s):
                        pe.wait_ge(gated_ok, 2 * s + 2)
                        for t in range(T):
                            for j in range(2):
                                last = nc.tensor.matmul(ps[:, BK_OUT, t * D:t * D + D],
                                                        gatedT[:, j, t * P:t * P + P], w_out[:, j, :],
                                                        start=j == 0, stop=j == 1)
                        last.then_inc(out_mm, 1)

                run_steps(pe, step, -2, 1, 13, B)
        L.free_semaphores()


def channel_mix(core):
    nc, dram, x, ps = core.nc, core.dram, core.x, core.ps
    with ExitStack() as ctx:
        L = Layer(core, "mix", ctx)
        w_r, w_k, w_v, mu = (core.weights[name] for name in ("W_r_T", "W_k_T", "W_v_T", "mix_vectors"))
        w_k_now, w_k_prev = L.sb("w_k_now", [P, D]), L.sb("w_k_prev", [P, D])
        w_r_now, w_r_prev = L.sb("w_r_now", [P, D]), L.sb("w_r_prev", [P, D])
        a = L.sb("a", [P, T, D])
        aT = L.sb("aT", [P, 2, 1 + N])
        r = L.sb("r", [P, 2, T, D])
        relu_k, k_act = L.sb("relu_k", [P, N]), L.sb("k_act", [P, N])
        y, z = L.sb("y", [P, T, D]), L.sb("z", [P, T, D])
        ln_x, ln_y = Stats(L, "ln_x", with_shift=True), Stats(L, "ln_y")
        now_ok, weights_ok = L.sem("now_ok"), L.sem("weights_ok")
        a_ok, aT_mm, aT_ok = L.sem("a_ok"), L.sem("aT_mm"), L.sem("aT_ok")
        k_mm, r_mm, r_ok, relu_ok, k_act_ok = (L.sem("k_mm"), L.sem("r_mm"), L.sem("r_ok"), L.sem("relu_ok"),
                                               L.sem("k_act_ok"))
        out_mm, y_ok, z_ok, x_ok = L.sem("out_mm"), L.sem("y_ok"), L.sem("z_ok"), L.sem("x_ok")
        BK_AT, BK_K, BK_R, BK_OUT = 0, 1, 2, 3

        with nc.Block() as block:
            @block.vector
            def _(dve):
                def step(s, u):
                    m, p = s + 3, s - 1
                    if live(p):
                        dve.wait_ge(ln_y.rstd_done, p + 1)
                        upto(dve, x_ok, p)
                        normalize(nc, ln_y, lambda t: z[:, t, :], lambda t: y[:, t, :]).then_inc(z_ok, 1)
                    if live(s):
                        dve.wait_ge(out_mm, s + 1)
                        dve.wait_ge(r_ok, s + 1)
                        upto(dve, z_ok, s)
                        nc.vector.tensor_tensor(y[:, :, :], ps[:, BK_OUT, :].rearrange("p (t d) -> p t d", t=T),
                                                r[:, u, :, :], ALU.mult).then_inc(y_ok, 1)
                        dve.wait_ge(y_ok, s + 1)
                        take_moments(core, dve, ln_y, lambda t: y[:, t, :], s)
                    if live(m):
                        upto(dve, ln_x.shift_done, m)
                        take_moments(core, dve, ln_x, lambda t: x[:, m, t, :], m)

                core.wait_weights(dve)
                step(-3, 1)
                for u in range(2):
                    nc.vector.memset(aT[:, u, 0:1], 0.0)
                for w, now, i in ((w_r, w_r_now, 0), (w_k, w_k_now, 1)):
                    nc.vector.tensor_scalar(now[:, :], w[:, :], mu[:, i:i + 1], None, ALU.mult).then_inc(now_ok, 1)
                dve.wait_ge(now_ok, 2)
                nc.vector.tensor_tensor(w_r_prev[:, :], w_r[:, :], w_r_now[:, :], ALU.subtract)
                nc.vector.tensor_tensor(w_k_prev[:, :], w_k[:, :], w_k_now[:, :],
                                        ALU.subtract).then_inc(weights_ok, 1)
                run_steps(dve, step, -2, 3, 11, B + 1)

            @block.gpsimd
            def _(pool):
                def step(s, u):
                    h, p = s + 2, s - 1
                    if live(h):
                        upto(pool, a_ok, h)
                        take_rstd(core, pool, ln_x, h)
                        take_shift(core, pool, ln_x, h)
                    if live(p):
                        pool.wait_ge(z_ok, p + 1)
                        pool.sem_inc(core.tick, 1)
                        nc.gpsimd.tensor_tensor(x[:, p, :, :], x[:, p, :, :], z[:, :, :], ALU.add).then_inc(x_ok, 1)
                    if live(s):
                        take_rstd(core, pool, ln_y, s)

                run_steps(pool, step, -2, 3, 13, B + 1)

            @block.scalar
            def _(act):
                def step(s, u):
                    h, f = s + 2, s + 1
                    if live(f):
                        act.wait_ge(aT_mm, f + 1)
                        upto(act, r_mm, f - 1)
                        nc.scalar.copy(aT[:, 1 - u, 1:1 + N], ps[:, BK_AT, :]).then_inc(aT_ok, 1)
                    if live(h):
                        act.wait_ge(ln_x.shift_done, h + 1)
                        upto(act, aT_mm, h)
                        normalize_act(nc, ln_x, lambda t: a[:, t, :], lambda t: x[:, h, t, :]).then_inc(a_ok, 1)
                    if live(f):
                        act.wait_ge(k_mm, f + 1)
                        upto(act, k_act_ok, f)
                        nc.scalar.activation(relu_k[:, :], ps[:, BK_K, :], ACT.Relu).then_inc(relu_ok, 1)
                        act.wait_ge(relu_ok, f + 1)
                        upto(act, out_mm, f)
                        nc.scalar.activation(k_act[:, :], relu_k[:, :], ACT.Square).then_inc(k_act_ok, 1)
                        act.wait_ge(r_mm, f + 1)
                        upto(act, y_ok, f - 1)
                        nc.scalar.activation(r[:, 1 - u, :, :], ps[:, BK_R, :].rearrange("p (t d) -> p t d", t=T),
                                             ACT.Sigmoid).then_inc(r_ok, 1)

                run_steps(act, step, -2, 3, 13, B)

            @block.tensor
            def _(pe):
                def step(s, u):
                    h, f, fu = s + 2, s + 1, 1 - u
                    if live(s):
                        pe.wait_ge(k_act_ok, s + 1)
                        upto(pe, y_ok, s)
                        for t in range(T):
                            last = nc.tensor.matmul(ps[:, BK_OUT, t * D:t * D + D], k_act[:, t * P:t * P + P],
                                                    w_v[:, :], start=True, stop=True)
                        last.then_inc(out_mm, 1)
                    if live(f):
                        pe.wait_ge(aT_ok, f + 1)
                        upto(pe, relu_ok, f)
                        nc.tensor.matmul(ps[:, BK_K, :], w_k_now[:, :], aT[:, fu, 1:1 + N], start=True, stop=False)
                        nc.tensor.matmul(ps[:, BK_K, :], w_k_prev[:, :], aT[:, fu, 0:N], start=False,
                                         stop=True).then_inc(k_mm, 1)
                    if live(h):
                        pe.wait_ge(a_ok, h + 1)
                        upto(pe, aT_ok, h)
                        for t in range(T):
                            last = nc.tensor.transpose(ps[:, BK_AT, t * P:t * P + P], a[:, t, :], core.ident[:, :])
                        last.then_inc(aT_mm, 1)
                    if live(f):
                        upto(pe, r_ok, f)
                        for t in range(T):
                            for lhs, rhs, first in ((1, w_r_now, True), (0, w_r_prev, False)):
                                last = nc.tensor.matmul(ps[:, BK_R, t * D:t * D + D],
                                                        aT[:, fu, lhs + t * P:lhs + t * P + P], rhs[:, :],
                                                        start=first, stop=not first)
                        last.then_inc(r_mm, 1)

                step(-2, 0)
                pe.wait_ge(weights_ok, 1)
                run_steps(pe, step, -1, 3, 13, B)


SLOTS = 20
GROUPS, GH = 4, 4
SHARED = ((0, "aT", 2), (1, "top_late", 0), (2, "q", 2), (3, "natural_late", -1), (4, "q_turned", 2),
          (5, "oT", -1), (6, "k", 2), (7, "out", -1), (8, "natural_0", 0), (9, "k_turned", 2), (11, "v", 1),
          (13, "natural_1", 0), (15, "top_early", 1), (18, "natural_2", 0))
FIRST_STEP = -3


def shared_user_before(s, task):
    uses = [(s + back + ahead, name) for back in (-1, 0) for _, name, ahead in SHARED]
    at = len(SHARED) + [name for _, name, _ in SHARED].index(task)
    earlier = [(name, b) for b, name in uses[:at] if live(b)]
    return earlier[-1] if earlier else None


def top_unit_parts(n, i):
    half, j = divmod(n, SLOTS // 2)
    h = half * HH
    if j < 4:
        return [(3, h + 2 * j + i, 0)], (3 * P, 1)
    if j < 8:
        h += 2 * (j - 4) + i
        return [(2, h, 0), (0, h, 3 * P)], (2 * P, 2)
    h += 4 * (j - 8) + 2 * i
    return [(1, h, 0), (1, h + 1, 2 * P)], (P, 2)


def causal_attention(core):
    nc, dram, x, ps = core.nc, core.dram, core.x, core.ps
    with ExitStack() as ctx:
        L = Layer(core, "att", ctx)
        w_q, w_q_turned, w_k, w_k_turned, w_v, w_o = (core.weights[name] for name in ATT_WEIGHTS)
        cos, sin, future = (core.weights[name] for name in ("cos", "sin", "future"))
        future_bf = L.sb("future_bf", [P, 2, P], BF16)
        a = L.sb("a", [P, T, D])
        aT = L.sb("aT", [P, 2, N])
        by_cos, by_sin = L.sb("by_cos", [P, N]), L.sb("by_sin", [P, N])
        full, rest = L.sb("full", [P, N]), L.sb("rest", [P, N])
        q_parts, k_parts = L.sb("q_parts", [P, 3, N], BF16), L.sb("k_parts", [P, 3, N], BF16)
        q_stack, k_stack = L.sb("q_stack", [KM, 2, NH, N], BF16), L.sb("k_stack", [KM, 2, NH, N], BF16)
        ones = L.sb("ones", [2, N], BF16)
        v = L.sb("v", [P, 2, T, NH, 32])
        top = L.sb("top", [P, T, NH])
        top_parts = L.sb("top_parts", [P, 2, T, 2, HH], BF16)
        top_row = L.sb("top_row", [2 * HH, N], BF16)
        e = L.sb("e", [P, 5, 2 * N])
        oT = L.sb("o_groupT", [P, N])
        o_rsum = L.sb("o_rsum", [P, T, GH])
        o, o_T = L.sb("o", [P, T, NH, DH]), L.sb("o_T", [P, N])
        y, z = L.sb("y", [P, T, D]), L.sb("z", [P, T, D])
        ln_x, ln_y = Stats(L, "ln_x"), Stats(L, "ln_y")

        made, ones_in = L.sem("made"), L.sem("ones_in")
        v_made = L.sem("v_made")
        a_ok, aT_mm, aT_ok = L.sem("a_ok"), L.sem("aT_mm"), L.sem("aT_ok")
        qk_mm = L.sem("qk_mm")
        rope_ok, full_ok, rest_ok, part_ok = L.sem("rope_ok"), L.sem("full_ok"), L.sem("rest_ok"), L.sem("part_ok")
        rest_last_ok = L.sem("rest_last_ok")
        stack_in = [L.sem("stack_in_early"), L.sem("stack_in_late")]
        v_mm, v_ok = L.sem("v_mm"), L.sem("v_ok")
        top_mm, top_ok, hi_ok, parts_ok = L.sem("top_mm"), L.sem("top_ok"), L.sem("hi_ok"), L.sem("parts_ok")
        row_mm, row_ok, row_in = L.sem("row_mm"), L.sem("row_ok"), L.sem("row_in")
        score_mm, exp_ok, causal_ok = L.sem("score_mm"), L.sem("exp_ok"), L.sem("causal_ok")
        attn_mm, oT_ok = L.sem("attn_mm"), L.sem("oT_ok")
        natural_mm, rsum_ok, o_ok = L.sem("natural_mm"), L.sem("rsum_ok"), L.sem("o_ok")
        o_T_mm, o_T_ok, out_mm, y_ok, z_ok, x_ok = (L.sem("o_T_mm"), L.sem("o_T_ok"), L.sem("out_mm"), L.sem("y_ok"),
                                                    L.sem("z_ok"), L.sem("x_ok"))

        BK_SCORE, BK_TOP, BK_ATTN, BK_SHARED = 0, 2, 6, 7
        shared = ps[:, BK_SHARED, :]
        shared_td = shared.rearrange("p (t d) -> p t d", t=T)
        shared_bf = shared.bitcast(BF16)
        STACK_IN = 16 * 2 * len(PARTS_Q)

        def e_heads(j):
            return e[:, j, :].rearrange("p (h c) -> p h c", h=2 if j < 4 else 4)

        UNIT = ((0, (0, 1)), (0, (2, 3)), (1, (0, 1)), (1, (2, 3)), (2, (0, 1, 2, 3)))

        with nc.Block() as block:
            @block.sync
            def _(sp):
                def load_top_row(b, half, u):
                    sp.wait_ge(row_ok, 2 * b + half + 1)
                    sp.dma_start(q_stack[KS:KM, u, half * HH:half * HH + HH, :],
                                 top_row[:, :]).then_inc(row_in, 16)

                def load_stacks(g, half, u):
                    for w, (stack, source, which) in enumerate(((q_stack, q_parts, PARTS_Q),
                                                                (k_stack, k_parts, PARTS_K))):
                        sp.wait_ge(rest_last_ok, 2 * g + w + 1)
                        for c, part in enumerate(which):
                            sp.dma_start(stack[c * DH:c * DH + DH, u, half * HH:half * HH + HH, :],
                                         source[half * DH * HH:half * DH * HH + DH * HH, part, :],
                                         ).then_inc(stack_in[half], 16)

                def step(s, u):
                    g, m = s + 2, s + 1
                    if live(s):
                        load_top_row(s, 1, u)
                        sp.wait_ge(score_mm, SLOTS * (2 * s + 1))
                    if live(g):
                        load_stacks(g, 0, u)
                    if live(m):
                        load_top_row(m, 0, 1 - u)
                    if live(g):
                        if live(s):
                            sp.wait_ge(score_mm, SLOTS * (2 * s + 2))
                        load_stacks(g, 1, u)

                sp.wait_ge(made, 1)
                sp.dma_start(k_stack[KS:KM, :, :, :].rearrange("r u h n -> r (u h) n"),
                             ones[:, :].unsqueeze(1).broadcast_to([2, 2 * NH, N])).then_inc(ones_in, 16)
                run_steps(sp, step, FIRST_STEP, 3, 13, B)

            @block.vector
            def _(dve):
                def reduce_unit(m, n):
                    dve.wait_ge(top_mm, SLOTS * m + n + 1)
                    banks = ps[:, BK_TOP + n % 2 * 2:BK_TOP + n % 2 * 2 + 2, :]
                    (qt, h, _), *more = top_unit_parts(n, 0)[0]
                    if qt == 3:
                        r = nc.vector.reduce_max(top[:, 3, h:h + 2], banks, AXX)
                    elif qt == 2:
                        nc.vector.reduce_max(top[:, 2, h:h + 2], banks[:, :, 0:3 * P], AXX)
                        r = nc.vector.reduce_max(top[:, 0, h:h + 2], banks[:, :, 3 * P:N], AXX)
                    else:
                        r = nc.vector.reduce_max(top[:, 1, h:h + 4], banks.rearrange("p i (h c) -> p (i h) c", h=2),
                                                 AXX)
                    r.then_inc(top_ok, 1)

                def split_top(m, half):
                    k = 2 * m + half
                    dve.wait_ge(top_ok, SLOTS * m + SLOTS // 2 * (half + 1))
                    upto(dve, row_mm, k - 1)
                    src = top[:, :, half * HH:half * HH + HH]
                    nc.vector.tensor_scalar(top_parts[:, half, :, 0, :], src, -1.0, None, ALU.mult).then_inc(hi_ok, 1)
                    dve.wait_ge(hi_ok, k + 1)
                    nc.vector.scalar_tensor_tensor(top_parts[:, half, :, 1, :], src, -1.0,
                                                   top_parts[:, half, :, 0, :], ALU.mult,
                                                   ALU.subtract).then_inc(parts_ok, 1)

                def rotate(g, i):
                    dve.wait_ge(qk_mm, 4 * g + i + 1)
                    upto(dve, full_ok, 2 * g + i // 2)
                    out, table = ((by_cos, cos), (by_sin, sin))[i % 2]
                    nc.vector.tensor_tensor(out[:, :], shared, table[:, :], ALU.mult).then_inc(rope_ok, 1)

                def normal_group(b, group):
                    k = GROUPS * b + group
                    dve.wait_ge(natural_mm, k + 1)
                    heads = shared.rearrange("p (t h c) -> p t h c", t=T, h=GH)
                    nc.vector.reciprocal(o_rsum[:, :, :], heads[:, :, :, DH]).then_inc(rsum_ok, 1)
                    dve.wait_ge(rsum_ok, k + 1)
                    if group == 0:
                        upto(dve, o_T_mm, b)
                    nc.vector.tensor_tensor(o[:, :, group * GH:group * GH + GH, :], heads[:, :, :, 0:DH],
                                            o_rsum[:, :, :].unsqueeze(3).broadcast_to([P, T, GH, DH]),
                                            ALU.mult).then_inc(o_ok, 1)

                def step(s, u):
                    l, g, m, p = s + 3, s + 2, s + 1, s - 1
                    for n in range(SLOTS):
                        if live(m):
                            reduce_unit(m, n)
                        for i, slot in enumerate((2, 4, 6, 9)):
                            if live(g) and n == slot:
                                rotate(g, i)
                        if live(p) and n == 3:
                            normal_group(p, 3)
                        for group, slot in enumerate((8, 13, 18)):
                            if live(s) and n == slot:
                                normal_group(s, group)
                        if live(p) and n == 10:
                            dve.wait_ge(y_ok, p + 1)
                            take_moments(core, dve, ln_y, lambda t: y[:, t, :], p)
                        if live(m) and n == 11:
                            split_top(m, 0)
                        if live(p) and n == 14:
                            dve.wait_ge(ln_y.rstd_done, p + 1)
                            upto(dve, x_ok, p)
                            normalize(nc, ln_y, lambda t: z[:, t, :], lambda t: y[:, t, :]).then_inc(z_ok, 1)
                        if live(l) and n == 12:
                            take_moments(core, dve, ln_x, lambda t: x[:, l, t, :], l)
                        if live(l) and n == 16:
                            dve.wait_ge(ln_x.rstd_done, l + 1)
                            upto(dve, aT_mm, l)
                            normalize(nc, ln_x, lambda t: a[:, t, :], lambda t: x[:, l, t, :]).then_inc(a_ok, 1)
                    if live(m):
                        split_top(m, 1)

                nc.vector.memset(ones[:, :], 1.0).then_inc(made, 1)
                step(FIRST_STEP, 1)
                core.wait_weights(dve)
                nc.vector.tensor_copy(future_bf[:, :, :], future[:, :].rearrange("p (i c) -> p i c",
                                                                                i=2)).then_inc(made, 1)
                run_steps(dve, step, FIRST_STEP + 1, 3, 13, B + 1)

            @block.gpsimd
            def _(pool):
                def add_rotated(g, w):
                    k = 2 * g + w
                    pool.wait_ge(rope_ok, 4 * g + 2 * w + 2)
                    upto(pool, rest_ok, k)
                    nc.gpsimd.tensor_tensor(full[:, :], by_cos[:, :], by_sin[:, :], ALU.add).then_inc(full_ok, 1)

                def take_rest(g, w, part):
                    k = 2 * g + w
                    parts = (q_parts, k_parts)[w]
                    pool.wait_ge(part_ok, 2 * k + part + 1)
                    if part == 0:
                        upto(pool, rest_last_ok, k)
                        nc.gpsimd.tensor_tensor(rest[:, :], full[:, :], parts[:, 0, :],
                                                ALU.subtract).then_inc(rest_ok, 1)
                    else:
                        pool.wait_ge(rest_ok, k + 1)
                        if w == 0:
                            for half in range(2):
                                upto(pool, stack_in[half], STACK_IN * g)
                        nc.gpsimd.tensor_tensor(parts[:, 2, :], rest[:, :], parts[:, 1, :],
                                                ALU.subtract).then_inc(rest_last_ok, 1)

                def keep_causal(s, n):
                    j = n % 5
                    pool.wait_ge(exp_ok, 2 * SLOTS * s + 2 * n + 2)
                    pool.sem_inc(core.tick, 1)
                    if j in (2, 3):
                        blocks = e_heads(j)[:, :, 0:2 * P]
                        pattern = [[0, 2], [0, 2], [1, P]]
                    else:
                        blocks = e_heads(j)[:, :, 0:P]
                        pattern = [[0, 2 if j < 4 else 4], [1, P]]
                    nc.gpsimd.affine_select(blocks, blocks, pattern, ALU.is_ge, 0.0, 0, -1).then_inc(causal_ok, 1)

                def step(s, u):
                    l, g, p = s + 3, s + 2, s - 1
                    for n in range(SLOTS):
                        if live(s):
                            keep_causal(s, n)
                        if live(g):
                            for w, slot in ((0, 5), (1, 10)):
                                if n == slot:
                                    add_rotated(g, w)
                                if n == slot + 1:
                                    take_rest(g, w, 0)
                                if n == slot + 3:
                                    take_rest(g, w, 1)
                        if live(p) and n == 12:
                            take_rstd(core, pool, ln_y, p)
                        if live(p) and n == 16:
                            pool.wait_ge(z_ok, p + 1)
                            pool.sem_inc(core.tick, 1)
                            nc.gpsimd.tensor_tensor(x[:, p, :, :], x[:, p, :, :], z[:, :, :],
                                                    ALU.add).then_inc(x_ok, 1)
                        if live(l) and n == 14:
                            take_rstd(core, pool, ln_x, l)

                step(FIRST_STEP, 1)
                nc.gpsimd.memset(v[:, :, :, :, DH:DH + 1], 1.0).then_inc(v_made, 1)
                nc.gpsimd.memset(v[:, :, :, :, DH + 1:32], 0.0).then_inc(v_made, 1)
                run_steps(pool, step, FIRST_STEP + 1, 3, 13, B + 1)

            @block.scalar
            def _(act):
                def exp_unit(s, n):
                    group, j = divmod(n, 5)
                    k = GROUPS * s + group
                    upto(act, attn_mm, 3 * (k - 1) + (1, 1, 2, 2, 3)[j])
                    for i in range(2):
                        act.wait_ge(score_mm, 2 * SLOTS * s + 2 * n + i + 1)
                        nc.scalar.activation(e[:, j, i * N:i * N + N], ps[:, BK_SCORE + i, :], ACT.Exp,
                                             scale=DH ** -0.5).then_inc(exp_ok, 1)

                def take_part(g, w, part):
                    k = 2 * g + w
                    act.wait_ge((full_ok, rest_ok)[part], k + 1)
                    if part == 0 and w == 0:
                        for half in range(2):
                            upto(act, stack_in[half], STACK_IN * g)
                    nc.scalar.copy((q_parts, k_parts)[w][:, part, :],
                                   (full, rest)[part][:, :]).then_inc(part_ok, 1)

                def take_group(s, group):
                    k = GROUPS * s + group
                    act.wait_ge(attn_mm, 3 * k + 3)
                    upto(act, natural_mm, k)
                    nc.scalar.copy(oT[:, :], ps[:, BK_ATTN, :]).then_inc(oT_ok, 1)

                def take_top_rows(b, half):
                    k = 2 * b + half
                    act.wait_ge(row_mm, k + 1)
                    upto(act, row_in, 16 * k)
                    nc.scalar.copy(top_row[:, :], shared_bf[0:2 * HH, 0:N]).then_inc(row_ok, 1)

                def step(s, u):
                    g, m, p = s + 2, s + 1, s - 1
                    for n in range(SLOTS):
                        if live(s):
                            exp_unit(s, n)
                        if live(g) and n == 0:
                            act.wait_ge(aT_mm, g + 1)
                            upto(act, v_mm, g - 1)
                            nc.scalar.copy(aT[:, u, :], shared).then_inc(aT_ok, 1)
                        for w, slots in ((0, (6, 8)), (1, (11, 13))):
                            if live(g) and n in slots:
                                take_part(g, w, slots.index(n))
                        if live(s) and n == 1:
                            take_top_rows(s, 1)
                        if live(p) and n == 1:
                            take_group(p, 3)
                        if live(p) and n == 5:
                            act.wait_ge(o_T_mm, p + 1)
                            upto(act, out_mm, p)
                            nc.scalar.copy(o_T[:, :], shared).then_inc(o_T_ok, 1)
                        for group, slot in enumerate((6, 11, 16)):
                            if live(s) and n == slot:
                                take_group(s, group)
                        if live(p) and n == 7:
                            act.wait_ge(out_mm, p + 1)
                            upto(act, z_ok, p)
                            nc.scalar.copy(y[:, :, :], shared_td).then_inc(y_ok, 1)
                        if live(m) and n == 11:
                            act.wait_ge(v_mm, m + 1)
                            upto(act, attn_mm, 3 * GROUPS * (m - 1))
                            nc.scalar.copy(v[:, 1 - u, :, :, 0:DH], shared.rearrange(
                                "p (t h d) -> p t h d", t=T, h=NH)).then_inc(v_ok, 1)
                        if live(m) and n == 15:
                            take_top_rows(m, 0)

                run_steps(act, step, FIRST_STEP, 3, 13, B + 1)

            @block.tensor
            def _(pe):
                def score_unit(s, n, i, u):
                    group, j = divmod(n, 5)
                    if n % (SLOTS // 2) == 0 and i == 0:
                        pe.wait_ge(row_in, 16 * (2 * s + n // (SLOTS // 2) + 1))
                    upto(pe, exp_ok, 2 * SLOTS * s + 2 * n + i - 1)
                    kt, heads = UNIT[j]
                    for k, h in enumerate(heads[len(heads) // 2 * i:len(heads) // 2 * (i + 1)]):
                        head = group * GH + h
                        for tile, c in ((3, 0), (1, P)) if kt == 1 else ((kt, 2 * P * k),):
                            last = nc.tensor.matmul(
                                ps[:, BK_SCORE + i, c:c + N - tile * P],
                                k_stack[:, u, head, tile * P:tile * P + P], q_stack[:, u, head, tile * P:N],
                                start=True, stop=True)
                    last.then_inc(score_mm, 1)

                def top_unit(m, n, i, u):
                    if n % (SLOTS // 2) == 0 and i == 0:
                        pe.wait_ge(stack_in[n // (SLOTS // 2)], STACK_IN * (m + 1))
                    if i == 0:
                        upto(pe, top_ok, SLOTS * m + n - 1)
                    bank = ps[:, BK_TOP + n % 2 * 2 + i, :]
                    parts, (mask_at, masks) = top_unit_parts(n, i)
                    for j, (qt, head, c) in enumerate(parts):
                        nc.tensor.matmul(bank[:, c:c + (qt + 1) * P], q_stack[0:KS, u, head, qt * P:qt * P + P],
                                         k_stack[0:KS, u, head, 0:(qt + 1) * P], start=j == 0, stop=False,
                                         skip_group_check=True)
                    if masks == 1:
                        out = bank[:, mask_at:mask_at + P]
                    else:
                        stride = P if mask_at == 2 * P else 2 * P
                        out = bank.rearrange("p (i c) -> p i c", c=P)[:, mask_at // P::stride // P, :]
                    last = nc.tensor.matmul(out, core.ident_bf[:, :], future_bf[:, 0:masks, :], start=False,
                                            stop=True, skip_group_check=True)
                    if i == 1:
                        last.then_inc(top_mm, 1)

                def attend(b, group, part, u):
                    if part == 0:
                        if group == 0:
                            pe.wait_ge(v_ok, b + 1)
                        upto(pe, oT_ok, GROUPS * b + group)
                    pe.wait_ge(causal_ok, SLOTS * b + 5 * group + (2, 4, 5)[part])
                    for tile in ((0,), (1, 3), (2,))[part]:
                        for h in range(GH):
                            if tile == 2:
                                src = e_heads(4)[:, h, :]
                            else:
                                j = (0 if tile == 0 else 2) + h // 2
                                c = P if tile == 1 else 0
                                src = e_heads(j)[:, h % 2, c:c + N - tile * P]
                            last = nc.tensor.matmul(ps[32 * h:32 * h + 32, BK_ATTN, tile * P:N],
                                                    v[:, u, tile, group * GH + h, :], src, start=tile == 0,
                                                    stop=tile == 2, tile_position=(0, 32 * h), skip_group_check=True)
                    last.then_inc(attn_mm, 1)

                def use_shared(s, task):
                    before = shared_user_before(s, task)
                    if before is None:
                        return
                    name, b = before
                    if name == "aT":
                        pe.wait_ge(aT_ok, b + 1)
                    elif name in ("top_early", "top_late"):
                        pe.wait_ge(row_ok, 2 * b + 1 + (name == "top_late"))
                    elif name in ("q", "q_turned", "k", "k_turned"):
                        i = ("q", "q_turned", "k", "k_turned").index(name)
                        pe.wait_ge(rope_ok, 4 * b + i + 1)
                    elif name == "v":
                        pe.wait_ge(v_ok, b + 1)
                    elif name == "oT":
                        pe.wait_ge(o_T_ok, b + 1)
                    elif name == "out":
                        pe.wait_ge(y_ok, b + 1)
                    else:
                        group = 3 if name == "natural_late" else int(name[-1])
                        pe.wait_ge(o_ok, GROUPS * b + group + 1)

                def natural(b, group):
                    pe.wait_ge(oT_ok, GROUPS * b + group + 1)
                    for t in range(T):
                        last = nc.tensor.transpose(shared_td[:, t, :], oT[:, t * P:t * P + P], core.ident[:, :])
                    last.then_inc(natural_mm, 1)

                def top_rows(b, half):
                    pe.wait_ge(parts_ok, 2 * b + half + 1)
                    for t in range(T):
                        last = nc.tensor.transpose(shared_bf[0:2 * HH, t * P:t * P + P],
                                                   top_parts[:, half, t, :, :], core.ident_bf[:, :])
                    last.then_inc(row_mm, 1)

                def step(s, u):
                    g, m, p = s + 2, s + 1, s - 1
                    for n in range(SLOTS):
                        for i in range(2):
                            if live(s):
                                score_unit(s, n, i, u)
                            if live(m):
                                top_unit(m, n, i, 1 - u)
                        if n == 0 and live(p):
                            attend(p, 3, 1, 1 - u)
                        if n == 1 and live(p):
                            attend(p, 3, 2, 1 - u)
                        if live(s):
                            if n % 5 == 3:
                                attend(s, n // 5, 0, u)
                            if n % 5 == 0 and n:
                                attend(s, n // 5 - 1, 1, u)
                            if n % 5 == 1 and n > 1:
                                attend(s, n // 5 - 1, 2, u)
                        for slot, task, ahead in SHARED:
                            if slot != n or not live(s + ahead):
                                continue
                            use_shared(s, task)
                            if task == "aT":
                                pe.wait_ge(a_ok, g + 1)
                                for t in range(T):
                                    last = nc.tensor.transpose(shared_td[:, t, :], a[:, t, :], core.ident[:, :])
                                last.then_inc(aT_mm, 1)
                            elif task in ("q", "q_turned", "k", "k_turned"):
                                if task == "q":
                                    pe.wait_ge(aT_ok, g + 1)
                                w = {"q": w_q, "q_turned": w_q_turned, "k": w_k, "k_turned": w_k_turned}[task]
                                nc.tensor.matmul(shared, w[:, :], aT[:, u, :], start=True,
                                                 stop=True).then_inc(qk_mm, 1)
                            elif task == "v":
                                for t in range(T):
                                    last = nc.tensor.matmul(shared_td[:, t, :], aT[:, 1 - u, t * P:t * P + P],
                                                            w_v[:, :], start=True, stop=True)
                                last.then_inc(v_mm, 1)
                            elif task == "top_late":
                                top_rows(s, 1)
                            elif task == "top_early":
                                top_rows(m, 0)
                            elif task == "natural_late":
                                natural(p, 3)
                            elif task.startswith("natural"):
                                natural(s, int(task[-1]))
                            elif task == "oT":
                                pe.wait_ge(o_ok, GROUPS * p + GROUPS)
                                for t in range(T):
                                    last = nc.tensor.transpose(shared_td[:, t, :], o[:, t, :, :].rearrange(
                                        "p h d -> p (h d)"), core.ident[:, :])
                                last.then_inc(o_T_mm, 1)
                            elif task == "out":
                                pe.wait_ge(o_T_ok, p + 1)
                                for t in range(T):
                                    last = nc.tensor.matmul(shared_td[:, t, :], o_T[:, t * P:t * P + P],
                                                            w_o[:, :], start=True, stop=True)
                                last.then_inc(out_mm, 1)

                core.wait_weights(pe)
                step(FIRST_STEP, 1)
                step(FIRST_STEP + 1, 0)
                pe.wait_ge(made, 2)
                step(FIRST_STEP + 2, 1)
                pe.wait_ge(ones_in, 16)
                pe.wait_ge(v_made, 2)
                run_steps(pe, step, 0, 3, 13, B + 1)


def soft_mixture(core):
    nc, dram, x, ps = core.nc, core.dram, core.x, core.ps
    with ExitStack() as ctx:
        L = Layer(core, "moe", ctx)
        w1, w2, gamma_row, gamma_slot_row, gamma, slot_raw = (
            core.weights[name] for name in ("w1", "w2", "gamma_x", "gamma_slot", "gamma_x_column", "slot_embeds"))
        slot_n = L.sb("slot_n", [P, T, D])
        slotT, slotT_bf = L.sb("slotT", [P, E_T]), L.sb("slotT_bf", [P, E_T], BF16)
        ones = L.sb("ones", [2, P], BF16)
        a, unit = L.sb("a", [P, T, D]), L.sb("unit", [P, T, D])
        mean_sq, mean_sq_sum, rrms = L.sb("mean_sq", [P, T]), L.sb("mean_sq_sum", [P, T]), L.sb("rrms", [P, T])
        token = L.sb("token", [P, 2, T, D + 1])
        tokenT, tokenT_bf = L.sb("tokenT", [P, 2, N]), L.sb("tokenT_bf", [P, N], BF16)
        top = L.sb("top", [P, 2, 2 * T])
        top_parts = L.sb("top_parts", [P, T, 2], BF16)
        top_row = L.sb("top_row", [2, 2, T, P], BF16)
        shifted = L.sb("shifted", [P, 2, E_T])
        weight = L.sb("weight", [P, 2 * T, N])
        slot_rsum, slot_in = L.sb("slot_rsum", [P, T]), L.sb("slot_in", [P, T, D])
        slot_inT, hiddenT = L.sb("slot_inT", [P, E_T]), L.sb("hiddenT", [P, FF // P, E_T])
        slot_out = L.sb("slot_out", [P, T, D + 1])
        y_rsum, y, z = L.sb("y_rsum", [P, T]), L.sb("y", [P, T, D]), L.sb("z", [P, T, D])
        ln_x, rms, ln_y = Stats(L, "ln_x"), Stats(L, "rms"), Stats(L, "ln_y")

        made = L.sem("made")
        a_ok, mean_sq_ok, rrms_ok, unit_ok = L.sem("a_ok"), L.sem("mean_sq_ok"), L.sem("rrms_ok"), L.sem("unit_ok")
        token_ok, tokenT_mm, tokenT_ok, tokenT_bf_ok = (L.sem("token_ok"), L.sem("tokenT_mm"), L.sem("tokenT_ok"),
                                                        L.sem("tokenT_bf_ok"))
        top_mm, top_ok, hi_ok, parts_ok = L.sem("top_mm"), L.sem("top_ok"), L.sem("hi_ok"), L.sem("parts_ok")
        row_mm, row_ok = L.sem("row_mm"), L.sem("row_ok")
        logit_mm, shifted_ok, rank_mm, weight_ok = (L.sem("logit_mm"), L.sem("shifted_ok"), L.sem("rank_mm"),
                                                    L.sem("weight_ok"))
        turned_mm, combine_ok = L.sem("turned_mm"), L.sem("combine_ok")
        slot_mm, slot_rsum_ok, slot_ok = L.sem("slot_mm"), L.sem("slot_rsum_ok"), L.sem("slot_ok")
        slotT_mm, slotT_ok = L.sem("slotT_mm"), L.sem("slotT_ok")
        hidden_mm, hidden_ok = L.sem("hidden_mm"), L.sem("hidden_ok")
        slot_out_mm, slot_out_ok = L.sem("slot_out_mm"), L.sem("slot_out_ok")
        out_mm, y_rsum_ok, y_ok, z_ok, x_ok = (L.sem("out_mm"), L.sem("y_rsum_ok"), L.sem("y_ok"), L.sem("z_ok"),
                                               L.sem("x_ok"))
        stored, table_ok = L.sem("stored"), L.sem("table_ok")
        warm = L.sb("warm", [P, 1])

        BK_T, BK_TURNED, BK_TOP, BK_ROW, BK_LOGIT, BK_WIDE = 0, 1, 2, 3, 4, 6
        row_ps = ps[:, BK_ROW, :].bitcast(BF16)

        def wide(t):
            return ps[:, BK_WIDE + t // 2, t % 2 * (D + 1):t % 2 * (D + 1) + D + 1]

        def wide_sums(bank):
            return ps[:, BK_WIDE + bank, 0:2 * (D + 1)].rearrange("p (t c) -> p t c", t=2)[:, :, D]

        def take_rrms(pool, k):
            pool.wait_ge(rms.moments_done, k + 1)
            nc.gpsimd.tensor_tensor(mean_sq[:, :], rms.moments[:, :, 0], rms.moments[:, :, 0],
                                    ALU.mult).then_inc(mean_sq_ok, 1)
            pool.wait_ge(mean_sq_ok, 3 * k + 1)
            nc.gpsimd.tensor_tensor(mean_sq_sum[:, :], mean_sq[:, :], rms.moments[:, :, 1],
                                    ALU.add).then_inc(mean_sq_ok, 1)
            pool.wait_ge(mean_sq_ok, 3 * k + 2)
            pool.sem_inc(core.tick, 1)
            nc.gpsimd.tensor_scalar(mean_sq[:, :], mean_sq_sum[:, :], NORM_FLOOR, None,
                                    ALU.max).then_inc(mean_sq_ok, 1)
            pool.wait_ge(mean_sq_ok, 3 * k + 3)
            nc.gpsimd.tensor_tensor(rrms[:, :], mean_sq[:, :], core.minus_half[:, :],
                                    ALU.pow).then_inc(rrms_ok, 1)

        with nc.Block() as block:
            @block.vector
            def _(dve):
                def top_unit(f, fu, i):
                    dve.wait_ge(top_mm, 8 * f + i + 1)
                    nc.vector.reduce_max(top[:, fu, i:i + 1], ps[:, BK_TOP + i % 2, :], AXX).then_inc(top_ok, 1)

                def step(s, u):
                    g, f, fu, p = s + 2, s + 1, 1 - u, s - 1
                    if live(p):
                        for j in range(2):
                            dve.wait_ge(out_mm, 2 * p + j + 1)
                            nc.vector.reciprocal(y_rsum[:, 2 * j:2 * j + 2], wide_sums(j)).then_inc(y_rsum_ok, 1)
                            dve.wait_ge(y_rsum_ok, 2 * p + j + 1)
                            for t in (2 * j, 2 * j + 1):
                                last = nc.vector.tensor_scalar(y[:, t, :], wide(t)[:, 0:D], y_rsum[:, t:t + 1],
                                                               None, ALU.mult)
                            last.then_inc(y_ok, 1)
                    for i in range(T):
                        if live(s):
                            dve.wait_ge(logit_mm, 4 * s + i + 1)
                            if i == 0:
                                dve.wait_ge(top_ok, 8 * s + 8)
                            upto(dve, turned_mm, 4 * s + i - 1)
                            nc.vector.tensor_scalar(shifted[:, i % 2, :], ps[:, BK_LOGIT + i % 2, :],
                                                    top[:, u, T + i:T + i + 1], None,
                                                    ALU.subtract).then_inc(shifted_ok, 1)
                        if live(f) and i == 0:
                            dve.wait_ge(tokenT_ok, f + 1)
                            nc.vector.tensor_copy(tokenT_bf[:, :], tokenT[:, fu, :]).then_inc(tokenT_bf_ok, 1)
                        if live(f) and i == 1:
                            top_unit(f, fu, 0)
                        if live(f) and i == 2:
                            top_unit(f, fu, 1)
                            top_unit(f, fu, 2)
                    if live(f):
                        top_unit(f, fu, 3)
                        dve.wait_ge(top_ok, 8 * f + 4)
                        upto(dve, row_mm, f)
                        nc.vector.tensor_scalar(top_parts[:, :, 0], top[:, fu, 0:T], -1.0, None,
                                                ALU.mult).then_inc(hi_ok, 1)
                        dve.wait_ge(hi_ok, f + 1)
                        nc.vector.scalar_tensor_tensor(top_parts[:, :, 1], top[:, fu, 0:T], -1.0, top_parts[:, :, 0],
                                                       ALU.mult, ALU.subtract).then_inc(parts_ok, 1)
                    if live(p):
                        dve.wait_ge(y_ok, 2 * p + 2)
                        take_moments(core, dve, ln_y, lambda t: y[:, t, :], p)
                    if live(s):
                        for j in range(2):
                            dve.wait_ge(slot_mm, 2 * s + j + 1)
                            nc.vector.reciprocal(slot_rsum[:, 2 * j:2 * j + 2], wide_sums(j)).then_inc(slot_rsum_ok, 1)
                            dve.wait_ge(slot_rsum_ok, 2 * s + j + 1)
                            for t in (2 * j, 2 * j + 1):
                                last = nc.vector.tensor_scalar(slot_in[:, t, :], wide(t)[:, 0:D],
                                                               slot_rsum[:, t:t + 1], None, ALU.mult)
                            last.then_inc(slot_ok, 1)
                    if live(f):
                        top_unit(f, fu, 4)
                    if live(g):
                        dve.wait_ge(ln_x.rstd_done, g + 1)
                        normalize(nc, ln_x, lambda t: a[:, t, :], lambda t: x[:, g, t, :]).then_inc(a_ok, 1)
                    if live(f):
                        top_unit(f, fu, 5)
                        top_unit(f, fu, 6)
                    if live(g):
                        dve.wait_ge(a_ok, g + 1)
                        take_moments(core, dve, rms, lambda t: a[:, t, :], g + 1)
                    if live(f):
                        top_unit(f, fu, 7)
                    if live(p):
                        dve.wait_ge(ln_y.rstd_done, p + 1)
                        upto(dve, x_ok, p)
                        normalize(nc, ln_y, lambda t: z[:, t, :], lambda t: y[:, t, :]).then_inc(z_ok, 1)
                    if live(s):
                        upto(dve, out_mm, 2 * s)
                        for j in range(2):
                            dve.wait_ge(slot_out_mm, 2 * s + j + 1)
                            nc.vector.tensor_copy(slot_out[:, 2 * j:2 * j + 2, 0:D],
                                                  ps[:, BK_T + j, 0:2 * D].rearrange(
                                                      "p (t d) -> p t d", t=2)).then_inc(slot_out_ok, 1)
                    if live(g):
                        dve.wait_ge(rrms_ok, g + 2)
                        upto(dve, token_ok, g)
                        upto(dve, tokenT_mm, g)
                        for t in range(T):
                            last = nc.vector.tensor_scalar(unit[:, t, :], a[:, t, :], rrms[:, t:t + 1], None, ALU.mult)
                        last.then_inc(unit_ok, 1)
                    h = s + 3
                    if live(h):
                        take_moments(core, dve, ln_x, lambda t: x[:, h, t, :], h)

                core.wait_weights(dve)
                take_moments(core, dve, rms, lambda t: slot_raw[:, t, :], 0)
                step(-3, 1)
                nc.vector.memset(ones[:, :], 1.0)
                nc.vector.memset(token[:, :, :, D:D + 1], 1.0)
                nc.vector.memset(slot_out[:, :, D:D + 1], 1.0)
                dve.wait_ge(rrms_ok, 1)
                for t in range(T):
                    last = nc.vector.scalar_tensor_tensor(slot_n[:, t, :], slot_raw[:, t, :], rrms[:, t:t + 1],
                                                          gamma_slot_row[:, :], ALU.mult, ALU.mult)
                last.then_inc(made, 1)
                step(-2, 0)
                dve.wait_ge(made, 2)
                nc.vector.tensor_copy(slotT[:, :], ps[:, BK_TURNED, :]).then_inc(made, 1)
                dve.wait_ge(made, 3)
                nc.vector.tensor_copy(slotT_bf[:, :], slotT[:, :]).then_inc(made, 1)
                run_steps(dve, step, -1, 3, 11, B + 1)

            @block.gpsimd
            def _(pool):
                def step(s, u):
                    h, g, f, p = s + 3, s + 2, s + 1, s - 1
                    if live(f):
                        pool.wait_ge(unit_ok, f + 1)
                        upto(pool, slot_mm, 2 * (f - 1))
                        nc.gpsimd.tensor_tensor(token[:, 1 - u, :, 0:D], unit[:, :, :],
                                                gamma_row[:, :].unsqueeze(1).broadcast_to([P, T, D]),
                                                ALU.mult).then_inc(token_ok, 1)
                    if live(p):
                        take_rstd(core, pool, ln_y, p)
                    if live(g):
                        take_rrms(pool, g + 1)
                    if live(p):
                        pool.wait_ge(z_ok, p + 1)
                        pool.sem_inc(core.tick, 1)
                        nc.gpsimd.tensor_tensor(x[:, p, :, :], x[:, p, :, :], z[:, :, :], ALU.add).then_inc(x_ok, 1)
                    if live(h):
                        take_rstd(core, pool, ln_x, h)

                take_rrms(pool, 0)
                run_steps(pool, step, -3, 3, 11, B + 1)

            @block.sync
            def _(sp):
                with sp.Fori(0, B) as b:
                    sp.wait_ge(x_ok, b + 1)
                    sp.dma_start(dram["out"][b].rearrange("(t p) d -> p t d", p=P),
                                 x[:, b, :, :]).then_inc(stored, 16)
                sp.wait_ge(stored, 16 * B)

            @block.scalar
            def _(act):
                def load_table(function, k):
                    upto(act, table_ok, k - 1)
                    nc.scalar.activation(warm[:, :], core.eps[:, 0:1], function).then_inc(table_ok, 1)

                def step(s, u):
                    f = s + 1
                    if live(f):
                        act.wait_ge(tokenT_mm, f + 1)
                        upto(act, logit_mm, 4 * (f - 1))
                        nc.scalar.activation(tokenT[:, 1 - u, :], ps[:, BK_T, :], ACT.Copy,
                                             scale=gamma[:, 0:1]).then_inc(tokenT_ok, 1)
                    if live(s):
                        for i in range(T):
                            act.wait_ge(rank_mm, 4 * s + i + 1)
                            if i == 0:
                                upto(act, slot_mm, 2 * s)
                            nc.scalar.activation(weight[:, i, :], ps[:, BK_LOGIT + i % 2, :],
                                                 ACT.Exp).then_inc(weight_ok, 1)
                            act.wait_ge(turned_mm, 4 * s + i + 1)
                            if i == 0:
                                upto(act, out_mm, 2 * s)
                            nc.scalar.activation(weight[:, T:2 * T, i * P:i * P + P],
                                                 ps[:, BK_TURNED, :].rearrange("p (e c) -> p e c", e=T),
                                                 ACT.Exp).then_inc(combine_ok, 1)
                    if live(f):
                        act.wait_ge(row_mm, f + 1)
                        upto(act, rank_mm, 4 * (f - 1))
                        nc.scalar.copy(top_row[:, 1 - u, :, :], row_ps[0:2, 0:E_T].rearrange(
                            "r (i p) -> r i p", i=T)).then_inc(row_ok, 1)
                    if live(s):
                        load_table(ACT.Gelu, 2 * s + 1)
                        upto(act, hidden_mm, 4 * s)
                        for j in range(2):
                            act.wait_ge(slotT_mm, 2 * s + j + 1)
                            nc.scalar.copy(slot_inT[:, 2 * j * P:2 * (j + 1) * P],
                                           ps[:, BK_T + j, 0:2 * P]).then_inc(slotT_ok, 1)
                        upto(act, slot_out_mm, 2 * s)
                        for j in range(FF // P):
                            act.wait_ge(hidden_mm, 4 * s + j + 1)
                            nc.scalar.activation(hiddenT[:, j, :], ps[:, BK_LOGIT + j % 2, :],
                                                 ACT.Gelu).then_inc(hidden_ok, 1)
                        load_table(ACT.Exp, 2 * s + 2)

                core.wait_weights(act)
                run_steps(act, step, -2, 1, 13, B)

            @block.tensor
            def _(pe):
                def top_unit(f, i):
                    upto(pe, top_ok, 8 * f + i - 1)
                    if i == 5:
                        pe.wait_ge(row_ok, f + 1)
                    lhs, rhs = (slotT_bf, tokenT_bf) if i < T else (tokenT_bf, slotT_bf)
                    c = i % T * P
                    nc.tensor.matmul(ps[:, BK_TOP + i % 2, :], lhs[:, c:c + P], rhs[:, :], start=True,
                                     stop=True).then_inc(top_mm, 1)

                def logits(s, u, i):
                    if i >= 2:
                        pe.wait_ge(weight_ok, 4 * s + i - 1)
                    nc.tensor.matmul(ps[:, BK_LOGIT + i % 2, :], tokenT[:, u, i * P:i * P + P], slotT[:, :],
                                     start=True, stop=False, skip_group_check=True).then_inc(logit_mm, 1)

                def finish_logits(s, u, i):
                    pe.wait_ge(shifted_ok, 4 * s + i + 1)
                    nc.tensor.matmul(ps[:, BK_LOGIT + i % 2, :], ones[:, :], top_row[:, u, :, :], start=False,
                                     stop=True, skip_group_check=True).then_inc(rank_mm, 1)
                    upto(pe, combine_ok, 4 * s + i)
                    for e in range(T):
                        last = nc.tensor.transpose(ps[:, BK_TURNED, e * P:e * P + P],
                                                   shifted[:, i % 2, e * P:e * P + P], core.ident[:, :])
                    last.then_inc(turned_mm, 1)

                def step(s, u):
                    f = s + 1
                    if live(f):
                        pe.wait_ge(unit_ok, f + 1)
                        upto(pe, slot_out_ok, 2 * (f - 1))
                        for t in range(T):
                            last = nc.tensor.transpose(ps[:, BK_T, t * P:t * P + P], unit[:, t, :], core.ident[:, :])
                        last.then_inc(tokenT_mm, 1)
                    if live(s):
                        upto(pe, hidden_ok, 4 * s)
                        logits(s, u, 0)
                        pe.wait_ge(row_ok, s + 1)
                        for i in range(1, T):
                            logits(s, u, i)
                            finish_logits(s, u, i - 1)
                            if i == 1 and live(f):
                                pe.wait_ge(tokenT_bf_ok, f + 1)
                            for k in ((0, 1), (2,), (3,))[i - 1] if live(f) else ():
                                top_unit(f, k)
                        finish_logits(s, u, 3)
                    elif live(f):
                        pe.wait_ge(tokenT_bf_ok, f + 1)
                        for i in range(T):
                            top_unit(f, i)
                    if live(f):
                        pe.wait_ge(parts_ok, f + 1)
                        for i in range(T):
                            last = nc.tensor.transpose(row_ps[0:2, i * P:i * P + P], top_parts[:, i, :],
                                                       core.ident_bf[:, :])
                        last.then_inc(row_mm, 1)
                    if live(s):
                        pe.wait_ge(weight_ok, 4 * s + 4)
                        pe.wait_ge(token_ok, s + 1)
                        upto(pe, y_ok, 2 * s)
                        for e in range(T):
                            for t in range(T):
                                last = nc.tensor.matmul(wide(e), weight[:, t, e * P:e * P + P], token[:, u, t, :],
                                                        start=t == 0, stop=t == T - 1)
                            if e % 2:
                                last.then_inc(slot_mm, 1)
                    if live(f):
                        top_unit(f, 4)
                    if live(s):
                        for e in range(T):
                            if e == 2 and live(f):
                                top_unit(f, 5)
                            if e % 2 == 0:
                                pe.wait_ge(slot_ok, 2 * s + e // 2 + 1)
                            if e == 2:
                                pe.wait_ge(combine_ok, 4 * s + 4)
                            last = nc.tensor.transpose(ps[:, BK_T + e // 2, e % 2 * P:e % 2 * P + P], slot_in[:, e, :],
                                                       core.ident[:, :])
                            if e % 2:
                                last.then_inc(slotT_mm, 1)
                    elif live(f):
                        top_unit(f, 5)
                    if live(f):
                        top_unit(f, 6)
                    if live(s):
                        pe.wait_ge(slotT_ok, 2 * s + 2)
                        for j in range(FF // P):
                            if j >= 2:
                                pe.wait_ge(hidden_ok, 4 * s + j - 1)
                            nc.tensor.matmul(ps[:, BK_LOGIT + j % 2, :], w1[:, j * P:j * P + P], slot_inT[:, :],
                                             start=True, stop=True).then_inc(hidden_mm, 1)
                            if j == 1 and live(f):
                                top_unit(f, 7)
                    elif live(f):
                        top_unit(f, 7)
                    if live(s):
                        for e in range(T):
                            for j in range(FF // P):
                                if e == 0:
                                    pe.wait_ge(hidden_ok, 4 * s + j + 1)
                                last = nc.tensor.matmul(ps[:, BK_T + e // 2, e % 2 * D:e % 2 * D + D],
                                                        hiddenT[:, j, e * P:e * P + P], w2[:, j, :], start=j == 0, stop=j == FF // P - 1)
                            if e % 2:
                                last.then_inc(slot_out_mm, 1)
                        for t in range(T):
                            for e in range(T):
                                if t == 0 and e % 2 == 0:
                                    pe.wait_ge(slot_out_ok, 2 * s + e // 2 + 1)
                                last = nc.tensor.matmul(wide(t), weight[:, T + e, t * P:t * P + P],
                                                        slot_out[:, e, :], start=e == 0, stop=e == T - 1)
                            if t % 2:
                                last.then_inc(out_mm, 1)

                pe.wait_ge(made, 1)
                for t in range(T):
                    last = nc.tensor.transpose(ps[:, BK_TURNED, t * P:t * P + P], slot_n[:, t, :], core.ident[:, :])
                last.then_inc(made, 1)
                pe.wait_ge(made, 4)
                run_steps(pe, step, -1, 1, 13, B)


def build(nc, dram):
    with ExitStack() as ctx:
        core = Core(nc, ctx, dram)
        core.tick = core.sem("tick")
        gated_attention(core)
        channel_mix(core)
        causal_attention(core)
        soft_mixture(core)


def kernel(**inputs):
    import concourse.bacc as bacc
    from concourse.bass_utils import run_bass_kernel_spmd

    got = {name: np.asarray(a) for name, a in inputs.items()}
    arrays = {}
    for name, a in got.items():
        short = name.split("_", 2)[2]
        arrays[short] = a
    for name in ("W_r", "W_k", "W_v", "Wv", "Wo"):
        arrays[f"{name}_T"] = arrays.pop(name).T
    for name in ("Wq", "Wk"):
        w = arrays.pop(name)
        arrays[f"{name}_T"] = w[qk_rows()].T
        arrays[f"{name}_turned_T"] = w[qk_rows(turned=True)].T
    arrays["gau_vectors"] = np.stack([arrays["ln_g"], arrays["ln_b"], arrays["b_qk"],
                                      *arrays["b_hidden"][HID:].reshape(2, D), *arrays["os_gamma"],
                                      *arrays["os_beta"]], axis=1)
    arrays["mix_vectors"] = np.stack([arrays.pop("mu_r"), arrays.pop("mu_k")], axis=1)
    for name in ("ln_g", "ln_b", "b_qk", "os_gamma", "os_beta"):
        arrays.pop(name)
    arrays.update(constants())
    arrays = {name: np.ascontiguousarray(a) for name, a in arrays.items()}

    nc = bacc.Bacc("TRN2", target_bir_lowering=False, num_devices=1)
    dram = {name: nc.dram_tensor(f"in_{name}", a.shape, mybir.dt.from_np(a.dtype), kind="ExternalInput").ap()
            for name, a in arrays.items()}
    dram["out"] = nc.dram_tensor("out", (B, N, D), F32, kind="ExternalOutput").ap()
    build(nc, dram)
    result = run_bass_kernel_spmd(nc, [{f"in_{name}": a for name, a in arrays.items()}], core_ids=[0])
    return result.results[0]["out"]
```

```python
from contextlib import ExitStack

import numpy as np

import concourse.bass as bass
from concourse import mybir
from concourse.alu_op_type import AluOpType as ALU

F32 = mybir.dt.float32
BF16 = mybir.dt.bfloat16
ACT = mybir.ActivationFunctionType
AXX = mybir.AxisListType.X

P = 128
B = 16
N = 512
T = N // P
D = 128
HID = 256
NH, DH = 16, 8
HH = NH // 2
E_T = 512
FF = 512
EPS = 1e-5
NORM_FLOOR = 1e-24 / D
MASKED = -1e30
PARTS_Q = (0, 0, 1, 1, 0, 2)
PARTS_K = (0, 1, 0, 1, 2, 0)
KS = DH * len(PARTS_Q)
KM = KS + 2


def live(b):
    return not isinstance(b, int) or 0 <= b < B


def upto(engine, sem, value):
    if not isinstance(value, int) or value > 0:
        engine.wait_ge(sem, value)


def run_steps(engine, step, first, loop_from, loop_to, last):
    for s in range(first, loop_from):
        step(s, s % 2)
    with engine.Fori(0, (loop_to - loop_from) // 2) as pair:
        for k in range(2):
            step(2 * pair + (loop_from + k), (loop_from + k) % 2)
    for s in range(loop_to, last):
        step(s, s % 2)


def qk_rows():
    half, d, h = np.meshgrid(np.arange(2), np.arange(DH), np.arange(HH), indexing="ij")
    return ((half * HH + h) * DH + d).reshape(-1)


def constants():
    p, col = np.arange(P), np.arange(N)
    inv_freq = (1.0 / np.float32(10000.0) ** (np.arange(0, DH, 2, dtype=np.float32) / DH)).astype(np.float32)
    d = p // HH % DH
    angle = col.astype(np.float32)[None, :] * inv_freq[d % (DH // 2)][:, None]
    tables = {
        "ident": np.eye(P),
        "keep": np.where((col[None, :] >= p[:, None]) | (col[None, :] >= P), 1.0, 0.0),
        "inv_pos": np.broadcast_to(1.0 / (col[None, :] + 1.0), (P, N)),
        "cos": np.cos(angle),
        "sin": np.sin(angle) * np.where(d < DH // 2, 1.0, -1.0)[:, None],
        "future": np.tile(np.where(p[None, :] > p[:, None], MASKED, 0.0), (1, 2)),
    }
    return {name: np.ascontiguousarray(a, dtype=np.float32) for name, a in tables.items()}


ATT_WEIGHTS = ("Wq_T", "Wk_T", "Wv_T", "Wo_T")


class Core:

    def __init__(self, nc, ctx, dram):
        self.nc, self.ctx, self.dram = nc, ctx, dram
        self.x = self.sb("x", [P, B, T, D])
        self.ps = ctx.enter_context(nc.psum_tensor("ps", [P, 8, N], F32))
        self.ident = self.sb("ident", [P, P])
        self.ident_bf = self.sb("ident_bf", [P, P], BF16)
        self.eps = self.sb("eps", [P, T])
        self.minus_half = self.sb("minus_half", [P, T])
        self.minus_one = self.sb("minus_one", [P, T])
        self.weights = {}
        self.loads = []
        self.weights_in = self.sem("weights_in")
        for name in ("W_r_T", "W_k_T", "W_v_T", *ATT_WEIGHTS):
            self.to_load(name, [P, D], dram[name])
        self.to_load("mix_vectors", [P, 2], dram["mix_vectors"])
        for name in ("cos", "sin"):
            self.to_load(name, [P, N], dram[name])
        self.to_load("future", [P, 2 * P], dram["future"])
        self.to_load("w1", [P, FF], dram["w1"])
        self.to_load("w2", [P, FF // P, D], dram["w2"].rearrange("(j p) d -> p j d", p=P))
        for name in ("gamma_x", "gamma_slot"):
            self.to_load(name, [P, D], dram[name].partition_broadcast(P))
        self.to_load("gamma_x_column", [P, 1], dram["gamma_x"].rearrange("(p o) -> p o", o=1))
        self.to_load("slot_embeds", [P, T, D], dram["slot_embeds"].rearrange("(h e) s d -> (e s) h d", h=T))

    def to_load(self, name, shape, source):
        self.weights[name] = self.sb(name, shape)
        self.loads.append((self.weights[name][tuple(slice(None) for _ in shape)], source))

    def load_weights(self, sp):
        for dst, src in self.loads:
            sp.dma_start(dst, src).then_inc(self.weights_in, 16)

    def wait_weights(self, engine):
        engine.wait_ge(self.weights_in, 16 * len(self.loads))

    def sb(self, name, shape, dtype=F32):
        return self.ctx.enter_context(self.nc.sbuf_tensor(name, shape, dtype))

    def sem(self, name):
        return self.ctx.enter_context(self.nc.semaphore(name))


class Layer:

    def __init__(self, core, prefix, ctx):
        self.nc, self.prefix, self.ctx, self.sems = core.nc, prefix, ctx, []

    def sb(self, name, shape, dtype=F32):
        return self.ctx.enter_context(self.nc.sbuf_tensor(f"{self.prefix}_{name}", shape, dtype))

    def sem(self, name):
        handle = self.nc.alloc_semaphore(name=f"{self.prefix}_{name}")
        self.sems.append(handle)
        return handle

    def free_semaphores(self):
        self.nc.clear_and_free_semaphores(self.sems)
        self.nc.all_engine_barrier()


class Space:

    def __init__(self, buffer):
        self.buffer, self.taken = buffer, 0

    def take(self, shape, dtype=F32, rows=P):
        start = self.taken
        self.taken += int(np.prod(shape)) // (1 if dtype == F32 else 2)
        part = self.buffer[0:rows, start:self.taken]
        if dtype != F32:
            part = part.bitcast(dtype)
        if len(shape) == 1:
            return part
        axes = "abcd"[:len(shape)]
        return part.rearrange(f"p ({' '.join(axes)}) -> p {' '.join(axes)}", **dict(zip(axes[1:], shape[1:])))


class Stats:

    def __init__(self, layer, name, with_shift=False):
        self.stats = layer.sb(f"{name}_stats", [P, T, 6])
        self.moments = layer.sb(f"{name}_moments", [P, T, 2])
        self.shifted = layer.sb(f"{name}_shifted", [P, T])
        self.rstd = layer.sb(f"{name}_rstd", [P, T])
        if with_shift:
            self.minus_mean = layer.sb(f"{name}_minus_mean", [P, T])
            self.shift = layer.sb(f"{name}_shift", [P, T])
        self.stats_done = layer.sem(f"{name}_stats_done")
        self.moments_done = layer.sem(f"{name}_moments_done")
        self.shifted_done = layer.sem(f"{name}_shifted_done")
        self.rstd_done = layer.sem(f"{name}_rstd_done")
        self.with_shift = with_shift
        if with_shift:
            self.shift_done = layer.sem(f"{name}_shift_done")


def take_moments(core, dve, st, src, b):
    nc = core.nc
    for t in range(T):
        nc.vector.bn_stats(st.stats[:, t, :], src(t)).then_inc(st.stats_done, 1)
    dve.wait_ge(st.stats_done, T * b + T)
    dve.sem_inc(core.tick, 1)
    for t in range(T):
        last = nc.vector.bn_aggr(st.moments[:, t, :], st.stats[:, t, :])
    last.then_inc(st.moments_done, 1)


def take_rstd(core, pool, st, b):
    nc = core.nc
    pool.wait_ge(st.moments_done, b + 1)
    nc.gpsimd.tensor_tensor(st.shifted[:, :], st.moments[:, :, 1], core.eps[:, :],
                            ALU.add).then_inc(st.shifted_done, 1)
    pool.wait_ge(st.shifted_done, 2 * b + 1 if st.with_shift else b + 1)
    nc.gpsimd.tensor_tensor(st.rstd[:, :], st.shifted[:, :], core.minus_half[:, :],
                            ALU.pow).then_inc(st.rstd_done, 1)


def take_shift(core, pool, st, b):
    nc = core.nc
    nc.gpsimd.tensor_tensor(st.minus_mean[:, :], st.moments[:, :, 0], core.minus_one[:, :],
                            ALU.mult).then_inc(st.shifted_done, 1)
    pool.wait_ge(st.shifted_done, 2 * b + 2)
    pool.wait_ge(st.rstd_done, b + 1)
    nc.gpsimd.tensor_tensor(st.shift[:, :], st.minus_mean[:, :], st.rstd[:, :],
                            ALU.mult).then_inc(st.shift_done, 1)


def normalize_act(nc, st, dst, src):
    for t in range(T):
        last = nc.scalar.activation(dst(t), src(t), ACT.Identity, bias=st.shift[:, t:t + 1],
                                    scale=st.rstd[:, t:t + 1])
    return last


def normalize(nc, st, dst, src):
    for t in range(T):
        last = nc.vector.tensor_scalar(dst(t), src(t), st.moments[:, t, 0:1], st.rstd[:, t:t + 1],
                                       ALU.subtract, ALU.mult)
    return last


def gated_attention(core):
    nc, dram, x, ps = core.nc, core.dram, core.x, core.ps
    with ExitStack() as ctx:
        L = Layer(core, "gau", ctx)
        w_hidden = L.sb("w_hidden", [P, 2 * HID])
        w_qk = L.sb("w_qk", [P, D])
        w_out = L.sb("w_out", [P, HID // P, D])
        keep, inv_pos = L.sb("keep", [P, N]), L.sb("inv_pos", [P, N])
        b_value = L.sb("b_value", [P, HID])
        b_out = L.sb("b_out", [P, D])
        per_feature = L.sb("per_feature", [P, 9])
        ln_g, ln_b, b_qk = (per_feature[:, i:i + 1] for i in range(3))
        b_gate, os_gamma, os_beta = (per_feature[:, i:i + 2] for i in (3, 5, 7))
        a = L.sb("a", [P, 2, T, D])
        a_bias = L.sb("a_bias", [P, 2, T, D])
        n2 = L.sb("n2", [P, T, D])
        nT = L.sb("nT", [P, N])
        value_pre = L.sb("value_pre", [P, T, HID])
        value = L.sb("value", [P, 2, T, HID])
        gateT = L.sb("gateT", [P, 2, 2, N])
        qk_act, q_aff = L.sb("qk_act", [P, N]), L.sb("q_aff", [P, N])
        qT, kT = L.sb("qT", [P, N]), L.sb("kT", [P, N])
        relu = L.sb("relu", [P, 3, N])
        prob = L.sb("prob", [P, 3, N])
        gatedT = L.sb("gatedT", [P, 2, N])
        y, z = L.sb("y", [P, T, D]), L.sb("z", [P, T, D])
        ln_x, ln_a, ln_y = Stats(L, "ln_x"), Stats(L, "ln_a"), Stats(L, "ln_y")

        weights_in = L.sem("weights_in")
        x_in = [L.sem("x_in_even"), L.sem("x_in_odd")]
        a_ok, n2_ok, a_bias_ok = L.sem("a_ok"), L.sem("n2_ok"), L.sem("a_bias_ok")
        nT_mm, nT_ok = L.sem("nT_mm"), L.sem("nT_ok")
        value_mm, value_pre_ok, value_ok = L.sem("value_mm"), L.sem("value_pre_ok"), L.sem("value_ok")
        gate_mm, gate_ok = L.sem("gate_mm"), L.sem("gate_ok")
        qk_mm, qk_act_ok, q_aff_ok, q_ok, k_ok = (L.sem("qk_mm"), L.sem("qk_act_ok"), L.sem("q_aff_ok"), L.sem("q_ok"),
                                                  L.sem("k_ok"))
        score_mm, relu_ok, prob_ok = L.sem("score_mm"), L.sem("relu_ok"), L.sem("prob_ok")
        attn_mm, gated_ok = L.sem("attn_mm"), L.sem("gated_ok")
        out_mm, y_ok, z_ok, x_ok = L.sem("out_mm"), L.sem("y_ok"), L.sem("z_ok"), L.sem("x_ok")

        BK_NT, BK_VALUE, BK_GATE, BK_SCORE = 0, 1, 3, 5
        BK_QK, BK_ATTN, BK_OUT = 0, 5, 7
        SCORES = ((0, 0, 0), (1, 1, 0), (3, 1, 3 * P), (2, 2, 0))

        def width(kt):
            return N - kt * P

        w_loads = [
            (core.ident[:, :], dram["ident"]),
            (w_hidden[:, :], dram["W_hidden"]), (w_qk[:, :], dram["W_qk"]),
            (w_out[:, :, :], dram["W_out"].rearrange("(j p) d -> p j d", p=P)),
            (keep[:, :], dram["keep"]), (inv_pos[:, :], dram["inv_pos"]),
            (b_value[:, :], dram["b_hidden"][0:HID].partition_broadcast(P)),
            (b_out[:, :], dram["b_out"].partition_broadcast(P)),
            (per_feature[:, :], dram["gau_vectors"]),
        ]
        W_IN = 16 * len(w_loads)

        with nc.Block() as block:
            @block.sync
            def _(sp):
                def load_x(b, u):
                    sp.dma_start(x[:, b, :, :], dram["x"][b].rearrange("(t p) d -> p t d", p=P)).then_inc(x_in[u], 16)

                load_x(0, 0)
                load_x(1, 1)
                for dst, src in w_loads:
                    sp.dma_start(dst, src).then_inc(weights_in, 16)
                core.load_weights(sp)
                with sp.Fori(1, B // 2) as pair:
                    for u in range(2):
                        sp.wait_ge(x_in[u], 16 * pair)
                        load_x(2 * pair + u, u)

            @block.vector
            def _(dve):
                nc.vector.memset(core.eps[:, :], EPS)
                nc.vector.memset(core.minus_half[:, :], -0.5)
                nc.vector.memset(core.minus_one[:, :], -1.0)

                def step(s, u):
                    h, g, f, p, gu, fu = s + 3, s + 2, s + 1, s - 1, u, 1 - u
                    if live(s):
                        for i, (kt, bank, at) in enumerate(SCORES):
                            dve.wait_ge(score_mm, 3 * s + bank + 1)
                            if i == 0:
                                upto(dve, prob_ok, 3 * s)
                            w = width(kt)
                            r = nc.vector.scalar_tensor_tensor(
                                relu[:, bank, at:at + w], ps[:, BK_SCORE + bank, at:at + w], 0.0, keep[:, 0:w],
                                ALU.max, ALU.mult)
                            if kt != 1:
                                r.then_inc(relu_ok, 1)
                    if live(g):
                        dve.wait_ge(ln_x.rstd_done, g + 1)
                        upto(dve, a_bias_ok, g - 1)
                        normalize(nc, ln_x, lambda t: a[:, gu, t, :], lambda t: x[:, g, t, :]).then_inc(a_ok, 1)
                    if live(p):
                        dve.wait_ge(ln_y.rstd_done, p + 1)
                        upto(dve, x_ok, p)
                        normalize(nc, ln_y, lambda t: z[:, t, :], lambda t: y[:, t, :]).then_inc(z_ok, 1)
                    if live(f):
                        dve.wait_ge(value_mm, f + 1)
                        upto(dve, value_ok, f)
                        for j in range(2):
                            last = nc.vector.tensor_tensor(
                                value_pre[:, 2 * j:2 * j + 2, :],
                                ps[:, BK_VALUE + j, :].rearrange("p (t h) -> p t h", t=2),
                                b_value[:, :].unsqueeze(1).broadcast_to([P, 2, HID]), ALU.add)
                        last.then_inc(value_pre_ok, 1)
                    if live(g):
                        dve.wait_ge(a_ok, g + 1)
                        take_moments(core, dve, ln_a, lambda t: a[:, gu, t, :], g)
                    if live(s):
                        dve.wait_ge(gate_ok, s + 1)
                        upto(dve, out_mm, s)
                        for j in range(2):
                            dve.wait_ge(attn_mm, 2 * s + j + 1)
                            nc.vector.tensor_tensor(gatedT[:, j, :], ps[:, BK_ATTN + j, :], gateT[:, u, j, :],
                                                    ALU.mult).then_inc(gated_ok, 1)
                    if live(g):
                        dve.wait_ge(ln_a.rstd_done, g + 1)
                        upto(dve, nT_mm, g)
                        normalize(nc, ln_a, lambda t: n2[:, t, :], lambda t: a[:, gu, t, :]).then_inc(n2_ok, 1)
                    if live(s):
                        dve.wait_ge(out_mm, s + 1)
                        dve.wait_ge(a_bias_ok, s + 1)
                        upto(dve, z_ok, s)
                        nc.vector.tensor_tensor(y[:, :, :], ps[:, BK_OUT, :].rearrange("p (t d) -> p t d", t=T),
                                                a_bias[:, u, :, :], ALU.add).then_inc(y_ok, 1)
                        dve.wait_ge(y_ok, s + 1)
                        take_moments(core, dve, ln_y, lambda t: y[:, t, :], s)

                    if live(h):
                        dve.wait_ge(x_in[1 - u], 16 + 8 * (h - (1 - u)))
                        take_moments(core, dve, ln_x, lambda t: x[:, h, t, :], h)

                step(-3, 1)
                step(-2, 0)
                dve.wait_ge(weights_in, W_IN)
                nc.vector.tensor_copy(core.ident_bf[:, :], core.ident[:, :])
                run_steps(dve, step, -1, 3, 11, B + 1)

            @block.gpsimd
            def _(pool):
                def step(s, u):
                    h, g, f, p, fu = s + 3, s + 2, s + 1, s - 1, 1 - u
                    if live(f):
                        pool.wait_ge(a_ok, f + 1)
                        upto(pool, y_ok, f - 1)
                        nc.gpsimd.tensor_tensor(
                            a_bias[:, fu, :, :], a[:, fu, :, :], b_out[:, :].unsqueeze(1).broadcast_to([P, T, D]),
                            ALU.add).then_inc(a_bias_ok, 1)
                    if live(g):
                        take_rstd(core, pool, ln_a, g)
                    if live(f):
                        pool.wait_ge(q_aff_ok, f + 1)
                        upto(pool, score_mm, 3 * f)
                        nc.gpsimd.tensor_tensor(qT[:, :], q_aff[:, :], inv_pos[:, :], ALU.mult).then_inc(q_ok, 1)
                    if live(p):
                        pool.wait_ge(z_ok, p + 1)
                        pool.sem_inc(core.tick, 1)
                        nc.gpsimd.tensor_tensor(x[:, p, :, :], x[:, p, :, :], z[:, :, :], ALU.add).then_inc(x_ok, 1)
                    if live(s):
                        take_rstd(core, pool, ln_y, s)
                    if live(h):
                        take_rstd(core, pool, ln_x, h)

                step(-3, 1)
                step(-2, 0)
                pool.wait_ge(weights_in, W_IN)
                run_steps(pool, step, -1, 3, 11, B + 1)

            @block.scalar
            def _(act):
                act.wait_ge(weights_in, W_IN)

                def step(s, u):
                    f, fu = s + 1, 1 - u
                    if live(f):
                        act.wait_ge(nT_mm, f + 1)
                        nc.scalar.activation(nT[:, :], ps[:, BK_NT, :], ACT.Identity, bias=ln_b,
                                             scale=ln_g).then_inc(nT_ok, 1)
                    if live(s):
                        upto(act, attn_mm, 2 * s)
                        for bank, w in ((0, N), (1, N), (2, width(2))):
                            act.wait_ge(relu_ok, 3 * s + bank + 1)
                            nc.scalar.activation(prob[:, bank, 0:w], relu[:, bank, 0:w],
                                                 ACT.Square).then_inc(prob_ok, 1)
                    if live(f):
                        act.wait_ge(qk_mm, f + 1)
                        upto(act, q_aff_ok, f)
                        upto(act, k_ok, f)
                        nc.scalar.activation(qk_act[:, :], ps[:, BK_QK, :], ACT.Silu,
                                             bias=b_qk).then_inc(qk_act_ok, 1)
                        act.wait_ge(qk_act_ok, f + 1)
                        upto(act, q_ok, f)
                        nc.scalar.activation(q_aff[:, :], qk_act[:, :], ACT.Identity, bias=os_beta[:, 0:1],
                                             scale=os_gamma[:, 0:1]).then_inc(q_aff_ok, 1)
                        upto(act, score_mm, 3 * f)
                        nc.scalar.activation(kT[:, :], qk_act[:, :], ACT.Identity, bias=os_beta[:, 1:2],
                                             scale=os_gamma[:, 1:2]).then_inc(k_ok, 1)
                    if live(f):
                        act.wait_ge(value_pre_ok, f + 1)
                        upto(act, attn_mm, 2 * (f - 1))
                        nc.scalar.activation(value[:, fu, :, :], value_pre[:, :, :], ACT.Silu).then_inc(value_ok, 1)
                        upto(act, gated_ok, 2 * (f - 1))
                        act.wait_ge(gate_mm, f + 1)
                        for j in range(2):
                            last = nc.scalar.activation(gateT[:, fu, j, :], ps[:, BK_GATE + j, :], ACT.Silu,
                                                        bias=b_gate[:, j:j + 1])
                        last.then_inc(gate_ok, 1)

                run_steps(act, step, -2, 1, 13, B)

            @block.tensor
            def _(pe):
                pe.wait_ge(weights_in, W_IN)

                def step(s, u):
                    f, fu = s + 1, 1 - u
                    if live(f):
                        pe.wait_ge(n2_ok, f + 1)
                        upto(pe, qk_act_ok, f)
                        for t in range(T):
                            last = nc.tensor.transpose(ps[:, BK_NT, t * P:t * P + P], n2[:, t, :], core.ident[:, :])
                        last.then_inc(nT_mm, 1)
                    if live(s):
                        pe.wait_ge(q_ok, s + 1)
                        pe.wait_ge(k_ok, s + 1)
                        upto(pe, gated_ok, 2 * s)
                        for kt, bank, at in SCORES:
                            if kt == 2:
                                upto(pe, y_ok, s)
                            last = nc.tensor.matmul(ps[:, BK_SCORE + bank, at:at + width(kt)],
                                                    kT[:, kt * P:kt * P + P], qT[:, kt * P:N], start=True, stop=True)
                            if kt != 1:
                                last.then_inc(score_mm, 1)
                    if live(f):
                        pe.wait_ge(nT_ok, f + 1)
                        nc.tensor.matmul(ps[:, BK_QK, :], w_qk[:, :], nT[:, :], start=True,
                                         stop=True).then_inc(qk_mm, 1)
                        upto(pe, value_pre_ok, f)
                        for t in range(T):
                            last = nc.tensor.matmul(ps[:, BK_VALUE + t // 2, t % 2 * HID:t % 2 * HID + HID],
                                                    nT[:, t * P:t * P + P], w_hidden[:, 0:HID], start=True, stop=True)
                        last.then_inc(value_mm, 1)
                        upto(pe, gate_ok, f)
                        for j in range(2):
                            last = nc.tensor.matmul(ps[:, BK_GATE + j, :], w_hidden[:, HID + j * P:HID + j * P + P],
                                                    nT[:, :], start=True, stop=True)
                        last.then_inc(gate_mm, 1)
                    if live(s):
                        pe.wait_ge(value_ok, s + 1)
                        pe.wait_ge(prob_ok, 3 * s + 3)
                        for j in range(2):
                            for i, (kt, bank, at) in enumerate(SCORES):
                                last = nc.tensor.matmul(ps[:, BK_ATTN + j, kt * P:N],
                                                        value[:, u, kt, j * P:j * P + P],
                                                        prob[:, bank, at:at + width(kt)], start=i == 0, stop=i == T - 1)
                            last.then_inc(attn_mm, 1)
                    if live(s):
                        for j in range(2):
                            pe.wait_ge(gated_ok, 2 * s + j + 1)
                            for t in range(T):
                                last = nc.tensor.matmul(ps[:, BK_OUT, t * D:t * D + D],
                                                        gatedT[:, j, t * P:t * P + P], w_out[:, j, :],
                                                        start=j == 0 and t == 0, stop=j == 1,
                                                        skip_group_check=True)
                        last.then_inc(out_mm, 1)

                run_steps(pe, step, -2, 1, 13, B)
        L.free_semaphores()


SHARED_FROM = B - 7


class MixPrograms:

    def __init__(self, vector, gpsimd, scalar, tensor, x_ok, z_ok, y_ok, r_ok, relu_ok, aT_ok):
        self.vector, self.gpsimd, self.scalar, self.tensor = vector, gpsimd, scalar, tensor
        self.x_ok, self.z_ok, self.y_ok = x_ok, z_ok, y_ok
        self.r_ok, self.relu_ok, self.aT_ok = r_ok, relu_ok, aT_ok


def channel_mix(core, ctx, space, z):
    nc, dram, x, ps = core.nc, core.dram, core.x, core.ps
    L = Layer(core, "mix", ctx)
    w_r, w_k, w_v, mu = (core.weights[name] for name in ("W_r_T", "W_k_T", "W_v_T", "mix_vectors"))
    w_k_now, w_k_prev, w_r_now, w_r_prev = (space.take([D]) for _ in range(4))
    a = space.take([T, D])
    aT = space.take([2, 1 + N])
    r = space.take([2, T, D])
    relu_k, k_act = space.take([N]), space.take([N])
    y = space.take([T, D])
    ln_x, ln_y = Stats(L, "ln_x", with_shift=True), Stats(L, "ln_y")
    now_ok, weights_ok = L.sem("now_ok"), L.sem("weights_ok")
    a_ok, aT_mm, aT_ok = L.sem("a_ok"), L.sem("aT_mm"), L.sem("aT_ok")
    k_mm, r_mm, r_ok, relu_ok, k_act_ok = (L.sem("k_mm"), L.sem("r_mm"), L.sem("r_ok"), L.sem("relu_ok"),
                                           L.sem("k_act_ok"))
    out_mm, y_ok, z_ok, x_ok = L.sem("out_mm"), L.sem("y_ok"), L.sem("z_ok"), L.sem("x_ok")
    BK_AT, BK_K, BK_R, BK_OUT = 0, 1, 2, 3

    def vector(dve):
        def step(s, u):
            m, p = s + 3, s - 1
            if live(p):
                dve.wait_ge(ln_y.rstd_done, p + 1)
                upto(dve, x_ok, p)
                normalize(nc, ln_y, lambda t: z[:, t, :], lambda t: y[:, t, :]).then_inc(z_ok, 1)
            if live(s):
                dve.wait_ge(out_mm, s + 1)
                dve.wait_ge(r_ok, s + 1)
                upto(dve, z_ok, s)
                nc.vector.tensor_tensor(y[:, :, :], ps[:, BK_OUT, :].rearrange("p (t d) -> p t d", t=T),
                                        r[:, u, :, :], ALU.mult).then_inc(y_ok, 1)
                dve.wait_ge(y_ok, s + 1)
                take_moments(core, dve, ln_y, lambda t: y[:, t, :], s)
            if live(m):
                upto(dve, ln_x.shift_done, m)
                take_moments(core, dve, ln_x, lambda t: x[:, m, t, :], m)

        core.wait_weights(dve)
        step(-3, 1)
        for u in range(2):
            nc.vector.memset(aT[:, u, 0:1], 0.0)
        for w, now, i in ((w_r, w_r_now, 0), (w_k, w_k_now, 1)):
            nc.vector.tensor_scalar(now[:, :], w[:, :], mu[:, i:i + 1], None, ALU.mult).then_inc(now_ok, 1)
        dve.wait_ge(now_ok, 2)
        nc.vector.tensor_tensor(w_r_prev[:, :], w_r[:, :], w_r_now[:, :], ALU.subtract)
        nc.vector.tensor_tensor(w_k_prev[:, :], w_k[:, :], w_k_now[:, :],
                                ALU.subtract).then_inc(weights_ok, 1)
        run_steps(dve, step, -2, 3, SHARED_FROM, SHARED_FROM)
        return step

    def gpsimd(pool):
        def step(s, u):
            h, p = s + 2, s - 1
            if live(h):
                upto(pool, a_ok, h)
                take_rstd(core, pool, ln_x, h)
                take_shift(core, pool, ln_x, h)
            if live(p):
                pool.wait_ge(z_ok, p + 1)
                pool.sem_inc(core.tick, 1)
                nc.gpsimd.tensor_tensor(x[:, p, :, :], x[:, p, :, :], z[:, :, :], ALU.add).then_inc(x_ok, 1)
            if live(s):
                take_rstd(core, pool, ln_y, s)

        run_steps(pool, step, -2, 3, SHARED_FROM, SHARED_FROM)
        return step

    def scalar(act):
        def step(s, u):
            h, f = s + 2, s + 1
            if live(f):
                act.wait_ge(aT_mm, f + 1)
                upto(act, r_mm, f - 1)
                nc.scalar.copy(aT[:, 1 - u, 1:1 + N], ps[:, BK_AT, :]).then_inc(aT_ok, 1)
            if live(h):
                act.wait_ge(ln_x.shift_done, h + 1)
                upto(act, aT_mm, h)
                normalize_act(nc, ln_x, lambda t: a[:, t, :], lambda t: x[:, h, t, :]).then_inc(a_ok, 1)
            if live(f):
                act.wait_ge(k_mm, f + 1)
                upto(act, k_act_ok, f)
                nc.scalar.activation(relu_k[:, :], ps[:, BK_K, :], ACT.Relu).then_inc(relu_ok, 1)
                act.wait_ge(relu_ok, f + 1)
                upto(act, out_mm, f)
                nc.scalar.activation(k_act[:, :], relu_k[:, :], ACT.Square).then_inc(k_act_ok, 1)
                act.wait_ge(r_mm, f + 1)
                upto(act, y_ok, f - 1)
                nc.scalar.activation(r[:, 1 - u, :, :], ps[:, BK_R, :].rearrange("p (t d) -> p t d", t=T),
                                     ACT.Sigmoid).then_inc(r_ok, 1)

        run_steps(act, step, -2, 3, SHARED_FROM, SHARED_FROM)
        return step

    def tensor(pe):
        def step(s, u):
            h, f, fu = s + 2, s + 1, 1 - u
            if live(s):
                pe.wait_ge(k_act_ok, s + 1)
                upto(pe, y_ok, s)
                for t in range(T):
                    last = nc.tensor.matmul(ps[:, BK_OUT, t * D:t * D + D], k_act[:, t * P:t * P + P],
                                            w_v[:, :], start=True, stop=True)
                last.then_inc(out_mm, 1)
            if live(f):
                pe.wait_ge(aT_ok, f + 1)
                upto(pe, relu_ok, f)
                nc.tensor.matmul(ps[:, BK_K, :], w_k_now[:, :], aT[:, fu, 1:1 + N], start=True, stop=False)
                nc.tensor.matmul(ps[:, BK_K, :], w_k_prev[:, :], aT[:, fu, 0:N], start=False,
                                 stop=True).then_inc(k_mm, 1)
            if live(h):
                pe.wait_ge(a_ok, h + 1)
                upto(pe, aT_ok, h)
                for t in range(T):
                    last = nc.tensor.transpose(ps[:, BK_AT, t * P:t * P + P], a[:, t, :], core.ident[:, :])
                last.then_inc(aT_mm, 1)
            if live(f):
                upto(pe, r_ok, f)
                for t in range(T):
                    for lhs, rhs, first in ((1, w_r_now, True), (0, w_r_prev, False)):
                        last = nc.tensor.matmul(ps[:, BK_R, t * D:t * D + D],
                                                aT[:, fu, lhs + t * P:lhs + t * P + P], rhs[:, :],
                                                start=first, stop=not first)
                last.then_inc(r_mm, 1)

        step(-2, 0)
        pe.wait_ge(weights_ok, 1)
        run_steps(pe, step, -1, 3, SHARED_FROM, SHARED_FROM)
        return step

    return MixPrograms(vector, gpsimd, scalar, tensor, x_ok, z_ok, y_ok, r_ok, relu_ok, aT_ok)


def finish_mix(mix_step, step):
    mix_step(SHARED_FROM, 1)
    step(FIRST_STEP, 1)
    cuts = (0, 3, 5, 8, 10, 12, SLOTS)
    for i, (start, end) in enumerate(zip(cuts, cuts[1:])):
        mix_step(SHARED_FROM + 1 + i, i % 2)
        step(FIRST_STEP + 1, 0, range(start, end))
    mix_step(B, 0)


SLOTS = 20
GROUPS, GH = 4, 4
SHARED = ((0, "aT", 2), (1, "top_late", 0), (2, "q", 2), (3, "natural_late", -1), (5, "oT", -1), (6, "k", 2),
          (8, "out", -1), (9, "natural_0", 0), (11, "v", 1), (13, "natural_1", 0), (15, "top_early", 1),
          (18, "natural_2", 0))
FIRST_STEP = -3


def shared_user_before(s, task):
    uses = [(s + back + ahead, name) for back in (-1, 0) for _, name, ahead in SHARED]
    at = len(SHARED) + [name for _, name, _ in SHARED].index(task)
    earlier = [(name, b) for b, name in uses[:at] if live(b)]
    return earlier[-1] if earlier else None


def top_unit_parts(n, i):
    half, j = divmod(n, SLOTS // 2)
    h = half * HH
    if j < 4:
        return [(3, h + 2 * j + i, 0)], (3 * P, 1)
    if j < 8:
        h += 2 * (j - 4) + i
        return [(2, h, 0), (0, h, 3 * P)], (2 * P, 2)
    h += 4 * (j - 8) + 2 * i
    return [(1, h, 0), (1, h + 1, 2 * P)], (P, 2)


def causal_attention(core):
    nc, dram, x, ps = core.nc, core.dram, core.x, core.ps
    with ExitStack() as ctx:
        L = Layer(core, "att", ctx)
        w_q, w_k, w_v, w_o = (core.weights[name] for name in ATT_WEIGHTS)
        cos, sin, future = (core.weights[name] for name in ("cos", "sin", "future"))
        future_bf = L.sb("future_bf", [P, 2, P], BF16)
        prep, stacks = L.sb("prep", [P, 12 * N]), L.sb("stacks", [P, 2 * NH * N])
        space = Space(prep)
        a, aT = space.take([T, D]), space.take([2, N])
        by_cos, by_sin = space.take([N]), space.take([N])
        by_sin_turned = space.take([N])
        full, rest = space.take([N]), space.take([N])
        q_parts, k_parts = space.take([3, N], BF16), space.take([3, N], BF16)
        space = Space(stacks)
        q_stack, k_stack = space.take([2, NH, N], BF16, KM), space.take([2, NH, N], BF16, KM)
        ones = L.sb("ones", [2, N], BF16)
        v = L.sb("v", [P, 2, T, NH, 32])
        top = L.sb("top", [P, T, NH])
        top_parts = L.sb("top_parts", [P, 2, T, 2, HH], BF16)
        top_row = L.sb("top_row", [2 * HH, N], BF16)
        e = L.sb("e", [P, 5, 2 * N])
        oT = L.sb("o_groupT", [P, N])
        o_rsum = L.sb("o_rsum", [P, T, GH])
        o, o_T = L.sb("o", [P, T, NH, DH]), L.sb("o_T", [P, N])
        y, z = L.sb("y", [P, T, D]), L.sb("z", [P, T, D])
        ln_x, ln_y = Stats(L, "ln_x"), Stats(L, "ln_y")
        mix = channel_mix(core, ctx, Space(e[:, :, :].rearrange("p j c -> p (j c)")),
                          o[:, :, :, :].rearrange("p t h d -> p t (h d)"))

        made, ones_in = L.sem("made"), L.sem("ones_in")
        v_made = L.sem("v_made")
        a_ok, aT_mm, aT_ok = L.sem("a_ok"), L.sem("aT_mm"), L.sem("aT_ok")
        qk_mm, turned_in = L.sem("qk_mm"), L.sem("turned_in")
        rope_ok, full_ok, rest_ok, part_ok = L.sem("rope_ok"), L.sem("full_ok"), L.sem("rest_ok"), L.sem("part_ok")
        rest_last_ok = L.sem("rest_last_ok")
        stack_in = [L.sem("stack_in_early"), L.sem("stack_in_late")]
        v_mm, v_ok = L.sem("v_mm"), L.sem("v_ok")
        top_mm, top_ok, hi_ok, parts_ok = L.sem("top_mm"), L.sem("top_ok"), L.sem("hi_ok"), L.sem("parts_ok")
        row_mm, row_ok, row_in = L.sem("row_mm"), L.sem("row_ok"), L.sem("row_in")
        score_mm, exp_ok, causal_ok = L.sem("score_mm"), L.sem("exp_ok"), L.sem("causal_ok")
        attn_mm, oT_ok = L.sem("attn_mm"), L.sem("oT_ok")
        natural_mm, rsum_ok, o_ok = L.sem("natural_mm"), L.sem("rsum_ok"), L.sem("o_ok")
        o_T_mm, o_T_ok, out_mm, y_ok, z_ok, x_ok = (L.sem("o_T_mm"), L.sem("o_T_ok"), L.sem("out_mm"), L.sem("y_ok"),
                                                    L.sem("z_ok"), L.sem("x_ok"))

        BK_SCORE, BK_TOP, BK_ATTN, BK_SHARED = 0, 2, 6, 7
        shared = ps[:, BK_SHARED, :]
        shared_td = shared.rearrange("p (t d) -> p t d", t=T)
        shared_bf = shared.bitcast(BF16)
        STACK_IN = 16 * 2 * len(PARTS_Q)

        def e_heads(j):
            return e[:, j, :].rearrange("p (h c) -> p h c", h=2 if j < 4 else 4)

        def prep_free(engine):
            engine.wait_ge(v_mm, B)
            for half in range(2):
                engine.wait_ge(stack_in[half], STACK_IN * B)
            engine.wait_ge(top_ok, SLOTS * B)

        def stacks_free(engine):
            engine.wait_ge(score_mm, 2 * SLOTS * B)

        def banks_free(pe):
            pe.wait_ge(exp_ok, 2 * SLOTS * B)
            pe.wait_ge(oT_ok, GROUPS * B)
            pe.wait_ge(y_ok, B)

        UNIT = ((0, (0, 1)), (0, (2, 3)), (1, (0, 1)), (1, (2, 3)), (2, (0, 1, 2, 3)))

        moe = soft_mixture(core, ctx, Space(prep), Space(stacks), prep_free, stacks_free, banks_free)

        with nc.Block() as block:
            @block.sync
            def _(sp):
                def load_top_row(b, half, u):
                    sp.wait_ge(row_ok, 2 * b + half + 1)
                    sp.dma_start(q_stack[KS:KM, u, half * HH:half * HH + HH, :],
                                 top_row[:, :]).then_inc(row_in, 16)

                def turn(g, w):
                    sp.wait_ge(rope_ok, 4 * g + 2 * w + 2)
                    size = HH * DH // 2
                    for to, start in ((0, 1), (1, 0), (2, 3), (3, 2)):
                        sp.dma_start(by_sin_turned[to * size:(to + 1) * size, :],
                                     by_sin[start * size:(start + 1) * size, :]).then_inc(turned_in, 16)

                def load_stacks(g, half, u):
                    for w, (stack, source, which) in enumerate(((q_stack, q_parts, PARTS_Q),
                                                                (k_stack, k_parts, PARTS_K))):
                        sp.wait_ge(rest_last_ok, 2 * g + w + 1)
                        for c, part in enumerate(which):
                            sp.dma_start(stack[c * DH:c * DH + DH, u, half * HH:half * HH + HH, :],
                                         source[half * DH * HH:half * DH * HH + DH * HH, part, :],
                                         ).then_inc(stack_in[half], 16)

                def step(s, u, slots=range(SLOTS)):
                    g, m = s + 2, s + 1
                    if live(s):
                        load_top_row(s, 1, u)
                    if live(g):
                        turn(g, 0)
                        turn(g, 1)
                    if live(s):
                        sp.wait_ge(score_mm, SLOTS * (2 * s + 1))
                    if live(g):
                        load_stacks(g, 0, u)
                    if live(m):
                        load_top_row(m, 0, 1 - u)
                    if live(g):
                        if live(s):
                            sp.wait_ge(score_mm, SLOTS * (2 * s + 2))
                        load_stacks(g, 1, u)

                sp.wait_ge(made, 1)
                sp.dma_start(k_stack[KS:KM, :, :, :].rearrange("r u h n -> r (u h) n"),
                             ones[:, :].unsqueeze(1).broadcast_to([2, 2 * NH, N])).then_inc(ones_in, 16)
                run_steps(sp, step, FIRST_STEP, 3, 13, B)
                moe.sync(sp)

            @block.vector
            def _(dve):
                def reduce_unit(m, n):
                    dve.wait_ge(top_mm, SLOTS * m + n + 1)
                    banks = ps[:, BK_TOP + n % 2 * 2:BK_TOP + n % 2 * 2 + 2, :]
                    (qt, h, _), *more = top_unit_parts(n, 0)[0]
                    if qt == 3:
                        r = nc.vector.reduce_max(top[:, 3, h:h + 2], banks, AXX)
                    elif qt == 2:
                        nc.vector.reduce_max(top[:, 2, h:h + 2], banks[:, :, 0:3 * P], AXX)
                        r = nc.vector.reduce_max(top[:, 0, h:h + 2], banks[:, :, 3 * P:N], AXX)
                    else:
                        r = nc.vector.reduce_max(top[:, 1, h:h + 4], banks.rearrange("p i (h c) -> p (i h) c", h=2),
                                                 AXX)
                    r.then_inc(top_ok, 1)

                def split_top(m, half):
                    k = 2 * m + half
                    dve.wait_ge(top_ok, SLOTS * m + SLOTS // 2 * (half + 1))
                    upto(dve, row_mm, k - 1)
                    src = top[:, :, half * HH:half * HH + HH]
                    nc.vector.tensor_scalar(top_parts[:, half, :, 0, :], src, -1.0, None, ALU.mult).then_inc(hi_ok, 1)
                    dve.wait_ge(hi_ok, k + 1)
                    nc.vector.scalar_tensor_tensor(top_parts[:, half, :, 1, :], src, -1.0,
                                                   top_parts[:, half, :, 0, :], ALU.mult,
                                                   ALU.subtract).then_inc(parts_ok, 1)

                def rotate(g, w):
                    k = 2 * g + w
                    dve.wait_ge(qk_mm, k + 1)
                    upto(dve, full_ok, k)
                    nc.vector.tensor_tensor(by_cos[:, :], shared, cos[:, :], ALU.mult).then_inc(rope_ok, 1)
                    upto(dve, turned_in, 64 * k)
                    nc.vector.tensor_tensor(by_sin[:, :], shared, sin[:, :], ALU.mult).then_inc(rope_ok, 1)

                def normal_group(b, group):
                    k = GROUPS * b + group
                    dve.wait_ge(natural_mm, k + 1)
                    heads = shared.rearrange("p (t h c) -> p t h c", t=T, h=GH)
                    nc.vector.reciprocal(o_rsum[:, :, :], heads[:, :, :, DH]).then_inc(rsum_ok, 1)
                    dve.wait_ge(rsum_ok, k + 1)
                    if group == 0:
                        upto(dve, o_T_mm, b)
                    nc.vector.tensor_tensor(o[:, :, group * GH:group * GH + GH, :], heads[:, :, :, 0:DH],
                                            o_rsum[:, :, :].unsqueeze(3).broadcast_to([P, T, GH, DH]),
                                            ALU.mult).then_inc(o_ok, 1)

                def step(s, u, slots=range(SLOTS)):
                    l, g, m, p = s + 3, s + 2, s + 1, s - 1
                    for n in slots:
                        if live(m):
                            reduce_unit(m, n)
                        for w, slot in enumerate((2, 6)):
                            if live(g) and n == slot:
                                rotate(g, w)
                        if live(p) and n == 3:
                            normal_group(p, 3)
                        for group, slot in enumerate((9, 13, 18)):
                            if live(s) and n == slot:
                                normal_group(s, group)
                        if live(p) and n == 10:
                            dve.wait_ge(y_ok, p + 1)
                            take_moments(core, dve, ln_y, lambda t: y[:, t, :], p)
                        if live(m) and n == 11:
                            split_top(m, 0)
                        if live(p) and n == 14:
                            dve.wait_ge(ln_y.rstd_done, p + 1)
                            upto(dve, x_ok, p)
                            normalize(nc, ln_y, lambda t: z[:, t, :], lambda t: y[:, t, :]).then_inc(z_ok, 1)
                        if live(l) and n == 12:
                            dve.wait_ge(mix.x_ok, l + 1)
                            take_moments(core, dve, ln_x, lambda t: x[:, l, t, :], l)
                        if live(l) and n == 16:
                            dve.wait_ge(ln_x.rstd_done, l + 1)
                            upto(dve, aT_mm, l)
                            normalize(nc, ln_x, lambda t: a[:, t, :], lambda t: x[:, l, t, :]).then_inc(a_ok, 1)
                    if live(m):
                        split_top(m, 1)

                nc.vector.memset(ones[:, :], 1.0).then_inc(made, 1)
                finish_mix(mix.vector(dve), step)
                nc.vector.tensor_copy(future_bf[:, :, :], future[:, :].rearrange("p (i c) -> p i c",
                                                                                i=2)).then_inc(made, 1)
                step(-1, 1)
                dve.wait_ge(mix.x_ok, B)
                run_steps(dve, step, 0, 3, 13, B - 1)
                finish_attention(step, *moe.vector(dve, x_ok))

            @block.gpsimd
            def _(pool):
                def add_rotated(g, w):
                    k = 2 * g + w
                    pool.wait_ge(rope_ok, 4 * g + 2 * w + 1)
                    pool.wait_ge(turned_in, 64 * (k + 1))
                    upto(pool, rest_ok, k)
                    nc.gpsimd.tensor_tensor(full[:, :], by_cos[:, :], by_sin_turned[:, :],
                                            ALU.add).then_inc(full_ok, 1)

                def take_rest(g, w, part):
                    k = 2 * g + w
                    parts = (q_parts, k_parts)[w]
                    pool.wait_ge(part_ok, 2 * k + part + 1)
                    if part == 0:
                        upto(pool, rest_last_ok, k)
                        nc.gpsimd.tensor_tensor(rest[:, :], full[:, :], parts[:, 0, :],
                                                ALU.subtract).then_inc(rest_ok, 1)
                    else:
                        pool.wait_ge(rest_ok, k + 1)
                        if w == 0:
                            for half in range(2):
                                upto(pool, stack_in[half], STACK_IN * g)
                        nc.gpsimd.tensor_tensor(parts[:, 2, :], rest[:, :], parts[:, 1, :],
                                                ALU.subtract).then_inc(rest_last_ok, 1)

                def keep_causal(s, n):
                    j = n % 5
                    pool.wait_ge(exp_ok, 2 * SLOTS * s + 2 * n + 2)
                    pool.sem_inc(core.tick, 1)
                    if j in (2, 3):
                        blocks = e_heads(j)[:, :, 0:2 * P]
                        pattern = [[0, 2], [0, 2], [1, P]]
                    else:
                        blocks = e_heads(j)[:, :, 0:P]
                        pattern = [[0, 2 if j < 4 else 4], [1, P]]
                    nc.gpsimd.affine_select(blocks, blocks, pattern, ALU.is_ge, 0.0, 0, -1).then_inc(causal_ok, 1)

                def step(s, u, slots=range(SLOTS)):
                    l, g, p = s + 3, s + 2, s - 1
                    for n in slots:
                        if live(s):
                            keep_causal(s, n)
                        if live(g):
                            for w, slot in ((0, 5), (1, 10)):
                                if n == slot:
                                    add_rotated(g, w)
                                if n == slot + 1:
                                    take_rest(g, w, 0)
                                if n == slot + 3:
                                    take_rest(g, w, 1)
                        if live(p) and n == 12:
                            take_rstd(core, pool, ln_y, p)
                        if live(p) and n == 16:
                            pool.wait_ge(z_ok, p + 1)
                            pool.sem_inc(core.tick, 1)
                            nc.gpsimd.tensor_tensor(x[:, p, :, :], x[:, p, :, :], z[:, :, :],
                                                    ALU.add).then_inc(x_ok, 1)
                        if live(l) and n == 14:
                            take_rstd(core, pool, ln_x, l)

                finish_mix(mix.gpsimd(pool), step)
                nc.gpsimd.memset(v[:, :, :, :, DH:DH + 1], 1.0).then_inc(v_made, 1)
                nc.gpsimd.memset(v[:, :, :, :, DH + 1:32], 0.0).then_inc(v_made, 1)
                run_steps(pool, step, -1, 3, 13, B - 1)
                finish_attention(step, *moe.gpsimd(pool))

            @block.scalar
            def _(act):
                def exp_unit(s, n):
                    group, j = divmod(n, 5)
                    k = GROUPS * s + group
                    upto(act, attn_mm, 3 * (k - 1) + (1, 1, 2, 2, 3)[j])
                    for i in range(2):
                        act.wait_ge(score_mm, 2 * SLOTS * s + 2 * n + i + 1)
                        nc.scalar.activation(e[:, j, i * N:i * N + N], ps[:, BK_SCORE + i, :], ACT.Exp,
                                             scale=DH ** -0.5).then_inc(exp_ok, 1)

                def take_part(g, w, part):
                    k = 2 * g + w
                    act.wait_ge((full_ok, rest_ok)[part], k + 1)
                    if part == 0 and w == 0:
                        for half in range(2):
                            upto(act, stack_in[half], STACK_IN * g)
                    nc.scalar.copy((q_parts, k_parts)[w][:, part, :],
                                   (full, rest)[part][:, :]).then_inc(part_ok, 1)

                def take_group(s, group):
                    k = GROUPS * s + group
                    act.wait_ge(attn_mm, 3 * k + 3)
                    upto(act, natural_mm, k)
                    nc.scalar.copy(oT[:, :], ps[:, BK_ATTN, :]).then_inc(oT_ok, 1)

                def take_top_rows(b, half):
                    k = 2 * b + half
                    act.wait_ge(row_mm, k + 1)
                    upto(act, row_in, 16 * k)
                    nc.scalar.copy(top_row[:, :], shared_bf[0:2 * HH, 0:N]).then_inc(row_ok, 1)

                def step(s, u, slots=range(SLOTS)):
                    g, m, p = s + 2, s + 1, s - 1
                    for n in slots:
                        if live(s):
                            exp_unit(s, n)
                        if live(g) and n == 0:
                            act.wait_ge(aT_mm, g + 1)
                            upto(act, v_mm, g - 1)
                            nc.scalar.copy(aT[:, u, :], shared).then_inc(aT_ok, 1)
                        for w, slots in ((0, (6, 8)), (1, (11, 13))):
                            if live(g) and n in slots:
                                take_part(g, w, slots.index(n))
                        if live(s) and n == 1:
                            take_top_rows(s, 1)
                        if live(p) and n == 1:
                            take_group(p, 3)
                        if live(p) and n == 5:
                            act.wait_ge(o_T_mm, p + 1)
                            upto(act, out_mm, p)
                            nc.scalar.copy(o_T[:, :], shared).then_inc(o_T_ok, 1)
                        for group, slot in enumerate((6, 11, 16)):
                            if live(s) and n == slot:
                                take_group(s, group)
                        if live(p) and n == 8:
                            act.wait_ge(out_mm, p + 1)
                            upto(act, z_ok, p)
                            nc.scalar.copy(y[:, :, :], shared_td).then_inc(y_ok, 1)
                        if live(m) and n == 11:
                            act.wait_ge(v_mm, m + 1)
                            upto(act, attn_mm, 3 * GROUPS * (m - 1))
                            nc.scalar.copy(v[:, 1 - u, :, :, 0:DH], shared.rearrange(
                                "p (t h d) -> p t h d", t=T, h=NH)).then_inc(v_ok, 1)
                        if live(m) and n == 15:
                            take_top_rows(m, 0)

                finish_mix(mix.scalar(act), step)
                step(-1, 1)
                act.wait_ge(mix.z_ok, B)
                run_steps(act, step, 0, 3, 13, B - 1)
                finish_attention(step, *moe.scalar(act))

            @block.tensor
            def _(pe):
                def score_unit(s, n, i, u):
                    group, j = divmod(n, 5)
                    if n % (SLOTS // 2) == 0 and i == 0:
                        pe.wait_ge(row_in, 16 * (2 * s + n // (SLOTS // 2) + 1))
                    upto(pe, exp_ok, 2 * SLOTS * s + 2 * n + i - 1)
                    kt, heads = UNIT[j]
                    for k, h in enumerate(heads[len(heads) // 2 * i:len(heads) // 2 * (i + 1)]):
                        head = group * GH + h
                        for tile, c in ((3, 0), (1, P)) if kt == 1 else ((kt, 2 * P * k),):
                            last = nc.tensor.matmul(
                                ps[:, BK_SCORE + i, c:c + N - tile * P],
                                k_stack[:, u, head, tile * P:tile * P + P], q_stack[:, u, head, tile * P:N],
                                start=True, stop=True)
                    last.then_inc(score_mm, 1)

                def top_unit(m, n, i, u):
                    if n % (SLOTS // 2) == 0 and i == 0:
                        pe.wait_ge(stack_in[n // (SLOTS // 2)], STACK_IN * (m + 1))
                    if i == 0:
                        upto(pe, top_ok, SLOTS * m + n - 1)
                    bank = ps[:, BK_TOP + n % 2 * 2 + i, :]
                    parts, (mask_at, masks) = top_unit_parts(n, i)
                    for j, (qt, head, c) in enumerate(parts):
                        nc.tensor.matmul(bank[:, c:c + (qt + 1) * P], q_stack[0:KS, u, head, qt * P:qt * P + P],
                                         k_stack[0:KS, u, head, 0:(qt + 1) * P], start=j == 0, stop=False,
                                         skip_group_check=True)
                    if masks == 1:
                        out = bank[:, mask_at:mask_at + P]
                    else:
                        stride = P if mask_at == 2 * P else 2 * P
                        out = bank.rearrange("p (i c) -> p i c", c=P)[:, mask_at // P::stride // P, :]
                    last = nc.tensor.matmul(out, core.ident_bf[:, :], future_bf[:, 0:masks, :], start=False,
                                            stop=True, skip_group_check=True)
                    if i == 1:
                        last.then_inc(top_mm, 1)

                def attend(b, group, part, u):
                    if part == 0:
                        if group == 0:
                            pe.wait_ge(v_ok, b + 1)
                        upto(pe, oT_ok, GROUPS * b + group)
                    pe.wait_ge(causal_ok, SLOTS * b + 5 * group + (2, 4, 5)[part])
                    for tile in ((0,), (1, 3), (2,))[part]:
                        for h in range(GH):
                            if tile == 2:
                                src = e_heads(4)[:, h, :]
                            else:
                                j = (0 if tile == 0 else 2) + h // 2
                                c = P if tile == 1 else 0
                                src = e_heads(j)[:, h % 2, c:c + N - tile * P]
                            last = nc.tensor.matmul(ps[32 * h:32 * h + 32, BK_ATTN, tile * P:N],
                                                    v[:, u, tile, group * GH + h, :], src, start=tile == 0,
                                                    stop=tile == 2, tile_position=(0, 32 * h), skip_group_check=True)
                    last.then_inc(attn_mm, 1)

                def use_shared(s, task):
                    before = shared_user_before(s, task)
                    if before is None:
                        return
                    name, b = before
                    if name == "aT":
                        pe.wait_ge(aT_ok, b + 1)
                    elif name in ("top_early", "top_late"):
                        pe.wait_ge(row_ok, 2 * b + 1 + (name == "top_late"))
                    elif name in ("q", "k"):
                        pe.wait_ge(rope_ok, 4 * b + (2 if name == "q" else 4))
                    elif name == "v":
                        pe.wait_ge(v_ok, b + 1)
                    elif name == "oT":
                        pe.wait_ge(o_T_ok, b + 1)
                    elif name == "out":
                        pe.wait_ge(y_ok, b + 1)
                    else:
                        group = 3 if name == "natural_late" else int(name[-1])
                        pe.wait_ge(o_ok, GROUPS * b + group + 1)

                def natural(b, group):
                    pe.wait_ge(oT_ok, GROUPS * b + group + 1)
                    for t in range(T):
                        last = nc.tensor.transpose(shared_td[:, t, :], oT[:, t * P:t * P + P], core.ident[:, :])
                    last.then_inc(natural_mm, 1)

                def top_rows(b, half):
                    pe.wait_ge(parts_ok, 2 * b + half + 1)
                    for t in range(T):
                        last = nc.tensor.transpose(shared_bf[0:2 * HH, t * P:t * P + P],
                                                   top_parts[:, half, t, :, :], core.ident_bf[:, :])
                    last.then_inc(row_mm, 1)

                def step(s, u, slots=range(SLOTS)):
                    g, m, p = s + 2, s + 1, s - 1
                    for n in slots:
                        for i in range(2):
                            if live(s):
                                score_unit(s, n, i, u)
                            if live(m):
                                top_unit(m, n, i, 1 - u)
                        if n == 0 and live(p):
                            attend(p, 3, 1, 1 - u)
                        if n == 1 and live(p):
                            attend(p, 3, 2, 1 - u)
                        if live(s):
                            if n % 5 == 3:
                                attend(s, n // 5, 0, u)
                            if n % 5 == 0 and n:
                                attend(s, n // 5 - 1, 1, u)
                            if n % 5 == 1 and n > 1:
                                attend(s, n // 5 - 1, 2, u)
                        for slot, task, ahead in SHARED:
                            if slot != n or not live(s + ahead):
                                continue
                            use_shared(s, task)
                            if task == "aT":
                                pe.wait_ge(a_ok, g + 1)
                                for t in range(T):
                                    last = nc.tensor.transpose(shared_td[:, t, :], a[:, t, :], core.ident[:, :])
                                last.then_inc(aT_mm, 1)
                            elif task in ("q", "k"):
                                if task == "q":
                                    pe.wait_ge(aT_ok, g + 1)
                                w = {"q": w_q, "k": w_k}[task]
                                nc.tensor.matmul(shared, w[:, :], aT[:, u, :], start=True,
                                                 stop=True).then_inc(qk_mm, 1)
                            elif task == "v":
                                for t in range(T):
                                    last = nc.tensor.matmul(shared_td[:, t, :], aT[:, 1 - u, t * P:t * P + P],
                                                            w_v[:, :], start=True, stop=True)
                                last.then_inc(v_mm, 1)
                            elif task == "top_late":
                                top_rows(s, 1)
                            elif task == "top_early":
                                top_rows(m, 0)
                            elif task == "natural_late":
                                natural(p, 3)
                            elif task.startswith("natural"):
                                natural(s, int(task[-1]))
                            elif task == "oT":
                                pe.wait_ge(o_ok, GROUPS * p + GROUPS)
                                for t in range(T):
                                    last = nc.tensor.transpose(shared_td[:, t, :], o[:, t, :, :].rearrange(
                                        "p h d -> p (h d)"), core.ident[:, :])
                                last.then_inc(o_T_mm, 1)
                            elif task == "out":
                                pe.wait_ge(o_T_ok, p + 1)
                                for t in range(T):
                                    last = nc.tensor.matmul(shared_td[:, t, :], o_T[:, t * P:t * P + P],
                                                            w_o[:, :], start=True, stop=True)
                                last.then_inc(out_mm, 1)

                core.wait_weights(pe)
                finish_mix(mix.tensor(pe), step)
                for sem in (mix.r_ok, mix.y_ok, mix.relu_ok, mix.aT_ok):
                    pe.wait_ge(sem, B)
                pe.wait_ge(made, 2)
                step(FIRST_STEP + 2, 1)
                pe.wait_ge(ones_in, 16)
                pe.wait_ge(v_made, 2)
                run_steps(pe, step, 0, 3, 13, B - 1)
                finish_attention(step, *moe.tensor(pe))


def soft_mixture(core, ctx, early, late, early_free, late_free, banks_free):
    nc, dram, x, ps = core.nc, core.dram, core.x, core.ps
    L = Layer(core, "moe", ctx)
    w1, w2, gamma_row, gamma_slot_row, gamma, slot_raw = (
        core.weights[name] for name in ("w1", "w2", "gamma_x", "gamma_slot", "gamma_x_column", "slot_embeds"))
    slot_n = early.take([T, D])
    slotT, slotT_bf = early.take([E_T]), early.take([E_T], BF16)
    ones = early.take([P], BF16, rows=2)
    a, unit = early.take([T, D]), early.take([T, D])
    mean_sq, mean_sq_sum, rrms = L.sb("mean_sq", [P, T]), L.sb("mean_sq_sum", [P, T]), L.sb("rrms", [P, T])
    token = early.take([2, T, D + 1])
    tokenT, tokenT_bf = early.take([2, N]), early.take([N], BF16)
    top = L.sb("top", [P, 2, 2 * T])
    top_parts = L.sb("top_parts", [P, T, 2], BF16)
    top_row = early.take([2, T, P], BF16, rows=2)
    shifted = late.take([2, E_T])
    weight = late.take([2 * T, N])
    slot_rsum, slot_in = L.sb("slot_rsum", [P, T]), late.take([T, D])
    slot_inT, hiddenT = late.take([E_T]), late.take([FF // P, E_T])
    slot_out = late.take([T, D + 1])
    y_rsum, y, z = L.sb("y_rsum", [P, T]), late.take([T, D]), late.take([T, D])
    ln_x, rms, ln_y = Stats(L, "ln_x"), Stats(L, "rms"), Stats(L, "ln_y")

    made = L.sem("made")
    a_ok, mean_sq_ok, rrms_ok, unit_ok = L.sem("a_ok"), L.sem("mean_sq_ok"), L.sem("rrms_ok"), L.sem("unit_ok")
    token_ok, tokenT_mm, tokenT_ok, tokenT_bf_ok = (L.sem("token_ok"), L.sem("tokenT_mm"), L.sem("tokenT_ok"),
                                                    L.sem("tokenT_bf_ok"))
    top_mm, top_ok, hi_ok, parts_ok = L.sem("top_mm"), L.sem("top_ok"), L.sem("hi_ok"), L.sem("parts_ok")
    row_mm, row_ok = L.sem("row_mm"), L.sem("row_ok")
    logit_mm, shifted_ok, rank_mm, weight_ok = (L.sem("logit_mm"), L.sem("shifted_ok"), L.sem("rank_mm"),
                                                L.sem("weight_ok"))
    turned_mm, combine_ok = L.sem("turned_mm"), L.sem("combine_ok")
    slot_mm, slot_rsum_ok, slot_ok = L.sem("slot_mm"), L.sem("slot_rsum_ok"), L.sem("slot_ok")
    slotT_mm, slotT_ok = L.sem("slotT_mm"), L.sem("slotT_ok")
    hidden_mm, hidden_ok = L.sem("hidden_mm"), L.sem("hidden_ok")
    slot_out_mm, slot_out_ok = L.sem("slot_out_mm"), L.sem("slot_out_ok")
    out_mm, y_rsum_ok, y_ok, z_ok, x_ok = (L.sem("out_mm"), L.sem("y_rsum_ok"), L.sem("y_ok"), L.sem("z_ok"),
                                           L.sem("x_ok"))
    stored, table_ok = L.sem("stored"), L.sem("table_ok")
    warm = L.sb("warm", [P, 1])

    BK_LOGIT, BK_TOP, BK_ROW, BK_T, BK_TURNED, BK_WIDE = 0, 2, 3, 4, 5, 6
    row_ps = ps[:, BK_ROW, :].bitcast(BF16)

    def wide(t):
        return ps[:, BK_WIDE + t // 2, t % 2 * (D + 1):t % 2 * (D + 1) + D + 1]

    def wide_sums(bank):
        return ps[:, BK_WIDE + bank, 0:2 * (D + 1)].rearrange("p (t c) -> p t c", t=2)[:, :, D]

    def take_rrms(pool, k):
        pool.wait_ge(rms.moments_done, k + 1)
        nc.gpsimd.tensor_tensor(mean_sq[:, :], rms.moments[:, :, 0], rms.moments[:, :, 0],
                                ALU.mult).then_inc(mean_sq_ok, 1)
        pool.wait_ge(mean_sq_ok, 3 * k + 1)
        nc.gpsimd.tensor_tensor(mean_sq_sum[:, :], mean_sq[:, :], rms.moments[:, :, 1],
                                ALU.add).then_inc(mean_sq_ok, 1)
        pool.wait_ge(mean_sq_ok, 3 * k + 2)
        pool.sem_inc(core.tick, 1)
        nc.gpsimd.tensor_scalar(mean_sq[:, :], mean_sq_sum[:, :], NORM_FLOOR, None,
                                ALU.max).then_inc(mean_sq_ok, 1)
        pool.wait_ge(mean_sq_ok, 3 * k + 3)
        nc.gpsimd.tensor_tensor(rrms[:, :], mean_sq[:, :], core.minus_half[:, :],
                                ALU.pow).then_inc(rrms_ok, 1)

    def vector(dve, x_before):
        def top_unit(f, fu, i):
            dve.wait_ge(top_mm, 8 * f + i + 1)
            nc.vector.reduce_max(top[:, fu, i:i + 1], ps[:, BK_TOP + i % 2, :], AXX).then_inc(top_ok, 1)

        def step(s, u):
            g, f, fu, p = s + 2, s + 1, 1 - u, s - 1
            if live(p):
                for j in range(2):
                    dve.wait_ge(out_mm, 2 * p + j + 1)
                    nc.vector.reciprocal(y_rsum[:, 2 * j:2 * j + 2], wide_sums(j)).then_inc(y_rsum_ok, 1)
                    dve.wait_ge(y_rsum_ok, 2 * p + j + 1)
                    for t in (2 * j, 2 * j + 1):
                        last = nc.vector.tensor_scalar(y[:, t, :], wide(t)[:, 0:D], y_rsum[:, t:t + 1],
                                                       None, ALU.mult)
                    last.then_inc(y_ok, 1)
            for i in range(T):
                if live(s):
                    dve.wait_ge(logit_mm, 4 * s + i + 1)
                    if i == 0:
                        dve.wait_ge(top_ok, 8 * s + 8)
                    upto(dve, turned_mm, 4 * s + i - 1)
                    nc.vector.tensor_scalar(shifted[:, i % 2, :], ps[:, BK_LOGIT + i % 2, :],
                                            top[:, u, T + i:T + i + 1], None,
                                            ALU.subtract).then_inc(shifted_ok, 1)
                if live(f) and i == 0:
                    dve.wait_ge(tokenT_ok, f + 1)
                    nc.vector.tensor_copy(tokenT_bf[:, :], tokenT[:, fu, :]).then_inc(tokenT_bf_ok, 1)
                if live(f) and i == 1:
                    top_unit(f, fu, 0)
                if live(f) and i == 2:
                    top_unit(f, fu, 1)
                    top_unit(f, fu, 2)
            if live(f):
                top_unit(f, fu, 3)
                dve.wait_ge(top_ok, 8 * f + 4)
                upto(dve, row_mm, f)
                nc.vector.tensor_scalar(top_parts[:, :, 0], top[:, fu, 0:T], -1.0, None,
                                        ALU.mult).then_inc(hi_ok, 1)
                dve.wait_ge(hi_ok, f + 1)
                nc.vector.scalar_tensor_tensor(top_parts[:, :, 1], top[:, fu, 0:T], -1.0, top_parts[:, :, 0],
                                               ALU.mult, ALU.subtract).then_inc(parts_ok, 1)
            if live(p):
                dve.wait_ge(y_ok, 2 * p + 2)
                take_moments(core, dve, ln_y, lambda t: y[:, t, :], p)
            if live(s):
                for j in range(2):
                    dve.wait_ge(slot_mm, 2 * s + j + 1)
                    nc.vector.reciprocal(slot_rsum[:, 2 * j:2 * j + 2], wide_sums(j)).then_inc(slot_rsum_ok, 1)
                    dve.wait_ge(slot_rsum_ok, 2 * s + j + 1)
                    for t in (2 * j, 2 * j + 1):
                        nc.vector.tensor_scalar(slot_in[:, t, :], wide(t)[:, 0:D], slot_rsum[:, t:t + 1], None,
                                                ALU.mult).then_inc(slot_ok, 1)
            if live(f):
                top_unit(f, fu, 4)
                top_unit(f, fu, 5)
            if live(g):
                dve.wait_ge(ln_x.rstd_done, g + 1)
                normalize(nc, ln_x, lambda t: a[:, t, :], lambda t: x[:, g, t, :]).then_inc(a_ok, 1)
            if live(f):
                top_unit(f, fu, 6)
            if live(g):
                dve.wait_ge(a_ok, g + 1)
                take_moments(core, dve, rms, lambda t: a[:, t, :], g + 1)
            if live(f):
                top_unit(f, fu, 7)
            if live(p):
                dve.wait_ge(ln_y.rstd_done, p + 1)
                upto(dve, x_ok, p)
                normalize(nc, ln_y, lambda t: z[:, t, :], lambda t: y[:, t, :]).then_inc(z_ok, 1)
            if live(s):
                upto(dve, out_mm, 2 * s)
                for j in range(2):
                    dve.wait_ge(slot_out_mm, 2 * s + j + 1)
                    nc.vector.tensor_copy(slot_out[:, 2 * j:2 * j + 2, 0:D],
                                          ps[:, BK_T + j, 0:2 * D].rearrange(
                                              "p (t d) -> p t d", t=2)).then_inc(slot_out_ok, 1)
            if live(g):
                dve.wait_ge(rrms_ok, g + 2)
                upto(dve, token_ok, g)
                upto(dve, tokenT_mm, g)
                for t in range(T):
                    last = nc.vector.tensor_scalar(unit[:, t, :], a[:, t, :], rrms[:, t:t + 1], None, ALU.mult)
                last.then_inc(unit_ok, 1)
            h = s + 3
            if live(h):
                dve.wait_ge(x_before, h + 1)
                take_moments(core, dve, ln_x, lambda t: x[:, h, t, :], h)

        def start():
            early_free(dve)
            take_moments(core, dve, rms, lambda t: slot_raw[:, t, :], 0)
            step(-3, 1)
            nc.vector.memset(ones[:, :], 1.0)
            nc.vector.memset(token[:, :, :, D:D + 1], 1.0)

        def norm_slots():
            dve.wait_ge(rrms_ok, 1)
            for t in range(T):
                last = nc.vector.scalar_tensor_tensor(slot_n[:, t, :], slot_raw[:, t, :], rrms[:, t:t + 1],
                                                      gamma_slot_row[:, :], ALU.mult, ALU.mult)
            last.then_inc(made, 1)
            step(-2, 0)

        def take_slotT():
            dve.wait_ge(made, 2)
            nc.vector.tensor_copy(slotT[:, :], ps[:, BK_TURNED, :]).then_inc(made, 1)
            dve.wait_ge(made, 3)
            nc.vector.tensor_copy(slotT_bf[:, :], slotT[:, :]).then_inc(made, 1)
            step(-1, 1)

        def remainder():
            late_free(dve)
            nc.vector.memset(slot_out[:, :, D:D + 1], 1.0)
            run_steps(dve, step, 0, 3, 11, B + 1)

        return start, norm_slots, take_slotT, remainder

    def gpsimd(pool):
        def step(s, u):
            h, g, f, p = s + 3, s + 2, s + 1, s - 1
            if live(f):
                pool.wait_ge(unit_ok, f + 1)
                upto(pool, slot_mm, 2 * (f - 1))
                nc.gpsimd.tensor_tensor(token[:, 1 - u, :, 0:D], unit[:, :, :],
                                        gamma_row[:, :].unsqueeze(1).broadcast_to([P, T, D]),
                                        ALU.mult).then_inc(token_ok, 1)
            if live(p):
                take_rstd(core, pool, ln_y, p)
            if live(g):
                take_rrms(pool, g + 1)
            if live(p):
                pool.wait_ge(z_ok, p + 1)
                pool.sem_inc(core.tick, 1)
                nc.gpsimd.tensor_tensor(x[:, p, :, :], x[:, p, :, :], z[:, :, :], ALU.add).then_inc(x_ok, 1)
            if live(h):
                take_rstd(core, pool, ln_x, h)

        def start():
            take_rrms(pool, 0)
            step(-3, 1)

        return start, lambda: step(-2, 0), lambda: step(-1, 1), lambda: run_steps(pool, step, 0, 3, 11, B + 1)

    def sync(sp):
        with sp.Fori(0, B) as b:
            sp.wait_ge(x_ok, b + 1)
            sp.dma_start(dram["out"][b].rearrange("(t p) d -> p t d", p=P),
                         x[:, b, :, :]).then_inc(stored, 16)
        sp.wait_ge(stored, 16 * B)

    def scalar(act):
        def load_table(function, k):
            upto(act, table_ok, k - 1)
            nc.scalar.activation(warm[:, :], core.eps[:, 0:1], function).then_inc(table_ok, 1)

        def dispatch_weights(s, i):
            act.wait_ge(rank_mm, 4 * s + i + 1)
            if i == 0:
                upto(act, slot_mm, 2 * s)
            nc.scalar.activation(weight[:, i, :], ps[:, BK_LOGIT + i % 2, :], ACT.Exp).then_inc(weight_ok, 1)

        def step(s, u):
            f = s + 1
            if live(f):
                act.wait_ge(tokenT_mm, f + 1)
                upto(act, logit_mm, 4 * (f - 1))
                nc.scalar.activation(tokenT[:, 1 - u, :], ps[:, BK_T, :], ACT.Copy,
                                     scale=gamma[:, 0:1]).then_inc(tokenT_ok, 1)
            if live(s):
                for i in range(T):
                    for k in ((0,), (1,), (2, 3), ())[i]:
                        dispatch_weights(s, k)
                    act.wait_ge(turned_mm, 4 * s + i + 1)
                    if i == 0:
                        upto(act, out_mm, 2 * s)
                    nc.scalar.activation(weight[:, T:2 * T, i * P:i * P + P],
                                         ps[:, BK_TURNED, :].rearrange("p (e c) -> p e c", e=T),
                                         ACT.Exp).then_inc(combine_ok, 1)
            if live(f):
                act.wait_ge(row_mm, f + 1)
                upto(act, rank_mm, 4 * (f - 1))
                nc.scalar.copy(top_row[:, 1 - u, :, :], row_ps[0:2, 0:E_T].rearrange(
                    "r (i p) -> r i p", i=T)).then_inc(row_ok, 1)
            if live(s):
                load_table(ACT.Gelu, 2 * s + 1)
                upto(act, hidden_mm, 4 * s)
                for j in range(2):
                    act.wait_ge(slotT_mm, 2 * s + j + 1)
                    nc.scalar.copy(slot_inT[:, 2 * j * P:2 * (j + 1) * P],
                                   ps[:, BK_T + j, 0:2 * P]).then_inc(slotT_ok, 1)
                upto(act, slot_out_mm, 2 * s)
                for j in range(FF // P):
                    act.wait_ge(hidden_mm, 4 * s + j + 1)
                    nc.scalar.activation(hiddenT[:, j, :], ps[:, BK_LOGIT + j % 2, :],
                                         ACT.Gelu).then_inc(hidden_ok, 1)
                load_table(ACT.Exp, 2 * s + 2)

        def start():
            core.wait_weights(act)
            early_free(act)

        def remainder():
            late_free(act)
            run_steps(act, step, 0, 1, 13, B)

        return start, lambda: None, lambda: step(-1, 1), remainder

    def tensor(pe):
        def top_unit(f, i):
            upto(pe, top_ok, 8 * f + i - 1)
            if i == 5:
                pe.wait_ge(row_ok, f + 1)
            lhs, rhs = (slotT_bf, tokenT_bf) if i < T else (tokenT_bf, slotT_bf)
            c = i % T * P
            nc.tensor.matmul(ps[:, BK_TOP + i % 2, :], lhs[:, c:c + P], rhs[:, :], start=True,
                             stop=True).then_inc(top_mm, 1)

        def logits(s, u, i):
            if i >= 2:
                pe.wait_ge(weight_ok, 4 * s + i - 1)
            nc.tensor.matmul(ps[:, BK_LOGIT + i % 2, :], tokenT[:, u, i * P:i * P + P], slotT[:, :],
                             start=True, stop=False, skip_group_check=True).then_inc(logit_mm, 1)

        def subtract_top(s, u, i):
            pe.wait_ge(shifted_ok, 4 * s + i + 1)
            nc.tensor.matmul(ps[:, BK_LOGIT + i % 2, :], ones[:, :], top_row[:, u, :, :], start=False,
                             stop=True, skip_group_check=True).then_inc(rank_mm, 1)

        def turn(s, i):
            upto(pe, combine_ok, 4 * s + i)
            for e in range(T):
                last = nc.tensor.transpose(ps[:, BK_TURNED, e * P:e * P + P],
                                           shifted[:, i % 2, e * P:e * P + P], core.ident[:, :])
            last.then_inc(turned_mm, 1)

        def top_rows(f):
            pe.wait_ge(parts_ok, f + 1)
            for i in range(T):
                last = nc.tensor.transpose(row_ps[0:2, i * P:i * P + P], top_parts[:, i, :],
                                       core.ident_bf[:, :])
            last.then_inc(row_mm, 1)

        def step(s, u):
            f = s + 1
            if live(f):
                pe.wait_ge(unit_ok, f + 1)
                upto(pe, slot_out_ok, 2 * (f - 1))
                for t in range(T):
                    last = nc.tensor.transpose(ps[:, BK_T, t * P:t * P + P], unit[:, t, :], core.ident[:, :])
                last.then_inc(tokenT_mm, 1)
            if live(s):
                upto(pe, hidden_ok, 4 * s)
                logits(s, u, 0)
                pe.wait_ge(row_ok, s + 1)
                for i in range(1, T):
                    logits(s, u, i)
                    subtract_top(s, u, i - 1)
                    turn(s, i - 1)
                    if i == 1 and live(f):
                        pe.wait_ge(tokenT_bf_ok, f + 1)
                    for k in ((0, 1), (2,), (3,))[i - 1] if live(f) else ():
                        top_unit(f, k)
                subtract_top(s, u, 3)
            elif live(f):
                pe.wait_ge(tokenT_bf_ok, f + 1)
                for i in range(T):
                    top_unit(f, i)
                top_rows(f)
            if live(s):
                pe.wait_ge(token_ok, s + 1)
                upto(pe, y_ok, 2 * s)
                for j in range(2):
                    if j == 1:
                        if live(f):
                            top_rows(f)
                        turn(s, 3)
                    for t in range(T):
                        if j == 0:
                            pe.wait_ge(weight_ok, 4 * s + t + 1)
                        for e in (2 * j, 2 * j + 1):
                            last = nc.tensor.matmul(wide(e), weight[:, t, e * P:e * P + P], token[:, u, t, :],
                                                    start=t == 0 and e == 2 * j, stop=t == T - 1,
                                                    skip_group_check=True)
                    last.then_inc(slot_mm, 1)
            if live(f):
                top_unit(f, 4)
            if live(s):
                for e in range(T):
                    if e == 2 and live(f):
                        top_unit(f, 5)
                    pe.wait_ge(slot_ok, 4 * s + e + 1)
                    if e == 2:
                        pe.wait_ge(combine_ok, 4 * s + 4)
                    last = nc.tensor.transpose(ps[:, BK_T + e // 2, e % 2 * P:e % 2 * P + P], slot_in[:, e, :],
                                               core.ident[:, :])
                    if e % 2:
                        last.then_inc(slotT_mm, 1)
            elif live(f):
                top_unit(f, 5)
            if live(f):
                top_unit(f, 6)
            if live(s):
                pe.wait_ge(slotT_ok, 2 * s + 2)
                for j in range(FF // P):
                    if j >= 2:
                        pe.wait_ge(hidden_ok, 4 * s + j - 1)
                    nc.tensor.matmul(ps[:, BK_LOGIT + j % 2, :], w1[:, j * P:j * P + P], slot_inT[:, :],
                                     start=True, stop=True).then_inc(hidden_mm, 1)
                    if j == 1 and live(f):
                        top_unit(f, 7)
            elif live(f):
                top_unit(f, 7)
            if live(s):
                for half in range(2):
                    for j in range(FF // P):
                        if half == 0:
                            pe.wait_ge(hidden_ok, 4 * s + j + 1)
                        for e in (2 * half, 2 * half + 1):
                            last = nc.tensor.matmul(ps[:, BK_T + half, e % 2 * D:e % 2 * D + D],
                                                    hiddenT[:, j, e * P:e * P + P], w2[:, j, :],
                                                    start=j == 0 and e % 2 == 0, stop=j == FF // P - 1,
                                                    skip_group_check=True)
                    last.then_inc(slot_out_mm, 1)
                for half in range(2):
                    for e in range(T):
                        if half == 0 and e % 2 == 0:
                            pe.wait_ge(slot_out_ok, 2 * s + e // 2 + 1)
                        for t in (2 * half, 2 * half + 1):
                            last = nc.tensor.matmul(wide(t), weight[:, T + e, t * P:t * P + P], slot_out[:, e, :],
                                                    start=e == 0 and t % 2 == 0, stop=e == T - 1,
                                                    skip_group_check=True)
                    last.then_inc(out_mm, 1)

        def transpose_slots():
            early_free(pe)
            pe.wait_ge(made, 1)
            for t in range(T):
                last = nc.tensor.transpose(ps[:, BK_TURNED, t * P:t * P + P], slot_n[:, t, :], core.ident[:, :])
            last.then_inc(made, 1)

        def first_maxima():
            pe.wait_ge(made, 4)
            step(-1, 1)

        def remainder():
            banks_free(pe)
            run_steps(pe, step, 0, 1, 13, B)

        return lambda: None, transpose_slots, first_maxima, remainder

    return LayerPrograms(sync, vector, gpsimd, scalar, tensor)


class LayerPrograms:

    def __init__(self, sync, vector, gpsimd, scalar, tensor):
        self.sync, self.vector, self.gpsimd, self.scalar, self.tensor = sync, vector, gpsimd, scalar, tensor


def finish_attention(step, start, second, third, remainder):
    start()
    step(B - 1, 1, range(0, 8))
    second()
    step(B - 1, 1, range(8, 20))
    step(B, 0, range(0, 6))
    third()
    step(B, 0, range(6, 20))
    remainder()


def build(nc, dram):
    with ExitStack() as ctx:
        core = Core(nc, ctx, dram)
        core.tick = core.sem("tick")
        gated_attention(core)
        causal_attention(core)


def kernel(**inputs):
    import concourse.bacc as bacc
    from concourse.bass_utils import run_bass_kernel_spmd

    got = {name: np.asarray(a) for name, a in inputs.items()}
    arrays = {}
    for name, a in got.items():
        short = name.split("_", 2)[2]
        arrays[short] = a
    for name in ("W_r", "W_k", "W_v", "Wv", "Wo"):
        arrays[f"{name}_T"] = arrays.pop(name).T
    for name in ("Wq", "Wk"):
        arrays[f"{name}_T"] = arrays.pop(name)[qk_rows()].T
    arrays["gau_vectors"] = np.stack([arrays["ln_g"], arrays["ln_b"], arrays["b_qk"],
                                      *arrays["b_hidden"][HID:].reshape(2, D), *arrays["os_gamma"],
                                      *arrays["os_beta"]], axis=1)
    arrays["mix_vectors"] = np.stack([arrays.pop("mu_r"), arrays.pop("mu_k")], axis=1)
    for name in ("ln_g", "ln_b", "b_qk", "os_gamma", "os_beta"):
        arrays.pop(name)
    arrays.update(constants())
    arrays = {name: np.ascontiguousarray(a) for name, a in arrays.items()}

    nc = bacc.Bacc("TRN2", target_bir_lowering=False, num_devices=1)
    dram = {name: nc.dram_tensor(f"in_{name}", a.shape, mybir.dt.from_np(a.dtype), kind="ExternalInput").ap()
            for name, a in arrays.items()}
    dram["out"] = nc.dram_tensor("out", (B, N, D), F32, kind="ExternalOutput").ap()
    build(nc, dram)
    result = run_bass_kernel_spmd(nc, [{f"in_{name}": a for name, a in arrays.items()}], core_ids=[0])
    return result.results[0]["out"]
```
